# Optimizing a Trainium2 kernel written in Bass

```python
import numpy as np
import jax
import jax.numpy as jnp

def _softmax(x, axis=-1):
    return jax.nn.softmax(x, axis=axis)

def _gelu(x):
    return jax.nn.gelu(x, approximate=True)

def _silu(x):
    return jax.nn.silu(x)

def _sigmoid(x):
    return jax.nn.sigmoid(x)

def _layernorm(x, axis=-1, eps=1e-05):
    m = jnp.mean(x, axis=axis, keepdims=True)
    v = jnp.var(x, axis=axis, keepdims=True)
    return (x - m) / jnp.sqrt(v + eps)

def _scatter_add(tgt, idx, src, axis=0):
    return tgt.at[idx].add(src)

def _segment_sum(src, seg, n):
    return jax.ops.segment_sum(src, seg, n)
kernel_name = 'mk_xattn_ffn_d2_seqx_r2_e77502'

def setup_inputs(seed: int=0):
    np.random.seed(seed)
    _w = jnp.asarray

    def _rec_inputs():
        import jax
        import jax.numpy as jnp
        _rk = jax.random.key(seed)
        x = 6.313e-05 + 0.9998 * jax.random.normal(jax.random.fold_in(_rk, 1), (8, 100, 512), jnp.float32)
        _lenS = 100 - jax.random.randint(jax.random.fold_in(_rk, 7), (8,), 0, max(1, 100 // 4) + 1, jnp.int32)
        _lenS2 = 722 - jax.random.randint(jax.random.fold_in(_rk, 8), (8,), 0, max(1, 722 // 4) + 1, jnp.int32)
        _ctx_1024P = jax.random.normal(jax.random.fold_in(_rk, 11), (8, 16, 512), jnp.float32)
        _ctx_1024c = jax.random.dirichlet(jax.random.fold_in(_rk, 511), 0.3 * jnp.ones((16,), jnp.float32), (8, 722))
        _ctx_1024t = jnp.einsum('bsk,bkd->bsd', _ctx_1024c, _ctx_1024P)
        _ctx_1024t = _ctx_1024t * jax.lax.rsqrt(jnp.mean(jnp.square(_ctx_1024t)) + 1e-12) * 0.953939
        ctx_1024 = -0.000214406 + 1.00034 * (_ctx_1024t + 0.3 * jax.random.normal(jax.random.fold_in(_rk, 611), (8, 722, 512), jnp.float32))
        _validS = jnp.arange(100)[None, :] < _lenS[:, None]
        _validS2 = jnp.arange(722)[None, :] < _lenS2[:, None]
        _causal = jnp.tril(jnp.ones((100, 100), dtype=bool))
        mask_BxS2_bk0 = jnp.logical_not(jnp.broadcast_to(_validS2[:, :], (8, 722)))
        return (x, ctx_1024, mask_BxS2_bk0)
    x, ctx_1024, mask_BxS2_bk0 = _rec_inputs()

    def _L0_xattn_setup():
        import jax, jax.numpy as jnp
        import numpy as np
        from jax import lax
        BIG = jnp.float32(1e+30)

        def _pairwise_euclidean(a, b):
            aa = jnp.sum(a * a, axis=-1)[:, None]
            bb = jnp.sum(b * b, axis=-1)[None, :]
            ab = a @ b.T
            return jnp.sqrt(jnp.maximum(aa + bb - 2.0 * ab, 0.0))

        def _dtw_cost(D):
            row0 = jnp.cumsum(D[0])

            def row_step(prev_row, d_row):
                first = d_row[0] + prev_row[0]

                def col_step(left, inp):
                    d_ij, up, diag = inp
                    r = d_ij + jnp.minimum(jnp.minimum(up, left), diag)
                    return (r, r)
                _, rest = lax.scan(col_step, first, (d_row[1:], prev_row[1:], prev_row[:-1]))
                row = jnp.concatenate([first[None], rest])
                return (row, row)
            _, rows = lax.scan(row_step, row0, D[1:])
            return jnp.concatenate([row0[None], rows], axis=0)

        def _backtrack(R, T1, T2):
            L = T1 + T2 - 1

            def step(carry, _):
                i, j, done = carry
                valid = jnp.logical_not(done)
                cd = jnp.where((i > 0) & (j > 0), R[jnp.maximum(i - 1, 0), jnp.maximum(j - 1, 0)], BIG)
                cu = jnp.where(i > 0, R[jnp.maximum(i - 1, 0), j], BIG)
                cl = jnp.where(j > 0, R[i, jnp.maximum(j - 1, 0)], BIG)
                choice = jnp.argmin(jnp.stack([cd, cu, cl]))
                ni = jnp.where(choice <= 1, i - 1, i)
                nj = jnp.where((choice == 0) | (choice == 2), j - 1, j)
                at_origin = (i == 0) & (j == 0)
                ni = jnp.where(at_origin, 0, ni)
                nj = jnp.where(at_origin, 0, nj)
                return ((ni, nj, done | at_origin), (i, j, valid))
            init = (jnp.int32(T1 - 1), jnp.int32(T2 - 1), jnp.bool_(False))
            _, (i_idx, j_idx, valid) = lax.scan(step, init, None, length=L)
            return (i_idx, j_idx, valid)

        def _align_one(small, large):
            T_small, d = small.shape
            T_large = large.shape[0]
            D = _pairwise_euclidean(small, large)
            R = _dtw_cost(D)
            i_idx, j_idx, valid = _backtrack(R, T_small, T_large)
            contrib = small[i_idx] * valid[:, None].astype(small.dtype)
            expanded = jnp.zeros((T_large, d), dtype=small.dtype).at[j_idx].add(contrib)
            return expanded
        key = jax.random.key(seed)
        k1, k2 = jax.random.split(key)
        teacher = jax.random.normal(k1, (16, 200, 512), dtype=jnp.float32)
        student = jax.random.normal(k2, (16, 300, 512), dtype=jnp.float32)
        return {'teacher_features': teacher, 'student_features': student}
    _L0_xattn_all = _L0_xattn_setup()
    _L0_xattn_in = {k: v for k, v in _L0_xattn_all.items() if k in ()}
    del _L0_xattn_all

    def _L0_ffn_setup():
        import jax, jax.numpy as jnp
        import numpy as np
        N_EXPERTS = 16
        TOP_K = int(N_EXPERTS * 0.2)
        EPS = 1e-12
        key = jax.random.key(seed)
        ks = jax.random.split(key, 6)
        B, T, D, H, E = (4, 512, 512, 1024, N_EXPERTS)
        x = jax.random.normal(ks[0], (B, T, D), dtype=jnp.float32)
        gate = jax.random.normal(ks[1], (D, E), dtype=jnp.float32)
        W1 = jax.random.normal(ks[2], (E, D, H), dtype=jnp.float32) * (1.0 / np.sqrt(D))
        b1 = jax.random.normal(ks[3], (E, H), dtype=jnp.float32) * 0.02
        W2 = jax.random.normal(ks[4], (E, H, D), dtype=jnp.float32) * (1.0 / np.sqrt(H))
        b2 = jax.random.normal(ks[5], (E, D), dtype=jnp.float32) * 0.02
        return {'x': x, 'gate': gate, 'W1': W1, 'b1': b1, 'W2': W2, 'b2': b2}
    _L0_ffn_all = _L0_ffn_setup()
    _L0_ffn_in = {k: v for k, v in _L0_ffn_all.items() if k in ('gate', 'W1', 'b1', 'W2', 'b2')}
    del _L0_ffn_all

    def _L1_xattn_setup():
        import jax, jax.numpy as jnp
        import numpy as np
        DIM = 512
        DIM_LATENT = 512
        DIM_HEAD = 64
        INNER = max(DIM, DIM_LATENT)
        HEADS = INNER // DIM_HEAD
        SCALE = DIM_HEAD ** (-0.5)
        LN_EPS = 1e-05
        RMS_EPS = 1e-08

        def layernorm(x, g, b):
            mu = jnp.mean(x, axis=-1, keepdims=True)
            var = jnp.mean(jnp.square(x - mu), axis=-1, keepdims=True)
            return (x - mu) * jax.lax.rsqrt(var + LN_EPS) * g + b

        def rmsnorm(x, gamma):
            n = jnp.linalg.norm(x, axis=-1, keepdims=True) * x.shape[-1] ** (-0.5)
            return x / jnp.maximum(n, RMS_EPS) * gamma
        key = jax.random.key(seed)
        ks = jax.random.split(key, 8)
        b, n, nl = (8, 1024, 256)
        x = jax.random.normal(ks[0], (b, n, DIM), dtype=jnp.float32)
        latents = jax.random.normal(ks[1], (b, nl, DIM_LATENT), dtype=jnp.float32)
        mask = jax.random.randint(ks[2], (b, n), 0, 2).astype(bool)
        init = lambda k, shape, fan_in: jax.random.normal(k, shape, jnp.float32) * fan_in ** (-0.5)
        return {'x': x, 'latents': latents, 'mask': mask, 'ln_x_g': jnp.ones((DIM,), jnp.float32), 'ln_x_b': jnp.zeros((DIM,), jnp.float32), 'ln_l_g': jnp.ones((DIM_LATENT,), jnp.float32), 'ln_l_b': jnp.zeros((DIM_LATENT,), jnp.float32), 'q_gamma': jnp.ones((DIM_HEAD,), jnp.float32), 'k_gamma': jnp.ones((DIM_HEAD,), jnp.float32), 'W_q': init(ks[3], (DIM_LATENT, INNER), DIM_LATENT), 'W_kv': init(ks[4], (DIM, 2 * INNER), DIM), 'W_out': init(ks[5], (INNER, DIM_LATENT), INNER), 'b_out': jnp.zeros((DIM_LATENT,), jnp.float32)}
    _L1_xattn_all = _L1_xattn_setup()
    _L1_xattn_in = {k: v for k, v in _L1_xattn_all.items() if k in ('ln_x_g', 'ln_x_b', 'ln_l_g', 'ln_l_b', 'q_gamma', 'k_gamma', 'W_q', 'W_kv', 'W_out', 'b_out')}
    del _L1_xattn_all

    def _L1_ffn_setup():
        import jax, jax.numpy as jnp
        import numpy as np
        TOP_K = 2
        key = jax.random.key(seed)
        ks = jax.random.split(key, 7)
        B_, S, D, F, E, R = (2, 1024, 512, 2048, 4, 4)
        x = jax.random.normal(ks[0], (B_, S, D), dtype=jnp.float32)
        Wg = jax.random.normal(ks[1], (E, D), dtype=jnp.float32) * (1.0 / np.sqrt(D))
        bg = jnp.zeros((E,), dtype=jnp.float32)
        Wi = jax.random.normal(ks[2], (F, D), dtype=jnp.float32) * (1.0 / np.sqrt(D))
        Wo = jax.random.normal(ks[3], (D, F), dtype=jnp.float32) * (1.0 / np.sqrt(F))
        A = jax.random.normal(ks[4], (E, R, D), dtype=jnp.float32) * (1.0 / np.sqrt(D))
        Bm = jax.random.normal(ks[5], (E, F, R), dtype=jnp.float32) * 0.01
        return {'x': x, 'Wg': Wg, 'bg': bg, 'Wi': Wi, 'Wo': Wo, 'A': A, 'B': Bm}
    _L1_ffn_all = _L1_ffn_setup()
    _L1_ffn_in = {k: v for k, v in _L1_ffn_all.items() if k in ('Wg', 'bg', 'Wi', 'Wo', 'A', 'B')}
    del _L1_ffn_all
    return {'x': x, 'ctx_1024': ctx_1024, 'mask_BxS2_bk0': mask_BxS2_bk0, 'L0_ffn_gate': _L0_ffn_in['gate'], 'L0_ffn_W1': _L0_ffn_in['W1'], 'L0_ffn_b1': _L0_ffn_in['b1'], 'L0_ffn_W2': _L0_ffn_in['W2'], 'L0_ffn_b2': _L0_ffn_in['b2'], 'L1_xattn_ln_x_g': _L1_xattn_in['ln_x_g'], 'L1_xattn_ln_x_b': _L1_xattn_in['ln_x_b'], 'L1_xattn_ln_l_g': _L1_xattn_in['ln_l_g'], 'L1_xattn_ln_l_b': _L1_xattn_in['ln_l_b'], 'L1_xattn_q_gamma': _L1_xattn_in['q_gamma'], 'L1_xattn_k_gamma': _L1_xattn_in['k_gamma'], 'L1_xattn_W_q': _L1_xattn_in['W_q'], 'L1_xattn_W_kv': _L1_xattn_in['W_kv'], 'L1_xattn_W_out': _L1_xattn_in['W_out'], 'L1_xattn_b_out': _L1_xattn_in['b_out'], 'L1_ffn_Wg': _L1_ffn_in['Wg'], 'L1_ffn_bg': _L1_ffn_in['bg'], 'L1_ffn_Wi': _L1_ffn_in['Wi'], 'L1_ffn_Wo': _L1_ffn_in['Wo'], 'L1_ffn_A': _L1_ffn_in['A'], 'L1_ffn_B': _L1_ffn_in['B']}

def reference(x, ctx_1024, mask_BxS2_bk0, L0_ffn_gate, L0_ffn_W1, L0_ffn_b1, L0_ffn_W2, L0_ffn_b2, L1_xattn_ln_x_g, L1_xattn_ln_x_b, L1_xattn_ln_l_g, L1_xattn_ln_l_b, L1_xattn_q_gamma, L1_xattn_k_gamma, L1_xattn_W_q, L1_xattn_W_kv, L1_xattn_W_out, L1_xattn_b_out, L1_ffn_Wg, L1_ffn_bg, L1_ffn_Wi, L1_ffn_Wo, L1_ffn_A, L1_ffn_B):
    import jax
    import jax.numpy as jnp

    def _L0_xattn_ref(teacher_features, student_features):
        import jax, jax.numpy as jnp
        import numpy as np
        from jax import lax
        BIG = jnp.float32(1e+30)

        def _pairwise_euclidean(a, b):
            aa = jnp.sum(a * a, axis=-1)[:, None]
            bb = jnp.sum(b * b, axis=-1)[None, :]
            ab = a @ b.T
            return jnp.sqrt(jnp.maximum(aa + bb - 2.0 * ab, 0.0))

        def _dtw_cost(D):
            row0 = jnp.cumsum(D[0])

            def row_step(prev_row, d_row):
                first = d_row[0] + prev_row[0]

                def col_step(left, inp):
                    d_ij, up, diag = inp
                    r = d_ij + jnp.minimum(jnp.minimum(up, left), diag)
                    return (r, r)
                _, rest = lax.scan(col_step, first, (d_row[1:], prev_row[1:], prev_row[:-1]))
                row = jnp.concatenate([first[None], rest])
                return (row, row)
            _, rows = lax.scan(row_step, row0, D[1:])
            return jnp.concatenate([row0[None], rows], axis=0)

        def _backtrack(R, T1, T2):
            L = T1 + T2 - 1

            def step(carry, _):
                i, j, done = carry
                valid = jnp.logical_not(done)
                cd = jnp.where((i > 0) & (j > 0), R[jnp.maximum(i - 1, 0), jnp.maximum(j - 1, 0)], BIG)
                cu = jnp.where(i > 0, R[jnp.maximum(i - 1, 0), j], BIG)
                cl = jnp.where(j > 0, R[i, jnp.maximum(j - 1, 0)], BIG)
                choice = jnp.argmin(jnp.stack([cd, cu, cl]))
                ni = jnp.where(choice <= 1, i - 1, i)
                nj = jnp.where((choice == 0) | (choice == 2), j - 1, j)
                at_origin = (i == 0) & (j == 0)
                ni = jnp.where(at_origin, 0, ni)
                nj = jnp.where(at_origin, 0, nj)
                return ((ni, nj, done | at_origin), (i, j, valid))
            init = (jnp.int32(T1 - 1), jnp.int32(T2 - 1), jnp.bool_(False))
            _, (i_idx, j_idx, valid) = lax.scan(step, init, None, length=L)
            return (i_idx, j_idx, valid)

        def _align_one(small, large):
            T_small, d = small.shape
            T_large = large.shape[0]
            D = _pairwise_euclidean(small, large)
            R = _dtw_cost(D)
            i_idx, j_idx, valid = _backtrack(R, T_small, T_large)
            contrib = small[i_idx] * valid[:, None].astype(small.dtype)
            expanded = jnp.zeros((T_large, d), dtype=small.dtype).at[j_idx].add(contrib)
            return expanded
        return jax.vmap(_align_one)(teacher_features, student_features)

    def _L0_ffn_ref(x, gate, W1, b1, W2, b2):
        import jax, jax.numpy as jnp
        import numpy as np
        N_EXPERTS = 16
        TOP_K = int(N_EXPERTS * 0.2)
        EPS = 1e-12
        raw_gate = jax.nn.softmax(jnp.einsum('btd,de->bte', x, gate), axis=-1)
        _, topk_idx = jax.lax.top_k(raw_gate, TOP_K)
        mask = jax.nn.one_hot(topk_idx, raw_gate.shape[-1], dtype=raw_gate.dtype).sum(axis=2)
        gate_topk = mask * raw_gate
        gate_topk = gate_topk / jnp.maximum(jnp.sum(jnp.abs(gate_topk), axis=-1, keepdims=True), EPS)
        hidden = jax.nn.relu(jnp.einsum('btd,edh->bteh', x, W1) + b1)
        expert_out = jnp.einsum('bteh,ehd->bted', hidden, W2) + b2
        return jnp.einsum('bte,bted->btd', gate_topk, expert_out)

    def _L1_xattn_ref(x, latents, mask, ln_x_g, ln_x_b, ln_l_g, ln_l_b, q_gamma, k_gamma, W_q, W_kv, W_out, b_out):
        import jax, jax.numpy as jnp
        import numpy as np
        DIM = 512
        DIM_LATENT = 512
        DIM_HEAD = 64
        INNER = max(DIM, DIM_LATENT)
        HEADS = INNER // DIM_HEAD
        SCALE = DIM_HEAD ** (-0.5)
        LN_EPS = 1e-05
        RMS_EPS = 1e-08

        def layernorm(x, g, b):
            mu = jnp.mean(x, axis=-1, keepdims=True)
            var = jnp.mean(jnp.square(x - mu), axis=-1, keepdims=True)
            return (x - mu) * jax.lax.rsqrt(var + LN_EPS) * g + b

        def rmsnorm(x, gamma):
            n = jnp.linalg.norm(x, axis=-1, keepdims=True) * x.shape[-1] ** (-0.5)
            return x / jnp.maximum(n, RMS_EPS) * gamma
        b, n, _ = x.shape
        nl = latents.shape[1]
        xn = layernorm(x, ln_x_g, ln_x_b)
        ln = layernorm(latents, ln_l_g, ln_l_b)
        q = ln @ W_q
        kv = jnp.concatenate([xn @ W_kv, ln @ W_kv], axis=1)
        k, v = (kv[..., :INNER], kv[..., INNER:])
        to_heads = lambda t: t.reshape(t.shape[0], t.shape[1], HEADS, DIM_HEAD).transpose(0, 2, 1, 3)
        q, k, v = (to_heads(q), to_heads(k), to_heads(v))
        qn = rmsnorm(q, q_gamma) * SCALE
        kn = rmsnorm(k, k_gamma)
        sim = jnp.einsum('bhid,bhjd->bhij', qn, kn)
        full_mask = jnp.pad(mask, ((0, 0), (0, nl)), constant_values=True)
        neg = -jnp.finfo(sim.dtype).max
        sim = jnp.where(full_mask[:, None, None, :], sim, neg)
        attn = jax.nn.softmax(sim.astype(jnp.float32), axis=-1).astype(sim.dtype)
        out = jnp.einsum('bhij,bhjd->bhid', attn, v)
        out = out.transpose(0, 2, 1, 3).reshape(b, nl, INNER)
        return out @ W_out + b_out

    def _L1_ffn_ref(x, Wg, bg, Wi, Wo, A, B):
        import jax, jax.numpy as jnp
        import numpy as np
        TOP_K = 2
        E = Wg.shape[0]
        logits = jnp.einsum('bsd,ed->bse', x, Wg) + bg
        scores = jax.nn.softmax(logits, axis=-1)
        topv, topi = jax.lax.top_k(scores, TOP_K)
        w = jnp.sum(jax.nn.one_hot(topi, E, dtype=x.dtype) * topv[..., None], axis=-2)
        base = jnp.einsum('bsd,fd->bsf', x, Wi)
        lora_low = jnp.einsum('bsd,erd->bser', x, A)
        lora = jnp.einsum('bser,efr->bsef', lora_low, B)
        h = jax.nn.relu(base[:, :, None, :] + lora)
        expert_out = jnp.einsum('bsef,df->bsed', h, Wo)
        out = jnp.einsum('bse,bsed->bsd', w, expert_out)
        return out
    x = x + _L0_xattn_ref(ctx_1024, _layernorm(x, axis=-1))
    x = x + _L0_ffn_ref(_layernorm(x, axis=-1), L0_ffn_gate, L0_ffn_W1, L0_ffn_b1, L0_ffn_W2, L0_ffn_b2)
    x = x + _L1_xattn_ref(ctx_1024, _layernorm(x, axis=-1), mask_BxS2_bk0, L1_xattn_ln_x_g, L1_xattn_ln_x_b, L1_xattn_ln_l_g, L1_xattn_ln_l_b, L1_xattn_q_gamma, L1_xattn_k_gamma, L1_xattn_W_q, L1_xattn_W_kv, L1_xattn_W_out, L1_xattn_b_out)
    x = x + _L1_ffn_ref(_layernorm(x, axis=-1), L1_ffn_Wg, L1_ffn_bg, L1_ffn_Wi, L1_ffn_Wo, L1_ffn_A, L1_ffn_B)
    return x

_drawn_inputs = setup_inputs


def setup_inputs(seed=0):
    import zlib

    import numpy as np

    out = dict(_drawn_inputs(seed))
    spreads = {'L1_xattn_ln_x_g': (1.0, 0.6),
     'L1_xattn_ln_x_b': (0.0, 0.8),
     'L1_xattn_ln_l_g': (1.0, 0.6),
     'L1_xattn_ln_l_b': (0.0, 0.8),
     'L1_xattn_q_gamma': (1.0, 0.6),
     'L1_xattn_k_gamma': (1.0, 0.6),
     'L1_xattn_b_out': (0.0, 0.8),
     'L1_ffn_bg': (0.0, 2.0)}
    factors = {'L0_ffn_b1': 29.555,
     'L0_ffn_b2': 8.0,
     'L1_xattn_W_q': 8.0,
     'L1_xattn_W_kv': 2.759,
     'L1_xattn_W_out': 2.679,
     'L1_ffn_Wg': 8.0,
     'L1_ffn_Wi': 3.01,
     'L1_ffn_A': 8.0,
     'L1_ffn_B': 8.0}
    for name, (base, spread) in spreads.items():
        noise = np.random.default_rng([zlib.crc32(name.encode()), seed]).standard_normal(out[name].shape)
        drawn = base * np.exp(spread * noise) if base else spread * noise
        out[name] = jnp.asarray(drawn.astype(out[name].dtype))
    for name, factor in factors.items():
        out[name] = (out[name] * factor).astype(out[name].dtype)
    return out
```

```python
import numpy as np
import concourse.bass as bass
from concourse import mybir
from contextlib import ExitStack

FP32 = mybir.dt.float32
BF16 = mybir.dt.bfloat16
I32 = mybir.dt.int32
U32 = mybir.dt.uint32
ALU = mybir.AluOpType
ACT = mybir.ActivationFunctionType
AX = mybir.AxisListType.X

B, S, D = 8, 100, 512
C = 722
P = 128
KD = D // P
CT = -(-C // P)
CR = [min(P, C - P * t) for t in range(CT)]
NB = P // B
BL = -(-C // NB)
SK = 2
ST = S + SK * (NB - 1)
BIG = 1e30
EPS = 1e-5


def allocator(nc, ctx):
    used = []

    def clear():
        nc.clear_and_free_semaphores(used)
        nc.all_engine_barrier()
    ctx.callback(clear)

    def sb(name, shape, dt=FP32):
        return ctx.enter_context(nc.sbuf_tensor(name, shape, dt))

    def pb(name, shape):
        n = 1
        for m in shape[1:]:
            n *= m
        bank = ctx.enter_context(nc.psum_tensor(name, [P, 512], FP32))[0:shape[0], 0:n]
        return bank if len(shape) == 2 else bank.rearrange("p (a b) -> p a b", b=shape[2])

    def sem(name):
        used.append(nc.alloc_semaphore(name))
        return used[-1]
    return sb, pb, sem


def make_linker(eng, sem):
    def link(ins):
        sem[1] += 1
        ins.then_inc(sem[0], 1)
        eng.wait_ge(sem[0], sem[1])
    return link


def distances(nc, io, res):
    ctx = ExitStack()
    with ctx:
        sb, pb, sem = allocator(nc, ctx)
        x_sb, ctx_rows, ident = res["x"], res["ctx_rows"], res["ident"]
        ones = res["ones"]
        xl = sb("xl", [S, B, D])
        stats = sb("stats_a", [S, B, 6])
        mv = sb("mv_a", [S, B, 2])
        rstd = sb("rstd_a", [S, B])
        xlT = sb("xlT", [P, KD, B * S])
        xlq = sb("xlq", [P, KD, B * S])
        bb = sb("bb", [P, B * S])
        cT = [sb(f"cT{i}", [P, KD, C]) for i in range(2)]
        aa = sb("aa", [P, B * CT])
        sqj = sb("sqj", [P, D])
        d2 = sb("d2", [P, 2, CT, S])
        ds = sb("ds", [P, 2, CT, S])
        tp = [pb(f"tpa{i}", [P, KD, P]) for i in range(2)]
        pbb = [pb(f"pbb{i}", [P, 512]) for i in range(2)]
        pd = [pb(f"pd{i}", [P, 512]) for i in range(2)]
        x_in, rows_in, id0, id1, on = sem("x_in"), [sem(f"rows_in{b}") for b in range(B)], sem("id0"), sem("id1"), sem("ones_set")
        ct_in = [sem(f"ct_in{i}") for i in range(2)]
        st_ok, var_ok, rs_ok, xl_ok = sem("st_ok"), sem("var_ok"), sem("rs_ok"), sem("xl_ok")
        tp_ok, xt_ok, xq_ok, bb_mm, bb_ok = sem("tp_ok"), sem("xt_ok"), sem("xq_ok"), sem("bb_mm"), sem("bb_ok")
        aa_ok, pd_ok, d2_ok, ds_ok = sem("aa_ok"), sem("pd_ok"), sem("d2_ok"), sem("ds_ok")
        ds_out = [sem(f"ds_out{i}") for i in range(2)]
        zf, z_ok = sem("zf"), sem("z_ok")
        TPT = 3
        block = ctx.enter_context(nc.Block())

        def store(sp, b):
            sp.wait_ge(ds_ok, b + 1)
            sp.dma_start(res["dist"][b, 0:P * (CT - 1), :].rearrange("(t p) j -> p t j", p=P),
                         ds[:, b % 2, 0:CT - 1, :]).then_inc(ds_out[b % 2], 16)
            sp.dma_start(res["dist"][b, P * (CT - 1):C, :], ds[0:CR[-1], b % 2, CT - 1, :]).then_inc(ds_out[b % 2], 16)

        @block.sync
        def _(sp):
            sp.dma_start(x_sb[:, :, :], io["x"].rearrange("b s d -> s b d")).then_inc(x_in, 16)
            for b in range(B):
                if b >= 2:
                    sp.wait_ge(pd_ok, 2 * (b - 1))
                sp.dma_start(cT[b % 2][:, :, :], io["ctxT"][b].rearrange("(k p) c -> p k c", p=P)).then_inc(ct_in[b % 2], 16)
                sp.dma_start(ctx_rows[:, b * CT:b * CT + CT - 1, :],
                             io["ctx"][b, 0:P * (CT - 1), :].rearrange("(t p) d -> p t d", p=P)).then_inc(rows_in[b], 16)
                sp.dma_start(ctx_rows[0:CR[-1], b * CT + CT - 1, :], io["ctx"][b, P * (CT - 1):C, :]).then_inc(rows_in[b], 16)
                if b >= 2:
                    store(sp, b - 2)
            store(sp, B - 2)
            store(sp, B - 1)
            for i in range(2):
                sp.wait_ge(ds_out[i], 32 * (B // 2))

        @block.gpsimd
        def _(pool):
            pool.memset(ident[:, :], 0.0).then_inc(id0, 1)
            pool.memset(ones[:, :], 1.0).then_inc(on, 1)
            pool.wait_ge(id0, 1)
            pool.affine_select(out=ident[:, :], in_=ident[:, :], compare_op=ALU.not_equal, fill=1.0, base=0,
                               pattern=[[-1, P]], channel_multiplier=1).then_inc(id1, 1)

        @block.vector
        def _(dve):
            link = make_linker(dve, res["dve_chain"])
            dve.memset(aa[:, :], 0.0).then_inc(res["z0"], 1)
            dve.memset(d2[:, :, :, :], 0.0).then_inc(zf, 1)
            dve.wait_ge(x_in, 16)
            for b in range(B):
                ins = dve.bn_stats(stats[:, b, :], x_sb[:, b, :])
            link(ins)
            for b in range(B):
                ins = dve.bn_aggr(mv[:, b, :], stats[:, b, :])
            link(ins)
            dve.tensor_scalar(rstd[:, :], mv[:, :, 1], EPS, None, ALU.add).then_inc(var_ok, 1)
            dve.wait_ge(st_ok, 1)
            link(dve.reciprocal(rstd[:, :], rstd[:, :]))
            for b in range(B):
                dve.tensor_scalar(xl[:, b, :], x_sb[:, b, :], mv[:, b, 0:1], rstd[:, b:b + 1],
                                  ALU.subtract, ALU.mult).then_inc(xl_ok, 1)
            for b in range(B):
                dve.wait_ge(tp_ok, b + 1)
                dve.tensor_scalar(xlT[:, :, b * S:(b + 1) * S], tp[b % 2][:, :, 0:S], -2.0, None, ALU.mult).then_inc(xt_ok, 1)
            for g in range(2):
                dve.wait_ge(bb_mm, g + 1)
                dve.tensor_copy(bb[:, g * 400:(g + 1) * 400], pbb[g][:, 0:400]).then_inc(bb_ok, 1)
            dve.wait_ge(bb_ok, 2)
            for b in range(B):
                dve.wait_ge(aa_ok, CT * (b + 1))
                if b >= 2:
                    dve.wait_ge(ds_ok, b - 1)
                for t in range(CT):
                    if t % TPT == 0:
                        dve.wait_ge(pd_ok, 2 * b + t // TPT + 1)
                    r, q = CR[t], t % TPT
                    ins = dve.scalar_tensor_tensor(d2[0:r, b % 2, t, :], pd[t // TPT][0:r, q * S:(q + 1) * S],
                                                   aa[0:r, b * CT + t:b * CT + t + 1], bb[0:r, b * S:(b + 1) * S],
                                                   ALU.add, ALU.add)
                    if q == TPT - 1:
                        ins.then_inc(d2_ok, 1)
                dve.wait_ge(d2_ok, 2 * b + 2)
                dve.tensor_scalar(d2[:, b % 2, :, :], d2[:, b % 2, :, :], 0.0, None, ALU.max).then_inc(rs_ok, 1)

        def roots(act, b):
            act.wait_ge(rs_ok, b + 1)
            if b >= 2:
                act.wait_ge(ds_out[b % 2], 32 * (b // 2))
            act.activation(ds[:, b % 2, :, :], d2[:, b % 2, :, :], ACT.Sqrt).then_inc(ds_ok, 1)

        @block.scalar
        def _(act):
            act.wait_ge(var_ok, 1)
            act.activation(rstd[:, :], rstd[:, :], ACT.Sqrt).then_inc(st_ok, 1)
            n = 0
            for g in range(2):
                act.wait_ge(xt_ok, 4 * g + 4)
                act.activation(xlq[:, :, g * 400:(g + 1) * 400], xlT[:, :, g * 400:(g + 1) * 400], ACT.Square,
                               scale=0.5).then_inc(xq_ok, 1)
            act.wait_ge(res["z0"], 1)
            for b in range(B):
                act.wait_ge(rows_in[b], 32)
                for t in range(CT):
                    if n:
                        act.wait_ge(aa_ok, n)
                    r = CR[t]
                    act.activation(sqj[0:r, :], ctx_rows[0:r, b * CT + t, :], ACT.Square,
                                   accum_out=aa[0:r, b * CT + t:b * CT + t + 1]).then_inc(aa_ok, 1)
                    n += 1
                if b >= 1:
                    roots(act, b - 1)
            roots(act, B - 1)

        @block.tensor
        def _(pe):
            pe.wait_ge(id1, 1)
            pe.wait_ge(on, 1)
            for b in range(B):
                pe.wait_ge(xl_ok, b + 1)
                if b >= 2:
                    pe.wait_ge(xt_ok, b - 1)
                for k in range(KD):
                    ins = pe.transpose(tp[b % 2][:, k, 0:S], xl[:, b, k * P:(k + 1) * P], ident[0:S, 0:S])
                ins.then_inc(tp_ok, 1)
            for g in range(2):
                pe.wait_ge(xq_ok, g + 1)
                for k in range(KD):
                    ins = pe.matmul(pbb[g][:, 0:400], ones[:, :], xlq[:, k, g * 400:(g + 1) * 400], start=k == 0, stop=k == KD - 1)
                ins.then_inc(bb_mm, 1)
            for b in range(B):
                pe.wait_ge(ct_in[b % 2], 16 * (b // 2 + 1))
                for t in range(CT):
                    r, q = CR[t], t % TPT
                    if q == 0 and b >= 1:
                        pe.wait_ge(d2_ok, 2 * b + t // TPT - 1)
                    for k in range(KD):
                        ins = pe.matmul(pd[t // TPT][0:r, q * S:(q + 1) * S], cT[b % 2][:, k, t * P:t * P + r],
                                        xlT[:, k, b * S:(b + 1) * S], start=k == 0, stop=k == KD - 1)
                    if q == TPT - 1:
                        ins.then_inc(pd_ok, 1)


def warp(nc, io, res):
    ctx = ExitStack()
    with ctx:
        sb, pb, sem = allocator(nc, ctx)
        cost_mem = sb("cost_mem", [P, (BL + 2) * ST])
        cost = cost_mem[:, 0:BL * ST].rearrange("p (a s) -> p a s", s=ST)
        path = cost_mem[:, 0:(BL + 2) * ST // 2].bitcast(BF16).rearrange("p (a s) -> p a s", s=ST)
        rise = cost_mem[:, (BL + 2) * ST // 2:(BL + 2) * ST].bitcast(BF16).rearrange("p (a s) -> p a s", s=ST)
        reach_mem = sb("reach_mem", [P, (BL + 2) * ST])
        reach = reach_mem[:, 0:(BL + 1) * (ST + 1)].rearrange("p (a s) -> p a s", s=ST + 1)
        reach_up = sb("reach_up", [P, BL + 1, ST + 1])
        path_down = reach_up[:, :, :].rearrange("p a s -> p (a s)")[:, 0:BL * ST // 2 + 1].bitcast(BF16)[:, 0:BL * ST].rearrange("p (a s) -> p a s", s=ST)
        step_min = sb("step_min", [P, BL])
        topcol = sb("topcol", [P, 1])
        lastrow = sb("lastrow", [P, 1])
        down = sb("down", [P, P])
        up = sb("up", [P, P], BF16)
        move = reach_mem[:, :].bitcast(BF16).rearrange("p (m a s) -> p m a s", m=2, s=ST)
        CH = ST // 5
        best = sb("best", [P, BL, CH])
        flow = sb("flow", [P, 2, BL + 2], BF16)
        into = sb("into", [P, BL + 1], BF16)
        ph = [pb(f"ph{i}", [P, 512]) for i in range(4)]
        c_in, c_set, k_set, k2_set = sem("c_in"), sem("c_set"), sem("k_set"), sem("k2_set")
        scanned, handed, scanned_r, handed_r = sem("scanned"), sem("handed"), sem("scanned_r"), sem("handed_r")
        topped, least, flowed, summed = sem("topped"), sem("least"), sem("flowed"), sem("summed")
        p_out, zero_set, z_out = sem("p_out"), sem("zero_set"), sem("z_out")
        turned, row_out = sem("turned"), sem("row_out")
        zero = sb("zero", [P, D])
        last_rows = C - (NB - 1) * BL
        U = len(ph)
        block = ctx.enter_context(nc.Block())

        def turn_rows(eng, copy, k):
            eng.wait_ge(scanned, ST)
            for a in range(k, BL + 1, 3):
                copy(reach_up[:, BL - a, :], reach[:, a, :]).then_inc(turned, 1)

        def rows_out(eng, copy, k):
            eng.wait_ge(scanned_r, ST)
            for a in range(k, BL, 3):
                copy(path_down[:, a, :], path[:, BL - a, :]).then_inc(row_out, 1)

        @block.sync
        def _(sp):
            sp.wait_ge(c_set, 1)
            for k in range(NB):
                r = BL if k < NB - 1 else last_rows
                sp.dma_start(cost[k * B:(k + 1) * B, 0:r, SK * k:SK * k + S],
                             res["dist"][:, k * BL:k * BL + r, :]).then_inc(c_in, 16)
            sp.wait_ge(zero_set, 1)
            for t in range(SLOT_TILES):
                sp.dma_start(res["xg"][t * P:(t + 1) * P, :], zero[:, :]).then_inc(z_out, 16)
                sp.dma_start(res["yg"][t * P:(t + 1) * P, :], zero[:, :]).then_inc(z_out, 16)
            sp.wait_ge(row_out, BL)
            for k in range(NB):
                r = BL if k < NB - 1 else last_rows
                sp.dma_start(res["path"][:, k * BL:k * BL + r, :],
                             path_down[k * B:(k + 1) * B, 0:r, SK * k:SK * k + S]).then_inc(p_out, 16)
            sp.wait_ge(p_out, 16 * NB)
            sp.wait_ge(z_out, 32 * SLOT_TILES)

        @block.gpsimd
        def _(pool):
            pool.memset(reach[:, 0, 0:SK + 1], BIG).then_inc(k_set, 1)
            pool.memset(reach[:, 1:BL + 1, 0], BIG).then_inc(k_set, 1)
            pool.memset(topcol[:, :], 0.0).then_inc(k_set, 1)
            pool.memset(down[:, :], 0.0).then_inc(k_set, 1)
            pool.memset(up[:, :], 0.0).then_inc(k_set, 1)
            pool.memset(lastrow[:, :], 0.0).then_inc(k_set, 1)
            pool.wait_ge(k_set, 6)
            pool.affine_select(out=lastrow[:, :], in_=lastrow[:, :], compare_op=ALU.is_gt, fill=1.0, base=P - B,
                               pattern=[[0, 1]], channel_multiplier=-1).then_inc(k2_set, 1)
            pool.memset(reach[0:B, 0, 0:1], 0.0).then_inc(k2_set, 1)
            pool.memset(topcol[0:B, :], BIG).then_inc(k2_set, 1)
            pool.affine_select(out=down[:, :], in_=down[:, :], compare_op=ALU.not_equal, fill=1.0, base=B,
                               pattern=[[-1, P]], channel_multiplier=1).then_inc(k2_set, 1)
            pool.affine_select(out=up[:, :], in_=up[:, :], compare_op=ALU.not_equal, fill=1.0, base=-B,
                               pattern=[[-1, P]], channel_multiplier=1).then_inc(k2_set, 1)

            turn_rows(pool, pool.tensor_copy, 1)
            rows_out(pool, pool.tensor_copy, 1)

        @block.scalar
        def _(act):
            for s in range(SK, ST):
                act.wait_ge(handed, s - SK + 1)
                act.activation(reach[:, 0, s + 1:s + 2], ph[(s - SK) % U][:, 0:1], ACT.Identity, bias=topcol[:, 0:1]).then_inc(topped, 1)
            turn_rows(act, act.copy, 2)
            rows_out(act, act.copy, 2)

        def col(a, d):
            return a.rearrange("p a o -> p (a o)") if d == 2 else a.rearrange("p m a o -> p m (a o)")

        def col2(a):
            return a.rearrange("p a o -> p o a").broadcast_to([P, 2, BL + 2])


        @block.tensor
        def _(pe):
            pe.wait_ge(k2_set, 5)

            def hand(s, u):
                pe.wait_ge(scanned, s + 1)
                pe.matmul(ph[u][:, 0:1], down[:, :], reach[:, BL, s + 1:s + 2], start=True, stop=True).then_inc(handed, 1)

            for s in range(ST - SK):
                hand(s, s % U)

            def hand_back(n, s, u):
                pe.wait_ge(scanned_r, n + 1)
                pe.matmul(ph[u][:, 0:1], up[:, :], path[:, BL + 1, s:s + 1], start=True, stop=True).then_inc(handed_r, 1)

            for n in range(ST - SK):
                hand_back(n, ST - 1 - n, n % U)

        @block.vector
        def _(dve):
            link = make_linker(dve, res["dve_chain"])
            dve.memset(cost[:, :, :], BIG).then_inc(c_set, 1)
            dve.memset(zero[:, :], 0.0).then_inc(zero_set, 1)
            dve.wait_ge(k2_set, 5)
            dve.wait_ge(c_in, 16 * NB)
            def step(s, u):
                if s:
                    dve.wait_ge(scanned, s)
                dve.tensor_tensor(step_min[:, :], col(reach[:, 1:BL + 1, s:s + 1], 2),
                                  col(reach[:, 0:BL, s:s + 1], 2), ALU.min).then_inc(least, 1)
                if u is not None:
                    dve.wait_ge(topped, s - SK + 1)
                dve.wait_ge(least, s + 1)
                dve.tensor_tensor_scan(col(reach[:, 1:BL + 1, s + 1:s + 2], 2), step_min[:, :],
                                       col(cost[:, :, s:s + 1], 2), reach[:, 0, s + 1:s + 2],
                                       ALU.min, ALU.add).then_inc(scanned, 1)

            for s in range(SK):
                step(s, None)
            for s in range(SK, ST):
                step(s, (s - SK) % U)


            turn_rows(dve, dve.tensor_copy, 0)
            dve.memset(path[:, 0, :], 0.0)
            dve.memset(rise[:, 0, :], 1.0)
            dve.memset(rise[:, BL + 1, :], 0.0)
            dve.wait_ge(turned, BL + 1)
            dve.memset(move[:, :, 0, :], 0.0)
            link(dve.memset(move[:, :, BL + 1, :], 0.0))
            for c in range(0, ST, CH):
                cd, cu, cl = reach_up[:, 1:BL + 1, c:c + CH], reach_up[:, 1:BL + 1, c + 1:c + CH + 1], reach_up[:, 0:BL, c:c + CH]
                lf, dg, rs = move[:, 0, 1:BL + 1, c:c + CH], move[:, 1, 1:BL + 1, c:c + CH], rise[:, 1:BL + 1, c:c + CH]
                link(dve.tensor_tensor(best[:, :, :], cu, cl, ALU.min))
                link(dve.tensor_tensor(lf, cl, cu, ALU.is_lt))
                link(dve.tensor_tensor(dg, cd, best[:, :, :], ALU.is_le))
                link(dve.scalar_tensor_tensor(lf, dg, 0.5, lf, ALU.is_lt, ALU.mult))
                link(dve.tensor_tensor(rs, dg, lf, ALU.is_equal))

            seed = dve.memset(into[:, :], 0.0)
            link(seed)
            link(dve.tensor_copy(into[:, BL - last_rows:BL - last_rows + 1], lastrow[:, 0:1]))

            def back(n, s, u):
                if n:
                    dve.wait_ge(scanned_r, n)
                    dve.tensor_tensor(flow[:, :, :], col(move[:, :, :, s + 1:s + 2], 3),
                                      col2(path[:, :, s + 1:s + 2]), ALU.mult).then_inc(flowed, 1)
                    dve.wait_ge(flowed, n)
                    dve.tensor_tensor(into[:, :], flow[:, 0, 1:BL + 2], flow[:, 1, 0:BL + 1], ALU.add).then_inc(summed, 1)
                    dve.wait_ge(summed, n)
                if u is not None:
                    dve.wait_ge(handed_r, n - SK + 1)
                dve.tensor_tensor_scan(col(path[:, 1:BL + 2, s:s + 1], 2), col(rise[:, 0:BL + 1, s:s + 1], 2), into[:, :],
                                       0.0 if u is None else ph[u][:, 0:1], ALU.mult, ALU.add).then_inc(scanned_r, 1)

            for n in range(SK):
                back(n, ST - 1 - n, None)
            for n in range(SK, ST):
                back(n, ST - 1 - n, (n - SK) % U)
            rows_out(dve, dve.tensor_copy, 0)



E_N, H = 16, 1024
HJ = H // P
TOPK = 3
SLOT_TILES = B * S * TOPK // P + E_N
XT = B * S


def layernorm_stats(link, dve, src, stats, mv, n):
    for i in range(n):
        ins = dve.bn_stats(stats[:, i, :], src[:, i, :])
    link(ins)
    for i in range(n):
        ins = dve.bn_aggr(mv[:, i, :], stats[:, i, :])
    link(ins)


def route(nc, io, res):
    ctx = ExitStack()
    with ctx:
        sb, pb, sem = allocator(nc, ctx)
        x_sb, ctx_rows, ident, ones = res["x"], res["ctx_rows"], res["ident"], res["ones"]
        pathb = sb("pathb", [P, B * CT, S], BF16)
        pathf = sb("pathf", [P, B * CT, S])
        gate_w = sb("gate_w", [P, KD, E_N])
        xn = sb("xn", [S, B, D])
        stats, mv, rstd = sb("stats_c", [S, B, 6]), sb("mv_c", [S, B, 2]), sb("rstd_c", [S, B])
        xnT = [sb(f"xnT{i}", [P, KD, S]) for i in range(2)]
        logit = sb("logit", [S, B, E_N])
        prob = sb("prob", [S, B, E_N])
        lmax, lsum = sb("lmax", [S, B]), sb("lsum", [S, B])
        top = sb("top", [S, B, 8])
        topi = sb("topi", [S, B, 8], U32)
        topf = sb("topf", [S, B, 8])
        tsum = sb("tsum", [S, B])
        iota_e = sb("iota_e", [S, E_N])
        hot = [sb(f"hot{k}", [S, B, E_N]) for k in range(TOPK)]
        chosen = sb("chosen", [S, B, E_N])
        before = sb("before", [S, S])
        tot = sb("tot", [S, B, E_N])
        off = sb("off", [S, B + 1, E_N])
        ntile, tiles_to, one_e = sb("ntile", [S, E_N]), sb("tiles_to", [S, E_N]), sb("one_e", [S, E_N])
        slot = sb("slot", [S, B, E_N])
        picked = sb("picked", [S, B, E_N])
        slotf = sb("slotf", [S, TOPK, B])
        px = [pb(f"px{i}", [S, D]) for i in range(2)]
        pt = [pb(f"pt{i}", [P, KD, P]) for i in range(2)]
        pl = pb("pl", [S, B, E_N])
        prank = pb("prank", [S, B * E_N])
        ptot = pb("ptot", [S, B, E_N])
        path_in, gate_in = sem("path_in"), sem("gate_in")
        pathf_ok, px_ok, x_ok, var_ok, st_ok, xn_ok = (sem(n) for n in ("pathf_ok", "px_ok", "x_ok", "var_c", "st_c", "xn_ok"))
        pt_ok, xnT_ok, pl_ok, sub_ok, exp_ok, cs_ok = (sem(n) for n in ("pt_ok", "xnT_ok", "pl_ok", "sub_ok", "exp_ok", "cs_ok"))
        cs0, hot_ok, rank_ok, slot_ok, sent = (sem(n) for n in ("cs0", "hot_ok", "rank_ok", "slot_ok", "sent"))
        block = ctx.enter_context(nc.Block())

        @block.sync
        def _(sp):
            sp.dma_start(gate_w[:, :, :], io["gate"].rearrange("(k p) e -> p k e", p=P)).then_inc(gate_in, 16)
            for b in range(B):
                sp.dma_start(pathb[:, b * CT:b * CT + CT - 1, :],
                             res["path"][b, 0:P * (CT - 1), :].rearrange("(t p) j -> p t j", p=P)).then_inc(path_in, 16)
                sp.dma_start(pathb[0:CR[-1], b * CT + CT - 1, :], res["path"][b, P * (CT - 1):C, :]).then_inc(path_in, 16)

        @block.gpsimd
        def _(pool):
            pool.iota(iota_e[:, :], pattern=[[1, E_N]], base=0, channel_multiplier=0,
                      allow_small_or_imprecise_dtypes=True).then_inc(cs_ok, 1)
            pool.memset(before[:, :], 1.0).then_inc(cs0, 1)
            pool.wait_ge(cs0, 1)
            pool.affine_select(out=before[:, :], in_=before[:, :], compare_op=ALU.is_gt, fill=0.0, base=0,
                               pattern=[[1, S]], channel_multiplier=-1).then_inc(cs_ok, 1)
            pool.wait_ge(slot_ok, 1)
            for k in range(TOPK):
                for b in range(B):
                    pool.indirect_dma_start(out=res["xg"], out_offset=bass.IndirectOffsetOnAxis(ap=res["slots"][:, k * B + b:k * B + b + 1], axis=0),
                                            in_=xn[:, b, :], in_offset=None).then_inc(sent, 16)
            pool.wait_ge(sent, 16 * TOPK * B)

        @block.tensor
        def _(pe):
            for b in range(B):
                pe.wait_ge(pathf_ok, b + 1)
                if b >= 2:
                    pe.wait_ge(x_ok, b - 1)
                for t in range(CT):
                    r = CR[t]
                    ins = pe.matmul(px[b % 2][:, :], pathf[0:r, b * CT + t, :], ctx_rows[0:r, b * CT + t, :], start=t == 0, stop=t == CT - 1)
                ins.then_inc(px_ok, 1)
            pe.wait_ge(gate_in, 16)
            for b in range(B):
                pe.wait_ge(xn_ok, b + 1)
                if b >= 2:
                    pe.wait_ge(xnT_ok, b - 1)
                for k in range(KD):
                    ins = pe.transpose(pt[b % 2][:, k, 0:S], xn[:, b, k * P:(k + 1) * P], ident[0:S, 0:S])
                ins.then_inc(pt_ok, 1)
                pe.wait_ge(xnT_ok, b + 1)
                for k in range(KD):
                    ins = pe.matmul(pl[:, b, :], xnT[b % 2][:, k, :], gate_w[:, k, :], start=k == 0, stop=k == KD - 1)
                ins.then_inc(pl_ok, 1)
            pe.wait_ge(hot_ok, 1)
            pe.wait_ge(cs_ok, 2)
            pe.matmul(prank[:, :], before[:, :], chosen[:, :, :].rearrange("p b e -> p (b e)"), start=True, stop=True).then_inc(rank_ok, 1)
            pe.matmul(ptot[:, :, :].rearrange("p b e -> p (b e)"), ones[0:S, 0:S], chosen[:, :, :].rearrange("p b e -> p (b e)"), start=True, stop=True).then_inc(rank_ok, 1)

        @block.scalar
        def _(act):
            act.wait_ge(var_ok, 1)
            act.activation(rstd[:, :], rstd[:, :], ACT.Sqrt).then_inc(st_ok, 1)
            act.wait_ge(sub_ok, 1)
            act.activation(prob[:, :, :], logit[:, :, :], ACT.Exp).then_inc(exp_ok, 1)

        @block.vector
        def _(dve):
            link = make_linker(dve, res["dve_chain"])
            dve.memset(one_e[:, :], 1.0)
            dve.wait_ge(path_in, 32 * B)
            for b in range(B):
                n = b * CT
                dve.tensor_copy(pathf[:, n:n + CT - 1, :], pathb[:, n:n + CT - 1, :])
                dve.tensor_copy(pathf[0:CR[-1], n + CT - 1, :], pathb[0:CR[-1], n + CT - 1, :]).then_inc(pathf_ok, 1)
            for b in range(B):
                dve.wait_ge(px_ok, b + 1)
                dve.tensor_tensor(x_sb[:, b, :], x_sb[:, b, :], px[b % 2][:, :], ALU.add).then_inc(x_ok, 1)
            dve.wait_ge(x_ok, B)
            layernorm_stats(link, dve, x_sb, stats, mv, B)
            dve.tensor_scalar(rstd[:, :], mv[:, :, 1], EPS, None, ALU.add).then_inc(var_ok, 1)
            dve.wait_ge(st_ok, 1)
            link(dve.reciprocal(rstd[:, :], rstd[:, :]))
            for b in range(B):
                dve.tensor_scalar(xn[:, b, :], x_sb[:, b, :], mv[:, b, 0:1], rstd[:, b:b + 1], ALU.subtract, ALU.mult).then_inc(xn_ok, 1)
            for b in range(B):
                dve.wait_ge(pt_ok, b + 1)
                if b >= 2:
                    dve.wait_ge(pl_ok, b - 1)
                dve.tensor_copy(xnT[b % 2][:, :, :], pt[b % 2][:, :, 0:S]).then_inc(xnT_ok, 1)
            dve.wait_ge(pl_ok, B)
            link(dve.tensor_reduce(lmax[:, :], pl[:, :, :], AX, ALU.max))
            dve.tensor_tensor(logit[:, :, :], pl[:, :, :], lmax[:, :].unsqueeze(2).broadcast_to([S, B, E_N]), ALU.subtract).then_inc(sub_ok, 1)
            dve.wait_ge(exp_ok, 1)
            link(dve.tensor_reduce(lsum[:, :], prob[:, :, :], AX, ALU.add))
            link(dve.reciprocal(lsum[:, :], lsum[:, :]))
            link(dve.tensor_tensor(prob[:, :, :], prob[:, :, :], lsum[:, :].unsqueeze(2).broadcast_to([S, B, E_N]), ALU.mult))
            for b in range(B):
                ins = dve.max(top[:, b, :], prob[:, b, :])
            link(ins)
            for b in range(B):
                ins = dve.max_index(topi[:, b, :], top[:, b, :], prob[:, b, :])
            link(ins)
            link(dve.tensor_copy(topf[:, :, :], topi[:, :, :]))
            dve.wait_ge(cs_ok, 2)
            for k in range(TOPK):
                ins = dve.tensor_tensor(hot[k][:, :, :], iota_e[:, :].unsqueeze(1).broadcast_to([S, B, E_N]),
                                        topf[:, :, k:k + 1].broadcast_to([S, B, E_N]), ALU.is_equal)
            link(ins)
            link(dve.tensor_tensor(chosen[:, :, :], hot[0][:, :, :], hot[1][:, :, :], ALU.add))
            ins = dve.tensor_tensor(chosen[:, :, :], chosen[:, :, :], hot[2][:, :, :], ALU.add)
            ins.then_inc(hot_ok, 1)
            link(dve.tensor_reduce(tsum[:, :], top[:, :, 0:TOPK], AX, ALU.add))
            link(dve.tensor_scalar(tsum[:, :], tsum[:, :], 1e-12, None, ALU.max))
            link(dve.reciprocal(tsum[:, :], tsum[:, :]))
            for k in range(TOPK):
                dve.tensor_tensor(res["gates"][:, k, :], top[:, :, k], tsum[:, :], ALU.mult)
            dve.wait_ge(rank_ok, 2)
            dve.memset(off[:, 0, :], 0.0)
            link(dve.tensor_copy(tot[:, :, :], ptot[:, :, :]))
            for b in range(B):
                link(dve.tensor_tensor(off[:, b + 1, :], off[:, b, :], tot[:, b, :], ALU.add))
            link(dve.memset(ntile[:, :], 1.0))
            for m in range(1, -(-XT // P)):
                link(dve.scalar_tensor_tensor(ntile[:, :], off[:, B, :], float(P * m), ntile[:, :], ALU.is_gt, ALU.add))
            link(dve.tensor_tensor_scan(tiles_to[:, :], one_e[:, :], ntile[:, :], 0.0, ALU.mult, ALU.add))
            dve.memset(res["table"][:, 0:1], 0)
            dve.tensor_copy(res["table"][:, 1:E_N + 1], tiles_to[:, :])
            link(dve.tensor_tensor(ntile[:, :], tiles_to[:, :], ntile[:, :], ALU.subtract))
            link(dve.tensor_tensor(slot[:, :, :], prank[:, :].rearrange("p (b e) -> p b e", e=E_N), off[:, 0:B, :], ALU.add))
            link(dve.scalar_tensor_tensor(slot[:, :, :], ntile[:, :].unsqueeze(1).broadcast_to([S, B, E_N]), float(P), slot[:, :, :], ALU.mult, ALU.add))
            for k in range(TOPK):
                link(dve.tensor_tensor(picked[:, :, :], hot[k][:, :, :], slot[:, :, :], ALU.mult))
                link(dve.tensor_reduce(slotf[:, k, :], picked[:, :, :], AX, ALU.add))
            dve.tensor_copy(res["slots"][:, :], slotf[:, :, :].rearrange("p k b -> p (k b)")).then_inc(slot_ok, 1)


INNER, HEADS, DH = 512, 8, 64
KC = P
NK = KC + S
NKD = C + S


def keep_rows(io, res, sb, sem, banks):
    mask8 = sb("mask8", [P, CT, B], mybir.dt.uint8)
    kept = sb("kept", [P, CT, B], BF16)
    lower = sb("lower", [P, P], BF16)
    onesb = sb("onesb", [P, P], BF16)
    slots_row = sb("slots_row", [P, KC])
    where = sb("where", [P, CT, 3], BF16)
    tot = sb("tot_k", [P, CT, B])
    off = sb("off_k", [P, CT + 1, B])
    pos = sb("pos_k", [P, CT, B])
    sel = [sb(f"sel{i}", [P, CT, KC], BF16) for i in range(2)]
    idxf = sb("idxf", [P, B])
    t128 = sb("t128", [P, B])
    base = sb("base_k", [P, B])
    idx = sb("idx_k", [P, B], I32)
    stats, mv, rstd = sb("stats_k", [P, B, 6]), sb("mv_k", [P, B, 2]), sb("rstd_k", [P, B])
    flag = sb("flag", [P, B])
    one8 = sb("one8", [P, B])
    runs = sb("runs", [P, B])
    kbias = res["kbias"]
    prk, ptk = banks[4][:, 0:CT * B], banks[4][:, CT * B:2 * CT * B]
    pidx = [banks[i][:, 0:3] for i in range(2)]
    pfil = [banks[2 + i][:, 0:KC] for i in range(2)]
    m_in, m0, cs0, cs, kept_ok, rk_ok, sel_ok, idx_mm, idx_rd, idx_ok = (sem(n) for n in (
        "m_in", "m0", "cs0k", "csk", "kept_ok", "rk_ok", "sel_ok", "idx_mm", "idx_rd", "idx_ok"))
    g_in, vark, sqk = sem("g_in"), sem("vark"), sem("sqk")

    def load(sp):
        sp.wait_ge(m0, 1)
        for t in range(CT):
            sp.dma_start(mask8[0:CR[t], t, :], io["maskT"][t * P:t * P + CR[t], :]).then_inc(m_in, 16)

    def constants(pool):
        pool.memset(lower[:, :], 1.0).then_inc(cs0, 1)
        pool.memset(onesb[:, :], 1.0).then_inc(cs, 1)
        pool.iota(slots_row[:, :], pattern=[[1, KC]], base=0, channel_multiplier=0,
                  allow_small_or_imprecise_dtypes=True).then_inc(cs, 1)
        pool.iota(where[:, :, 0], pattern=[[0, CT]], base=0, channel_multiplier=1,
                  allow_small_or_imprecise_dtypes=True).then_inc(cs, 1)
        pool.iota(where[:, :, 1], pattern=[[1, CT]], base=0, channel_multiplier=0,
                  allow_small_or_imprecise_dtypes=True).then_inc(cs, 1)
        pool.memset(where[:, :, 2], 1.0).then_inc(cs, 1)
        pool.iota(base[:, :], pattern=[[C, B]], base=0, channel_multiplier=0,
                  allow_small_or_imprecise_dtypes=True).then_inc(cs, 1)
        pool.wait_ge(cs0, 1)
        pool.affine_select(out=lower[:, :], in_=lower[:, :], compare_op=ALU.is_gt, fill=0.0, base=0,
                           pattern=[[1, P]], channel_multiplier=-1).then_inc(cs, 1)

    def gather(pool):
        pool.wait_ge(idx_ok, 1)
        for b in range(B):
            pool.indirect_dma_start(out=res["rows_k"][:, b, :], out_offset=None, in_=io["ctx"].rearrange("b c d -> (b c) d"),
                                    in_offset=bass.IndirectOffsetOnAxis(ap=idx[:, b:b + 1], axis=0)).then_inc(g_in, 16)

    def ranks(pe):
        pe.wait_ge(cs, 7)
        pe.wait_ge(kept_ok, 1)
        pe.matmul(prk[:, :], lower[:, :], kept[:, :, :].rearrange("p t b -> p (t b)"), start=True, stop=True).then_inc(rk_ok, 1)
        pe.matmul(ptk[:, :], onesb[:, :], kept[:, :, :].rearrange("p t b -> p (t b)"), start=True, stop=True).then_inc(rk_ok, 1)

    def choose(pe, b):
        pe.wait_ge(sel_ok, b + 1)
        if b >= 2:
            pe.wait_ge(idx_rd, b - 1)
        for t in range(CT):
            pe.matmul(pidx[b % 2][:, :], sel[b % 2][:, t, :], where[:, t, :], start=t == 0, stop=t == CT - 1)
        for t in range(CT):
            ins = pe.matmul(pfil[b % 2][:, :], onesb[:, :], sel[b % 2][:, t, :], start=t == 0, stop=t == CT - 1)
        ins.then_inc(idx_mm, 1)

    def root(act):
        act.wait_ge(vark, 1)
        act.activation(rstd[:, :], rstd[:, :], ACT.Sqrt).then_inc(sqk, 1)

    def read_index(dve, b):
        dve.wait_ge(idx_mm, b + 1)
        dve.tensor_copy(idxf[:, b:b + 1], pidx[b % 2][:, 0:1])
        dve.tensor_copy(t128[:, b:b + 1], pidx[b % 2][:, 1:2])
        dve.tensor_scalar(kbias[:, b, 0:KC], pfil[b % 2][0:S, :], -BIG, BIG, ALU.mult, ALU.add).then_inc(idx_rd, 1)

    def rows(dve, link):
        dve.memset(mask8[:, :, :], 0).then_inc(m0, 1)
        dve.memset(off[:, 0, :], 0.0)
        dve.memset(one8[:, :], 1.0)
        dve.memset(kbias[:, :, KC:NK], 0.0)
        dve.memset(res["runs"][:, 0:1], 0)
        dve.wait_ge(m_in, 16 * CT)
        dve.tensor_copy(kept[:, :, :], mask8[:, :, :]).then_inc(kept_ok, 1)
        dve.wait_ge(rk_ok, 2)
        link(dve.tensor_copy(tot[:, :, :], ptk[:, :].rearrange("p (t b) -> p t b", b=B)))
        for t in range(CT):
            link(dve.tensor_tensor(off[:, t + 1, :], off[:, t, :], tot[:, t, :], ALU.add))
        link(dve.tensor_tensor(pos[:, :, :], prk[:, :].rearrange("p (t b) -> p t b", b=B), off[:, 0:CT, :], ALU.add))
        link(dve.scalar_tensor_tensor(pos[:, :, :], pos[:, :, :], 1.0, kept[:, :, :], ALU.add, ALU.mult))
        link(dve.tensor_scalar(pos[:, :, :], pos[:, :, :], -1.0, None, ALU.add))
        link(dve.tensor_scalar(flag[:, :], off[:, CT, :], float(KC), None, ALU.is_gt))
        link(dve.tensor_tensor_scan(runs[:, :], one8[:, :], flag[:, :], 0.0, ALU.mult, ALU.add))
        dve.tensor_copy(res["flag"][:, :], flag[:, :])
        link(dve.tensor_copy(res["runs"][:, 1:B + 1], runs[:, :]))
        dve.wait_ge(cs, 7)
        for b in range(B):
            if b >= 2:
                dve.wait_ge(idx_mm, b - 1)
            for t in range(CT):
                ins = dve.tensor_scalar(sel[b % 2][:, t, :], slots_row[:, :], pos[:, t, b:b + 1], None, ALU.is_equal)
            ins.then_inc(sel_ok, 1)
            if b:
                read_index(dve, b - 1)
        read_index(dve, B - 1)
        dve.wait_ge(idx_rd, B)
        link(dve.scalar_tensor_tensor(idxf[:, :], t128[:, :], float(P), idxf[:, :], ALU.mult, ALU.add))
        link(dve.tensor_tensor(idxf[:, :], idxf[:, :], base[:, :], ALU.add))
        dve.tensor_copy(idx[:, :], idxf[:, :]).then_inc(idx_ok, 1)
        dve.wait_ge(g_in, 16 * B)
        rk = res["rows_k"]
        layernorm_stats(link, dve, rk, stats, mv, B)
        dve.tensor_scalar(rstd[:, :], mv[:, :, 1], EPS, None, ALU.add).then_inc(vark, 1)
        dve.wait_ge(sqk, 1)
        link(dve.reciprocal(rstd[:, :], rstd[:, :]))
        for b in range(B):
            dve.tensor_scalar(rk[:, b, :], rk[:, b, :], mv[:, b, 0:1], rstd[:, b:b + 1], ALU.subtract, ALU.mult)

    def free(act):
        act.wait_ge(idx_rd, B)
    return load, constants, gather, ranks, choose, root, rows, free


def experts(nc, io, res):
    ctx = ExitStack()
    with ctx:
        sb, pb, sem = allocator(nc, ctx)
        x_sb, ident = res["x"], res["ident"]
        W1 = [sb(f"W1_{u}", [P, KD, H]) for u in range(2)]
        W2 = [sb(f"W2_{u}", [P, HJ, D]) for u in range(2)]
        b1 = sb("b1", [P, E_N * HJ])
        b2 = [sb(f"b2_{u}", [P, D]) for u in range(2)]
        xgT = sb("xgT", [P, SLOT_TILES, KD * P])
        hT = sb("hT", [P, HJ, P])
        y = sb("y", [P, D])
        NY = 8
        yk = sb("yk", [P, NY, D])
        NX = 4
        xg = [yk[:, u, :] for u in range(NX)]
        NH = 4
        banks = [pb(f"phid{i}", [P, D]) for i in range(NH)]
        ph = [bank[:, 0:P] for bank in banks]
        py = pb("py", [P, D])
        ptx = [pb(f"ptx{i}", [P, KD * P]) for i in range(2)]
        w_in = [sem(f"w_in{u}") for u in range(2)]
        b1_in, xg_in = sem("b1_in"), [sem(f"xg_in{u}") for u in range(NX)]
        xt_mm, xt_ok, h_mm, relu_ok, y_mm, y_ok, y_out, y_free = (sem(n) for n in (
            "xt_mm", "xt_okd", "h_mm", "relu_ok", "y_mm", "y_ok", "y_out", "y_free"))
        yk_in = [sem(f"yk_in{i}") for i in range(NY)]
        added = sem("added")
        load_mask, constants, gather_kept, ranks, choose, root, keep_all, free = keep_rows(io, res, sb, sem, banks + [py])
        TAIL = SLOT_TILES - SLOT_TILES % NX
        HEAD = 2 * B
        block = ctx.enter_context(nc.Block())
        first_tile = res["table"]

        def tiles_of(eng, e):
            a = eng.value_load(first_tile[0:1, bass.ds(e, 1)], min_val=0, max_val=SLOT_TILES - 1)
            b = eng.value_load(first_tile[0:1, bass.ds(e + 1, 1)], min_val=1, max_val=SLOT_TILES)
            return a, b

        @block.sync
        def _(sp):
            def load(e, u):
                sp.dma_start(W1[u][:, :, :], io["W1"][bass.ds(e, 1), :, :].rearrange("o (k p) h -> p (o k) h", p=P)).then_inc(w_in[u], 16)
                sp.dma_start(W2[u][:, :, :], io["W2"][bass.ds(e, 1), :, :].rearrange("o (j p) d -> p (o j) d", p=P)).then_inc(w_in[u], 16)
                sp.dma_start(b2[u][:, :], io["b2"][bass.ds(e, 1), :].broadcast_to([P, D])).then_inc(w_in[u], 16)

            def load_x(w, u, wait=True):
                if wait:
                    sp.wait_ge(xt_mm, w + (1 - NX))
                sp.dma_start(xg[u][:, :], res["xg"][bass.ds(w * P, P), :]).then_inc(xg_in[u], 16)

            load_mask(sp)
            for u in range(NX):
                load_x(u, u, False)
            for w in range(NX, HEAD):
                load_x(w, w % NX)
            load(0, 0)
            sp.dma_start(b1[:, :], io["b1T"]).then_inc(b1_in, 16)
            with sp.Fori(HEAD, TAIL - 1, NX) as w:
                for u in range(NX):
                    load_x(w + u, u)
            for w in range(TAIL, SLOT_TILES):
                load_x(w, w % NX)
            load(1, 1)
            with sp.Fori(2, E_N - 1, 2) as e:
                for u in range(2):
                    done = sp.value_load(first_tile[0:1, bass.ds(e + (u - 1), 1)], min_val=1, max_val=SLOT_TILES)
                    sp.wait_ge(y_ok, done + 1)
                    load(e + u, u)

        @block.tensor
        def _(pe):
            def turn(w, u, wait=True):
                pe.wait_ge(xg_in[u], NX * (w - u) + 16)
                if wait:
                    pe.wait_ge(xt_ok, w - 1)
                for k in range(KD):
                    ins = pe.transpose(ptx[u % 2][:, k * P:(k + 1) * P], xg[u][:, k * P:(k + 1) * P], ident[:, :])
                ins.then_inc(xt_mm, 1)

            turn(0, 0, False)
            turn(1, 1, False)
            ranks(pe)
            for b in range(B):
                if b:
                    turn(2 * b, 2 * b % NX)
                    turn(2 * b + 1, (2 * b + 1) % NX)
                choose(pe, b)
            with pe.Fori(HEAD, TAIL - 1, NX) as w:
                for u in range(NX):
                    turn(w + u, u)
            for w in range(TAIL, SLOT_TILES):
                turn(w, w % NX)

            with pe.Fori(0, E_N - 1, 2) as e:
                for u in range(2):
                    t0, t1 = tiles_of(pe, e + u)
                    with pe.Fori(t0, t1) as w:
                        pe.wait_ge(w_in[u], 24 * e + 48)
                        pe.wait_ge(xt_ok, w + 1)
                        for j in range(HJ + 2):
                            if j < HJ:
                                pe.wait_ge(relu_ok, 8 * w + j + 1)
                                for k in range(KD):
                                    ins = pe.matmul(ph[j % NH][:, :], W1[u][:, k, j * P:(j + 1) * P],
                                                    xgT[:, bass.ds(w, 1), k * P:(k + 1) * P].rearrange("p o t -> p (o t)"), start=k == 0, stop=k == KD - 1)
                                ins.then_inc(h_mm, 1)
                            if j >= 2:
                                if j == 2:
                                    pe.wait_ge(y_ok, w + 1)
                                pe.wait_ge(relu_ok, 8 * w + j - 2 + 1 + NH)
                                ins = pe.matmul(py[:, :], hT[:, j - 2, :], W2[u][:, j - 2, :], start=j == 2, stop=j == HJ + 1)
                        ins.then_inc(y_mm, 1)

        @block.scalar
        def _(act):
            def keep(w, u):
                act.wait_ge(xt_mm, w + 1)
                act.copy(xgT[:, bass.ds(w, 1), :].rearrange("p o t -> p (o t)"), ptx[u][:, :]).then_inc(xt_ok, 1)

            with act.Fori(0, SLOT_TILES - 1, 2) as w:
                for u in range(2):
                    keep(w + u, u)
            root(act)
            act.wait_ge(b1_in, 16)
            free(act)
            act.memzero(hT[:, 0, :]).then_inc(relu_ok, NH)
            with act.Fori(0, E_N - 1, 2) as e:
                for u in range(2):
                    t0, t1 = tiles_of(act, e + u)
                    with act.Fori(t0, t1) as w:
                        for j in range(HJ):
                            act.wait_ge(h_mm, 8 * w + j + 1)
                            act.activation(hT[:, j, :], ph[j % NH][:, :], ACT.Relu,
                                           bias=b1[:, bass.ds((e + u) * HJ + j, 1)]).then_inc(relu_ok, 1)

        @block.vector
        def _(dve):
            dve.sem_inc(y_ok, 1)
            keep_all(dve, make_linker(dve, res["dve_chain"]))
            with dve.Fori(0, E_N - 1, 2) as e:
                for u in range(2):
                    t0, t1 = tiles_of(dve, e + u)
                    with dve.Fori(t0, t1) as w:
                        dve.wait_ge(w_in[u], 24 * e + 48)
                        dve.wait_ge(y_mm, w + 1)
                        dve.wait_ge(y_free, w + 1)
                        dve.tensor_tensor(y[:, :], py[:, :], b2[u][:, :], ALU.add).then_inc(y_ok, 1)
            for i in range(TOPK * B):
                b, k = i // TOPK, i % TOPK
                dve.wait_ge(yk_in[i % NY], 16 * (i // NY + 1))
                if k:
                    dve.wait_ge(added, i)
                dve.scalar_tensor_tensor(x_sb[:, b, :], yk[0:S, i % NY, :], res["gates"][:, k, b:b + 1], x_sb[:, b, :],
                                         ALU.mult, ALU.add).then_inc(added, 1)

        @block.gpsimd
        def _(pool):
            constants(pool)
            gather_kept(pool)
            last = pool.value_load(first_tile[0:1, E_N:E_N + 1], min_val=E_N, max_val=SLOT_TILES)
            pool.sem_inc(y_free, 1)
            with pool.Fori(0, last) as w:
                pool.wait_ge(y_ok, w + 2)
                pool.dma_start(res["yg"][bass.ds(w * P, P), :], y[:, :]).then_inc(y_out, 16)
                pool.wait_ge(y_out, 16 * w + 16)
                pool.sem_inc(y_free, 1)
            for i in range(TOPK * B):
                b, k = i // TOPK, i % TOPK
                if i >= NY:
                    pool.wait_ge(added, i - NY + 1)
                pool.indirect_dma_start(out=yk[0:S, i % NY, :], out_offset=None, in_=res["yg"],
                                        in_offset=bass.IndirectOffsetOnAxis(ap=res["slots"][:, k * B + b:k * B + b + 1], axis=0)).then_inc(yk_in[i % NY], 16)


def attend(nc, io, res):
    ctx = ExitStack()
    with ctx:
        sb, pb, sem = allocator(nc, ctx)
        x_sb, ident, rows, lat = res["x"], res["ident"], res["rows_k"], res["lat"]
        Wq, Wkv, Wo = res["Wq"], res["Wkv"], res["Wo"]
        vec, qk_scale, bout = res["vec"], res["qk_scale"], res["bout"]
        stats, mv, rstd = sb("stats_e", [S, B, 6]), sb("mv_e", [S, B, 2]), sb("rstd_e", [S, B])
        st_g, st_l = sb("st_g", [P, D]), sb("st_l", [S, D])
        kb = [sb(f"kb{u}", [S, NK]) for u in range(2)]
        lnT = sb("lnT", [P, KD, NK])
        qkn = sb("qkn", [P, 3, D])
        NR = [S, S, P]
        sq = sb("sq", [P, D])
        ssq = sb("ssq", [P, 3, HEADS])
        half = sb("half", [P, HEADS])
        rn = sb("rn", [P, 3, HEADS])
        v = [sb(f"v{u}", [P, 2, D]) for u in range(2)]
        kT = [sb(f"kT{u}", [P, KD, NK]) for u in range(2)]
        qT = [sb(f"qT{u}", [P, KD, S]) for u in range(2)]
        sc = [sb(f"sc{i}", [S, NK]) for i in range(2)]
        pr = [sb(f"pr{i}", [S, NK]) for i in range(2)]
        prT = [sb(f"prT{i}", [P, 2, S]) for i in range(2)]
        least = [sb(f"least{u}", [S, HEADS]) for u in range(2)]
        total = [sb(f"total{u}", [S, HEADS]) for u in range(2)]
        rtot = sb("rtot", [S, HEADS])
        took = sem("took")
        o = sb("o", [S, D])
        oT = sb("oT", [P, KD, S])
        att = res["att"]
        bt = pb("bt", [P, D])
        bk = [pb(f"bk{i}", [P, D]) for i in range(2)]
        bs = [pb(f"bs{i}", [S, NK]) for i in range(2)]
        bp = [pb(f"bp{i}", [P, 2 * S]) for i in range(2)]
        bo = pb("bo", [S, D])
        w_in = res["attn_in"]
        var_ok, root_ok = sem("var_e"), sem("root_e")
        (staged, t_mm, t_free, k_mm, sq_ok, ss_ok, pow_ok, unit_ok, s_mm, least_ok, exp_ok, p_mm, pv_mm, o_ok, setup) = (
            sem(n) for n in ("staged", "t_mm", "t_free", "k_mm", "sq_ok", "ss_ok", "pow_ok", "unit_ok", "s_mm", "least_ok",
                             "exp_oke", "p_mm", "pv_mm", "o_ok", "setup"))
        k_free = [sem(f"k_free{i}") for i in range(2)]
        pt_ok = [sem("pt_oke0"), sem("pt_oke1")]
        ln_ok, sums, rt_ok = sem("ln_ok"), sem("sums"), sem("rt_ok")
        gammas = sb("gammas", [P, 2])
        block = ctx.enter_context(nc.Block())
        LAT = KC

        def rows_T(pe, n, idx):
            src, r = ((st_g, P), (st_l, S))[idx]
            pe.wait_ge(staged, n + 1)
            if not (isinstance(n, int) and n == 0 and idx == 0):
                pe.wait_ge(t_free, 6 * n + idx)
            for k in range(KD):
                ins = pe.transpose(bt[:, k * P:k * P + r], src[:, k * P:(k + 1) * P], ident[0:r, 0:r])
            ins.then_inc(t_mm, 1)

        def product(pe, n, idx):
            c0, c1 = (LAT, NK) if idx in (0, 1, 3) else (0, KC)
            w = Wq[:, :, :] if idx == 0 else Wkv[:, :, 0:D] if idx in (1, 2) else Wkv[:, :, D:2 * D]
            pe.wait_ge(t_free, 6 * n + 2)
            if not (isinstance(n, int) and n == 0 and idx < 2):
                pe.wait_ge(k_free[idx % 2], 3 * n + idx // 2)
            for k in range(KD):
                ins = pe.matmul(bk[idx % 2][0:c1 - c0, :], lnT[:, k, c0:c1], w[:, k, :], start=k == 0, stop=k == KD - 1)
            ins.then_inc(k_mm, 2 if isinstance(n, int) and n == 0 and idx == 4 else 1)

        def unit_T(pe, n, i):
            r = NR[i]
            pe.wait_ge(unit_ok, 3 * n + i + 1)
            pe.wait_ge(t_free, 6 * n + 2 + i)
            for k in range(KD):
                ins = pe.transpose(bt[:, k * P:k * P + r], qkn[0:r, i, k * P:(k + 1) * P], ident[0:r, 0:r])
            ins.then_inc(t_mm, 2 if isinstance(n, int) and n == 0 and i == 2 else 1)

        def scores(pe, b, u, h):
            pe.wait_ge(least_ok, 8 * b + h + 1)
            lo = DH * (h % 2)
            pe.matmul(bs[h % 2][:, :], qT[u][lo:lo + DH, h // 2, :], kT[u][lo:lo + DH, h // 2, :], start=True, stop=True).then_inc(s_mm, 1)

        def probs_T(pe, b, h):
            pe.wait_ge(exp_ok, 8 * b + h + 3)
            pe.wait_ge(pt_ok[h % 2], 4 * b + h // 2 + 1)
            pe.transpose(bp[h % 2][:, 0:S], pr[h % 2][:, 0:KC], ident[0:S, 0:S])
            pe.transpose(bp[h % 2][0:S, S:2 * S], pr[h % 2][:, KC:NK], ident[0:S, 0:S]).then_inc(p_mm, 1)

        def values(pe, b, u, h):
            pe.wait_ge(pt_ok[h % 2], 4 * b + h // 2 + 2)
            pe.matmul(bo[:, h * DH:(h + 1) * DH], prT[h % 2][:, 0, :], v[u][:, 0, h * DH:(h + 1) * DH], start=True, stop=False)
            pe.matmul(bo[:, h * DH:(h + 1) * DH], prT[h % 2][0:S, 1, :], v[u][0:S, 1, h * DH:(h + 1) * DH], start=False, stop=True).then_inc(pv_mm, 1)

        @block.tensor
        def _(pe):
            def prepare(n, i):
                if i < 2:
                    rows_T(pe, n, i)
                elif i in (5, 7, 9):
                    unit_T(pe, n, (i - 5) // 2)
                else:
                    product(pe, n, i - 2 if i < 5 else i // 2)

            def sums_T(b, last):
                pe.wait_ge(o_ok, b + 2)
                pe.wait_ge(t_free, 6 * b + (6 if last else 11))
                for k in range(KD):
                    ins = pe.transpose(bt[:, k * P:k * P + S], o[:, k * P:(k + 1) * P], ident[0:S, 0:S])
                ins.then_inc(t_mm, 1)

            def project(b, last):
                pe.wait_ge(t_free, 6 * b + (7 if last else 12))
                pe.wait_ge(k_free[1], 3 * b + (3 if last else 5))
                for k in range(KD):
                    ins = pe.matmul(bk[1][0:S, :], oT[:, k, :], Wo[:, k, :], start=k == 0, stop=k == KD - 1)
                ins.then_inc(k_mm, 1)

            def batch(b, u, first, last):
                pe.wait_ge(t_free, 6 * b + 5)
                scores(pe, b, u, 0)
                scores(pe, b, u, 1)
                if not first:
                    sums_T(b - 1, False)
                for h in range(HEADS):
                    if not last:
                        prepare(b + 1, h)
                    if h == 0 and not first:
                        project(b - 1, False)
                    probs_T(pe, b, h)
                    if h + 2 < HEADS:
                        scores(pe, b, u, h + 2)
                    if h == 0:
                        pe.wait_ge(k_free[1], 3 * b + 2)
                        pe.wait_ge(k_free[0], 3 * b + 3)
                        pe.wait_ge(o_ok, b + 1)
                    if h >= 1:
                        values(pe, b, u, h - 1)
                values(pe, b, u, HEADS - 1)
                if not last:
                    prepare(b + 1, 8)
                    prepare(b + 1, 9)

            pe.wait_ge(w_in, 48)
            pe.sem_inc(p_mm, 2)
            pe.sem_inc(pv_mm, 2)
            for i in range(10):
                prepare(0, i)
            batch(0, 0, True, False)
            with pe.Fori(1, B - 2, 2) as b:
                for u in range(2):
                    batch(b + u, 1 - u, False, False)
            batch(B - 1, 1, False, True)
            sums_T(B - 1, True)
            project(B - 1, True)

        @block.sync
        def _(sp):
            sp.dma_start(vec[:, :, :], io["vec"]).then_inc(res["vec_in"], 16)
            sp.dma_start(gammas[:, :], io["gammas"]).then_inc(res["vec_in"], 16)
            sp.dma_start(bout[:, :], io["bout"].rearrange("(o d) -> o d", o=1).broadcast_to([S, D])).then_inc(res["vec_in"], 16)
            sp.dma_start(Wq[:, :, :], io["Wq"].rearrange("(k p) n -> p k n", p=P)).then_inc(w_in, 16)
            sp.dma_start(Wkv[:, :, :], io["Wkv"].rearrange("(k p) n -> p k n", p=P)).then_inc(w_in, 16)
            sp.dma_start(Wo[:, :, :], io["Wout"].rearrange("(k p) n -> p k n", p=P)).then_inc(w_in, 16)

        @block.gpsimd
        def _(pool):
            def stage(n, u):
                if not (isinstance(n, int) and n == 0):
                    pool.wait_ge(t_mm, 6 * n - 4)
                    pool.wait_ge(least_ok, 8 * n - 6)
                pool.tensor_copy(st_g[:, :], rows[:, bass.ds(n, 1), :].rearrange("p o d -> p (o d)"))
                pool.tensor_copy(st_l[:, :], lat[:, bass.ds(n, 1), :].rearrange("p o d -> p (o d)"))
                pool.tensor_copy(kb[u][:, :], res["kbias"][:, bass.ds(n, 1), :].rearrange("p o d -> p (o d)")).then_inc(staged, 1)

            def norms(n):
                for i in range(3):
                    r = NR[i]
                    pool.wait_ge(k_free[i % 2], 3 * n + 1 + i // 2)
                    if not (isinstance(n, int) and n == 0 and i == 0):
                        pool.wait_ge(ss_ok, 3 * n + i)
                    pool.tensor_tensor(sq[0:r, :], qkn[0:r, i, :], qkn[0:r, i, :], ALU.mult).then_inc(sq_ok, 1)
                    pool.wait_ge(ss_ok, 3 * n + i + 1)
                    pool.tensor_tensor(rn[0:r, i, :], ssq[0:r, i, :], half[0:r, :], ALU.pow).then_inc(pow_ok, 1)

            pool.memset(half[:, :], -0.5).then_inc(setup, 1)
            pool.wait_ge(setup, 1)
            pool.wait_ge(ln_ok, 1)
            stage(0, 0)
            norms(0)
            with pool.Fori(1, B - 2, 2) as n:
                for u in range(2):
                    stage(n + u, 1 - u)
                    norms(n + u)
            stage(B - 1, 1)
            norms(B - 1)

        @block.scalar
        def _(act):
            def soft(b, u, h):
                act.wait_ge(least_ok, 8 * b + h + 3)
                act.wait_ge(p_mm, 8 * b + h + 1)
                act.activation(pr[h % 2][:, :], sc[h % 2][:, :], ACT.Exp, bias=least[u][:, h:h + 1], scale=-1.0,
                               accum_out=total[u][:, h:h + 1]).then_inc(exp_ok, 1)

            def keep_probs(b, h):
                act.wait_ge(p_mm, 8 * b + h + 3)
                act.wait_ge(pv_mm, 8 * b + h + 1)
                act.activation(prT[1][:, 0, :], bp[1][:, 0:S], ACT.Copy)
                act.activation(prT[1][0:S, 1, :], bp[1][0:S, S:2 * S], ACT.Copy).then_inc(pt_ok[1], 1)

            def prepare(n, u, i):
                first = isinstance(n, int) and n == 0
                if i == 1:
                    act.wait_ge(t_mm, 6 * n + 2)
                    for k in range(KD):
                        ins = act.activation(lnT[:, k, LAT:NK], bt[:, k * P:k * P + S], ACT.Identity,
                                             scale=vec[:, 2, k:k + 1], bias=vec[:, 3, k:k + 1])
                    ins.then_inc(t_free, 1)
                if i == 2:
                    act.wait_ge(k_mm, 6 * n + 1)
                    act.activation(qkn[0:S, 0, :], bk[0][0:S, :], ACT.Copy).then_inc(k_free[0], 1)
                if i == 4:
                    act.wait_ge(k_mm, 6 * n + 3)
                    act.activation(qkn[:, 2, :], bk[0][:, :], ACT.Copy).then_inc(k_free[0], 1)
                if i == 6:
                    act.wait_ge(k_mm, 6 * n + 4)
                    act.activation(v[u][0:S, 1, :], bk[1][0:S, :], ACT.Copy).then_inc(k_free[1], 2 if first else 1)
                if i == 8:
                    act.wait_ge(k_mm, 6 * n + 5)
                    act.activation(v[u][:, 0, :], bk[0][:, :], ACT.Copy).then_inc(k_free[0], 1)
                if i == 5:
                    act.wait_ge(t_mm, 6 * n + 3)
                    act.activation(qT[u][:, :, :], bt[:, :].rearrange("p (k s) -> p k s", k=KD)[:, :, 0:S], ACT.Copy,
                                   scale=qk_scale[:, 0:1]).then_inc(t_free, 1)
                if i == 9:
                    act.wait_ge(t_mm, 6 * n + 5)
                    act.activation(kT[u][:, :, 0:KC], bt[:, :].rearrange("p (k s) -> p k s", k=KD), ACT.Copy).then_inc(t_free, 2 if first else 1)

            def batch(b, u, first, last):
                soft(b, u, 0)
                for h in range(HEADS):
                    if h + 1 < HEADS:
                        soft(b, u, h + 1)
                    if not last:
                        prepare(b + 1, 1 - u, h)
                    if h % 2:
                        keep_probs(b, h)
                if not last:
                    prepare(b + 1, 1 - u, 8)
                    prepare(b + 1, 1 - u, 9)

            act.wait_ge(var_ok, 1)
            act.activation(rstd[:, :], rstd[:, :], ACT.Sqrt).then_inc(root_ok, 1)
            act.wait_ge(var_ok, 2)
            act.activation(rstd[:, :], rstd[:, :], ACT.Sqrt).then_inc(root_ok, 1)
            act.wait_ge(w_in, 48)
            act.wait_ge(res["vec_in"], 48)
            act.wait_ge(res["vec_ok"], 1)
            act.sem_inc(exp_ok, 2)
            act.sem_inc(pt_ok[1], 1)
            for i in range(10):
                prepare(0, 0, i)
            batch(0, 0, True, False)
            with act.Fori(1, B - 2, 2) as b:
                for u in range(2):
                    batch(b + u, 1 - u, False, False)
            batch(B - 1, 1, False, True)

        @block.vector
        def _(dve):
            link = make_linker(dve, res["dve_chain"])

            def reduce(n, i):
                r = NR[i]
                dve.wait_ge(sq_ok, 3 * n + i + 1)
                dve.tensor_reduce(ssq[0:r, i, :], sq[0:r, :].rearrange("p (h d) -> p h d", d=DH), AX, ALU.add).then_inc(sums, 1)
                dve.wait_ge(sums, 3 * n + i + 1)
                dve.tensor_scalar(ssq[0:r, i, :], ssq[0:r, i, :], 1.0 / DH, 1e-16, ALU.mult, ALU.max).then_inc(ss_ok, 1)

            def unit(n, i):
                r = NR[i]
                dve.wait_ge(pow_ok, 3 * n + i + 1)
                q = qkn[0:r, i, :].rearrange("p (h d) -> p h d", d=DH)
                dve.tensor_tensor(q, q, rn[0:r, i, :].unsqueeze(2).broadcast_to([r, HEADS, DH]), ALU.mult).then_inc(unit_ok, 1)

            def prepare(n, u, i):
                if i == 0:
                    dve.wait_ge(t_mm, 6 * n + 1)
                    for k in range(KD):
                        ins = dve.tensor_scalar(lnT[:, k, 0:KC], bt[:, k * P:(k + 1) * P], vec[:, 0, k:k + 1], vec[:, 1, k:k + 1],
                                                ALU.mult, ALU.add)
                    ins.then_inc(t_free, 1)
                if i == 3:
                    dve.wait_ge(k_mm, 6 * n + 2)
                    dve.tensor_copy(qkn[0:S, 1, :], bk[1][0:S, :]).then_inc(k_free[1], 1)
                    reduce(n, 0)
                if i == 4:
                    unit(n, 0)
                    reduce(n, 1)
                if i == 5:
                    unit(n, 1)
                    reduce(n, 2)
                if i == 6:
                    unit(n, 2)
                if i == 7:
                    dve.wait_ge(t_mm, 6 * n + 4)
                    dve.tensor_copy(kT[u][:, :, LAT:NK], bt[:, :].rearrange("p (k s) -> p k s", k=KD)[:, :, 0:S]).then_inc(t_free, 1)

            def lowest(b, u, h):
                dve.wait_ge(s_mm, 8 * b + h + 1)
                dve.wait_ge(exp_ok, 8 * b + h + 1)
                dve.sem_inc(took, 1)
                dve.tensor_tensor_reduce(out=sc[h % 2][:, :], in0=bs[h % 2][:, :], in1=kb[u][:, :], scale=1.0, scalar=3e38,
                                         op0=ALU.add, op1=ALU.min, accum_out=least[u][:, h:h + 1]).then_inc(least_ok, 1)

            def keep_probs(b, h):
                dve.wait_ge(p_mm, 8 * b + h + 3)
                dve.wait_ge(pv_mm, 8 * b + h + 1)
                dve.tensor_copy(prT[0][:, 0, :], bp[0][:, 0:S])
                dve.tensor_copy(prT[0][0:S, 1, :], bp[0][0:S, S:2 * S]).then_inc(pt_ok[0], 1)

            def sums_over(b, u):
                dve.wait_ge(exp_ok, 8 * b + 10)
                dve.reciprocal(rtot[:, :], total[u][:, :]).then_inc(rt_ok, 1)
                dve.wait_ge(rt_ok, b + 1)
                dve.wait_ge(pv_mm, 8 * b + 10)
                dve.wait_ge(t_mm, 6 * b + 6)
                dve.tensor_tensor(o[:, :].rearrange("p (h d) -> p h d", d=DH), bo[:, :].rearrange("p (h d) -> p h d", d=DH),
                                  rtot[:, :].unsqueeze(2).broadcast_to([S, HEADS, DH]), ALU.mult).then_inc(o_ok, 1)

            def sums_kept(b, last):
                dve.wait_ge(t_mm, 6 * b + (7 if last else 12))
                dve.tensor_copy(oT[:, :, :], bt[:, :].rearrange("p (k s) -> p k s", k=KD)[:, :, 0:S]).then_inc(t_free, 1)

            def add_bias(b, last):
                dve.wait_ge(k_mm, 6 * b + (7 if last else 12))
                dve.tensor_tensor(att[:, bass.ds(b, 1), :].rearrange("p o d -> p (o d)"), bk[1][0:S, :], bout[:, :], ALU.add).then_inc(k_free[1], 1)

            def batch(b, u, first, last):
                lowest(b, u, 0)
                if not first:
                    sums_over(b - 1, 1 - u)
                for h in range(HEADS):
                    if h + 1 < HEADS:
                        lowest(b, u, h + 1)
                    if h == 0 and not first:
                        sums_kept(b - 1, False)
                    if not last:
                        prepare(b + 1, 1 - u, h)
                    if h == 0 and not first:
                        add_bias(b - 1, False)
                    if h % 2 == 0:
                        keep_probs(b, h)

            for i in range(2):
                src = x_sb if i == 0 else lat
                layernorm_stats(link, dve, src, stats, mv, B)
                dve.tensor_scalar(rstd[:, :], mv[:, :, 1], EPS, None, ALU.add).then_inc(var_ok, 1)
                dve.wait_ge(root_ok, i + 1)
                link(dve.reciprocal(rstd[:, :], rstd[:, :]))
                for b in range(B):
                    ins = dve.tensor_scalar(lat[:, b, :], src[:, b, :], mv[:, b, 0:1], rstd[:, b:b + 1], ALU.subtract, ALU.mult)
                link(ins)
            dve.sem_inc(ln_ok, 1)
            dve.wait_ge(res["vec_in"], 48)
            dve.scalar_tensor_tensor(qk_scale[:, :], gammas[:, 0:1], -DH ** -0.5, gammas[:, 1:2], ALU.mult, ALU.mult).then_inc(res["vec_ok"], 1)
            dve.sem_inc(least_ok, 2)
            dve.sem_inc(pt_ok[0], 1)
            dve.sem_inc(o_ok, 1)
            for i in range(10):
                prepare(0, 0, i)
            batch(0, 0, True, False)
            with dve.Fori(1, B - 2, 2) as b:
                for u in range(2):
                    batch(b + u, 1 - u, False, False)
            batch(B - 1, 1, False, True)
            sums_over(B - 1, 1)
            sums_kept(B - 1, True)
            add_bias(B - 1, True)


def attend_full(nc, io, res):
    NT = CT + 1
    KR = CR + [S]
    STEPS = NT + 2 * NT + 1 + NT + 1 + 3 * HEADS + 2
    HALF = NKD // 2
    FIRST_T = 512 // S
    ctx = ExitStack()
    with ctx:
        sb, pb, sem = allocator(nc, ctx)
        ident, lat = res["ident"], res["lat"]
        Wq, Wkv, Wo = res["Wq"], res["Wkv"], res["Wo"]
        vec, qk_scale, bout, att = res["vec"], res["qk_scale"], res["bout"], res["att"]
        stats, mv, rstd = sb("stats_d", [P, CT, 6]), sb("mv_d", [P, CT, 2]), sb("rstd_d", [P, CT])
        rows = sb("rows_d", [P, NT, D])
        vals = sb("vals_d", [P, NT, D])
        q = sb("q_d", [S, D])
        lnT = sb("lnT_d", [P, KD, NKD])
        qT = sb("qT_d", [P, KD, S])
        mask8 = sb("mask8_d", [S, C], mybir.dt.uint8)
        bias = sb("bias_d", [S, NKD])
        ssq, rn, half = sb("ssq_d", [P, HEADS]), sb("rn_d", [P, HEADS]), sb("half_d", [P, HEADS])
        sc, pr = sb("sc_d", [S, NKD]), sb("pr_d", [S, NKD])
        prT = sb("prT_d", [P, NT, S])
        low, least, total, rtot = sb("low_d", [S, 2]), sb("least_d", [S, 1]), sb("total_d", [S, HEADS]), sb("rtot_d", [S, HEADS])
        took = sem("took_d")
        o, oT = sb("o_d", [S, D]), sb("oT_d", [P, KD, S])
        bt, b0, b1, p0, p1, bo = (pb(n, [P, 512]) for n in ("bt_d", "b0_d", "b1_d", "p0_d", "p1_d", "bo_d"))
        d_in, batch_done, pe_turn, dve_turn, ask_act, act_did, ask_pool, pool_did, hset = (sem(n) for n in (
            "d_in", "batch_done", "pe_turn", "dve_turn", "ask_act", "act_did", "ask_pool", "pool_did", "hset"))
        block = ctx.enter_context(nc.Block())
        cols = [P * t for t in range(CT)] + [C]

        def each_full(eng, body):
            with eng.Fori(0, B) as b:
                f = eng.value_load(res["flag"][0:1, bass.ds(b, 1)], min_val=0, max_val=1)
                r = eng.value_load(res["runs"][0:1, bass.ds(b, 1)], min_val=0, max_val=B - 1)
                with eng.If(f == 1):
                    body(b, r)

        @block.sync
        def _(sp):
            def body(b, r):
                sp.wait_ge(batch_done, r + 1)
                sp.dma_start(rows[:, 0:CT - 1, :], io["ctx"][bass.ds(b, 1), 0:P * (CT - 1), :].rearrange("o (t p) d -> p (o t) d", p=P)).then_inc(d_in, 16)
                sp.dma_start(rows[0:CR[-1], CT - 1, :], io["ctx"][bass.ds(b, 1), P * (CT - 1):C, :].rearrange("o p d -> (o p) d")).then_inc(d_in, 16)
                sp.dma_start(mask8[:, :], io["mask"][bass.ds(b, 1), :].broadcast_to([S, C])).then_inc(d_in, 16)
            each_full(sp, body)

        @block.tensor
        def _(pe):
            def body(b, r):
                n = [0]

                def turn(work):
                    n[0] += 1
                    pe.wait_ge(dve_turn, STEPS * r + n[0])
                    work().then_inc(pe_turn, 1)

                def turned(dst, src, rr):
                    def work():
                        for k in range(KD):
                            ins = pe.transpose(dst[:, k * P:k * P + rr], src[:, k * P:(k + 1) * P], ident[0:rr, 0:rr])
                        return ins
                    return work

                def times(dst, lhs, w):
                    def work():
                        for k in range(KD):
                            ins = pe.matmul(dst, lhs(k), w[:, k, :], start=k == 0, stop=k == KD - 1)
                        return ins
                    return work

                for t in range(NT):
                    turn(turned(bt, rows[0:KR[t], t, :], KR[t]))
                for t in range(NT):
                    for w in (Wkv[:, :, 0:D], Wkv[:, :, D:2 * D]):
                        turn(times(b0[0:KR[t], :], lambda k: lnT[:, k, cols[t]:cols[t] + KR[t]], w))
                turn(times(b0[0:S, :], lambda k: lnT[:, k, C:NKD], Wq))
                for t in range(NT):
                    turn(turned(bt, rows[0:KR[t], t, :], KR[t]))
                turn(turned(bt, q[:, :], S))
                for h in range(HEADS):
                    lo, c, hd = DH * (h % 2), h // 2, slice(h * DH, (h + 1) * DH)

                    def scores():
                        pe.matmul(b0[0:S, 0:HALF], qT[lo:lo + DH, c, :], lnT[lo:lo + DH, c, 0:HALF], start=True, stop=True)
                        return pe.matmul(b1[0:S, 0:HALF], qT[lo:lo + DH, c, :], lnT[lo:lo + DH, c, HALF:NKD], start=True, stop=True)

                    def probs():
                        for t in range(NT):
                            dst, k = (p0, t) if t < FIRST_T else (p1, t - FIRST_T)
                            ins = pe.transpose(dst[0:KR[t], k * S:(k + 1) * S], pr[:, cols[t]:cols[t] + KR[t]], ident[0:S, 0:S])
                        return ins

                    def sums():
                        for t in range(NT):
                            ins = pe.matmul(bo[0:S, hd], prT[0:KR[t], t, :], vals[0:KR[t], t, hd], start=t == 0, stop=t == NT - 1)
                        return ins
                    turn(scores)
                    turn(probs)
                    turn(sums)
                turn(turned(bt, o[:, :], S))
                turn(times(b0[0:S, :], lambda k: oT[:, k, :], Wo))
                assert n[0] == STEPS
            each_full(pe, body)

        @block.scalar
        def _(act):
            def body(b, r):
                act.wait_ge(ask_act, (HEADS + 1) * r + 1)
                act.activation(rstd[:, :], rstd[:, :], ACT.Sqrt).then_inc(act_did, 1)
                for h in range(HEADS):
                    act.wait_ge(ask_act, (HEADS + 1) * r + h + 2)
                    act.activation(pr[:, :], sc[:, :], ACT.Exp, bias=least[:, 0:1], scale=-1.0, accum_out=total[:, h:h + 1]).then_inc(act_did, 1)
            each_full(act, body)

        @block.gpsimd
        def _(pool):
            pool.memset(half[:, :], -0.5).then_inc(hset, 1)
            pool.wait_ge(hset, 1)

            def body(b, r):
                for t in range(NT + 1):
                    n = KR[t] if t < NT else S
                    pool.wait_ge(ask_pool, (NT + 1) * r + t + 1)
                    pool.tensor_tensor(rn[0:n, :], ssq[0:n, :], half[0:n, :], ALU.pow).then_inc(pool_did, 1)
            each_full(pool, body)

        @block.vector
        def _(dve):
            dve.memset(rows[:, CT - 1, :], 0.0)
            dve.memset(rstd[:, :], 1.0)
            dve.drain()
            dve.sem_inc(batch_done, 1)

            def body(b, r):
                n, a, g = [0], [0], [0]

                def give():
                    dve.drain().then_inc(dve_turn, 1)

                def take():
                    n[0] += 1
                    dve.wait_ge(pe_turn, STEPS * r + n[0])
                    dve.sem_inc(took, 1)

                def ask(who, s_ask, s_did, per, count):
                    dve.drain().then_inc(s_ask, 1)
                    count[0] += 1
                    dve.wait_ge(s_did, per * r + count[0])
                    dve.sem_inc(took, 1)

                dve.wait_ge(d_in, 48 * r + 48)
                for t in range(CT):
                    dve.bn_stats(stats[0:CR[t], t, :], rows[0:CR[t], t, :])
                dve.drain()
                for t in range(CT):
                    dve.bn_aggr(mv[0:CR[t], t, :], stats[0:CR[t], t, :])
                dve.drain()
                for t in range(CT):
                    dve.tensor_scalar(rstd[0:CR[t], t:t + 1], mv[0:CR[t], t, 1:2], EPS, None, ALU.add)
                ask(None, ask_act, act_did, HEADS + 1, a)
                dve.reciprocal(rstd[:, :], rstd[:, :])
                dve.drain()
                for t in range(CT):
                    dve.tensor_scalar(rows[0:CR[t], t, :], rows[0:CR[t], t, :], mv[0:CR[t], t, 0:1], rstd[0:CR[t], t:t + 1], ALU.subtract, ALU.mult)
                dve.tensor_copy(rows[0:S, CT, :], lat[:, bass.ds(b, 1), :].rearrange("p o d -> p (o d)"))
                dve.tensor_copy(bias[:, 0:C], mask8[:, :])
                dve.drain()
                dve.tensor_scalar(bias[:, 0:C], bias[:, 0:C], -BIG, BIG, ALU.mult, ALU.add)
                dve.memset(bias[:, C:NKD], 0.0)
                give()
                for t in range(NT):
                    take()
                    i = 0 if t < CT else 2
                    for k in range(KD):
                        dve.tensor_scalar(lnT[:, k, cols[t]:cols[t] + KR[t]], bt[:, k * P:k * P + KR[t]], vec[:, i, k:k + 1],
                                          vec[:, i + 1, k:k + 1], ALU.mult, ALU.add)
                    give()

                def unit(x, rr):
                    xh = x.rearrange("p (h d) -> p h d", d=DH)
                    dve.tensor_tensor(sc[0:S, 0:D] if rr == S else prT[0:rr, 0:6, :].rearrange("p t s -> p (t s)")[:, 0:D], x, x, ALU.mult)
                    sq = (sc[0:S, 0:D] if rr == S else prT[0:rr, 0:6, :].rearrange("p t s -> p (t s)")[:, 0:D]).rearrange("p (h d) -> p h d", d=DH)
                    dve.drain()
                    dve.tensor_reduce(ssq[0:rr, :], sq, AX, ALU.add)
                    dve.drain()
                    dve.tensor_scalar(ssq[0:rr, :], ssq[0:rr, :], 1.0 / DH, 1e-16, ALU.mult, ALU.max)
                    ask(None, ask_pool, pool_did, NT + 1, g)
                    dve.tensor_tensor(xh, xh, rn[0:rr, :].unsqueeze(2).broadcast_to([rr, HEADS, DH]), ALU.mult)

                for t in range(NT):
                    take()
                    dve.tensor_copy(rows[0:KR[t], t, :], b0[0:KR[t], :])
                    dve.drain()
                    unit(rows[0:KR[t], t, :], KR[t])
                    give()
                    take()
                    dve.tensor_copy(vals[0:KR[t], t, :], b0[0:KR[t], :])
                    give()
                take()
                dve.tensor_copy(q[:, :], b0[0:S, :])
                dve.drain()
                unit(q[:, :], S)
                give()
                for t in range(NT):
                    take()
                    dve.tensor_copy(lnT[:, :, cols[t]:cols[t] + KR[t]], bt[:, :].rearrange("p (k s) -> p k s", k=KD)[:, :, 0:KR[t]])
                    give()
                take()
                dve.tensor_scalar(qT[:, :, :], bt[:, :].rearrange("p (k s) -> p k s", k=KD)[:, :, 0:S], qk_scale[:, 0:1], None, ALU.mult)
                give()
                for h in range(HEADS):
                    take()
                    for i, bank in enumerate((b0, b1)):
                        dve.tensor_tensor_reduce(out=sc[:, i * HALF:(i + 1) * HALF], in0=bank[0:S, 0:HALF], in1=bias[:, i * HALF:(i + 1) * HALF],
                                                 scale=1.0, scalar=3e38, op0=ALU.add, op1=ALU.min, accum_out=low[:, i:i + 1])
                    dve.drain()
                    dve.tensor_tensor(least[:, :], low[:, 0:1], low[:, 1:2], ALU.min)
                    ask(None, ask_act, act_did, HEADS + 1, a)
                    give()
                    take()
                    for t in range(NT):
                        src, k = (p0, t) if t < FIRST_T else (p1, t - FIRST_T)
                        dve.tensor_copy(prT[0:KR[t], t, :], src[0:KR[t], k * S:(k + 1) * S])
                    give()
                    take()
                    if h < HEADS - 1:
                        give()
                dve.reciprocal(rtot[:, :], total[:, :])
                dve.drain()
                dve.tensor_tensor(o[:, :].rearrange("p (h d) -> p h d", d=DH), bo[0:S, :].rearrange("p (h d) -> p h d", d=DH),
                                  rtot[:, :].unsqueeze(2).broadcast_to([S, HEADS, DH]), ALU.mult)
                give()
                take()
                dve.tensor_copy(oT[:, :, :], bt[:, :].rearrange("p (k s) -> p k s", k=KD)[:, :, 0:S])
                give()
                take()
                dve.tensor_tensor(att[:, bass.ds(b, 1), :].rearrange("p o d -> p (o d)"), b0[0:S, :], bout[:, :], ALU.add)
                dve.drain().then_inc(batch_done, 1)
                assert n[0] == STEPS
            each_full(dve, body)
            for b in range(B):
                dve.tensor_tensor(res["x"][:, b, :], res["x"][:, b, :], att[:, b, :], ALU.add)


F, E_L, R_L = 2048, 4, 4
FJ = F // P
ER = E_L * R_L


def feed_forward(nc, io, res):
    ctx = ExitStack()
    with ctx:
        sb, pb, sem = allocator(nc, ctx)
        x_sb, ident, ones = res["x"], res["ident"], res["ones"]
        Wi, WoT = sb("Wi", [P, KD, F]), sb("WoT", [P, FJ, D])
        Bt = sb("Bt", [2 * 32, F])
        WgA = sb("WgA", [P, KD, E_L + ER])
        bg = sb("bg", [S, E_L])
        stats, mv, rstd = sb("stats_f", [S, B, 6]), sb("mv_f", [S, B, 2]), sb("rstd_f", [S, B])
        xn = sb("xn_f", [S, B, D])
        xT = sb("xT_f", [P, KD, XT])
        lga = sb("lga", [S, B, E_L + ER])
        score = sb("score", [S, B, 8])
        lmax, lsum = sb("lmax_f", [S, B]), sb("lsum_f", [S, B])
        top, topi, topf = sb("top_f", [S, B, 8]), sb("topi_f", [S, B, 8], U32), sb("topf_f", [S, B, 8])
        iota_e = sb("iota_f", [S, E_L])
        hot = [sb(f"hot_f{k}", [S, B, E_L]) for k in range(2)]
        low = sb("low_f", [S, B, 64])
        lowT = sb("lowT", [64, XT])
        wrep = [sb(f"wrep{i}", [S, P]) for i in range(2)]
        wb = [sb(f"wb{k}", [P, XT]) for k in range(2)]
        NT4 = XT // 2
        h1 = [sb(f"h1_{i}", [P, NT4]) for i in range(2)]
        h2 = [sb(f"h2_{i}", [P, NT4]) for i in range(2)]
        hs = [sb(f"hs{i}", [P, NT4]) for i in range(3)]
        NBK = 3
        bank = [pb(f"bf{i}", [P, 512]) for i in range(NBK)]
        acc = [pb(f"acc{i}", [P, 512]) for i in range(4)]
        bx = pb("bx", [P, 512])
        w_in, wi_in, wo_in = sem("wf_in"), sem("wi_in"), sem("wo_in")
        (x_ok, var_ok, root_ok, xn_ok, t_mm, t_ok, l_mm, l_ok, sub_ok, exp_ok, low_ok, lt_mm, lt_ok, rep_ok, wb_mm, wb_ok, cs,
         base_mm, read1, d_mm, read2, hs_ok, acc_mm, acc_rd, out_s) = (sem("f_" + n) for n in (
             "x_ok", "var_ok", "root_ok", "xn_ok", "t_mm", "t_ok", "l_mm", "l_ok", "sub_ok", "exp_ok", "low_ok", "lt_mm", "lt_ok",
             "rep_ok", "wb_mm", "wb_ok", "cs", "base_mm", "read1", "d_mm", "read2", "hs_ok", "acc_mm", "acc_rd", "out_s"))
        block = ctx.enter_context(nc.Block())

        @block.sync
        def _(sp):
            sp.dma_start(WgA[:, :, :], io["WgA"].rearrange("(k p) e -> p k e", p=P)).then_inc(w_in, 16)
            sp.dma_start(bg[:, :], io["bg"].rearrange("(o e) -> o e", o=1).broadcast_to([S, E_L])).then_inc(w_in, 16)
            for i in range(2):
                sp.dma_start(Bt[32 * i:32 * i + ER, :], io["Bt"]).then_inc(w_in, 16)
            sp.dma_start(Wi[:, :, :], io["WiT"].rearrange("(k p) f -> p k f", p=P)).then_inc(wi_in, 16)
            sp.dma_start(WoT[:, :, :], io["WoT"].rearrange("(j p) d -> p j d", p=P)).then_inc(wo_in, 16)
            for b in range(B):
                sp.wait_ge(acc_rd, b + 1)
                sp.dma_start(io["out"][b], x_sb[:, b, :]).then_inc(out_s, 16)
            sp.wait_ge(out_s, 16 * B)

        @block.gpsimd
        def _(pool):
            pool.iota(iota_e[:, :], pattern=[[1, E_L]], base=0, channel_multiplier=0,
                      allow_small_or_imprecise_dtypes=True).then_inc(cs, 1)
            pool.memset(low[:, :, :], 0.0).then_inc(cs, 1)
            pool.memset(score[:, :, :], -1.0).then_inc(cs, 1)
            for i in range(2 * FJ):
                pool.wait_ge(read2, i + 1)
                if i >= 3:
                    pool.wait_ge(acc_mm, i - 2)
                pool.tensor_tensor(hs[i % 3][:, :], h1[i % 2][:, :], h2[i % 2][:, :], ALU.add).then_inc(hs_ok, 1)

        @block.scalar
        def _(act):
            act.wait_ge(var_ok, 1)
            act.activation(rstd[:, :], rstd[:, :], ACT.Sqrt).then_inc(root_ok, 1)
            act.wait_ge(sub_ok, 1)
            act.activation(score[:, :, 0:E_L], score[:, :, 0:E_L], ACT.Exp).then_inc(exp_ok, 1)

        @block.tensor
        def _(pe):
            for b in range(B):
                pe.wait_ge(xn_ok, b + 1)
                if b >= 2:
                    pe.wait_ge(t_ok, b - 1)
                for k in range(KD):
                    ins = pe.transpose(bank[b % 2][:, k * P:k * P + S], xn[:, b, k * P:(k + 1) * P], ident[0:S, 0:S])
                ins.then_inc(t_mm, 1)
            pe.wait_ge(w_in, 64)
            pe.wait_ge(t_ok, B)
            for b in range(B):
                for k in range(KD):
                    ins = pe.matmul(bx[0:S, b * 32:b * 32 + E_L + ER], xT[:, k, b * S:(b + 1) * S], WgA[:, k, :], start=k == 0, stop=k == KD - 1)
            ins.then_inc(l_mm, 1)
            pe.wait_ge(low_ok, 1)
            for b in range(B):
                ins = pe.transpose(bank[b // 4][0:64, (b % 4) * S:(b % 4 + 1) * S], low[:, b, :], ident[0:S, 0:S])
                if b % 4 == 3:
                    ins.then_inc(lt_mm, 1)
            for i in range(2 * B):
                k, b = i // B, i % B
                pe.wait_ge(rep_ok, i + 1)
                if i == 0:
                    pe.wait_ge(lt_ok, 2)
                ins = pe.matmul(acc[i // 4][:, (b % 4) * S:(b % 4 + 1) * S], wrep[i % 2][:, :], ident[0:S, 0:S], start=True, stop=True)
                ins.then_inc(wb_mm, 1)
            pe.wait_ge(wb_ok, 4)
            pe.wait_ge(wi_in, 16)

            def base(i):
                g, f = i // FJ, i % FJ
                if i >= NBK:
                    pe.wait_ge(read2, i - NBK + 1)
                for k in range(KD):
                    pe.matmul(bank[i % NBK][:, 0:NT4], Wi[:, k, f * P:(f + 1) * P], xT[:, k, g * NT4:(g + 1) * NT4], start=k == 0, stop=False)
                pe.matmul(bank[i % NBK][:, 0:NT4], Bt[0:ER, f * P:(f + 1) * P], lowT[0:ER, g * NT4:(g + 1) * NT4], start=False, stop=True).then_inc(base_mm, 1)

            def second(i):
                g, f = i // FJ, i % FJ
                pe.wait_ge(read1, i + 1)
                pe.matmul(bank[i % NBK][:, 0:NT4], Bt[32:32 + ER, f * P:(f + 1) * P], lowT[32:32 + ER, g * NT4:(g + 1) * NT4],
                          start=False, stop=True, skip_group_check=True).then_inc(d_mm, 1)

            def down(i):
                g, f = i // FJ, i % FJ
                pe.wait_ge(hs_ok, i + 1)
                if g and f == 0:
                    pe.wait_ge(acc_rd, 4)
                for j in range(4):
                    ins = pe.matmul(acc[j][0:S, :], hs[i % 3][:, j * S:(j + 1) * S], WoT[:, f, :], start=f == 0, stop=f == FJ - 1)
                ins.then_inc(acc_mm, 1)

            n = 2 * FJ
            for i in range(n + 2):
                if i < n:
                    base(i)
                if 1 <= i <= n:
                    second(i - 1)
                if i == 2:
                    pe.wait_ge(wo_in, 16)
                if i >= 2:
                    down(i - 2)

        @block.vector
        def _(dve):
            link = make_linker(dve, res["dve_chain"])
            layernorm_stats(link, dve, x_sb, stats, mv, B)
            dve.tensor_scalar(rstd[:, :], mv[:, :, 1], EPS, None, ALU.add).then_inc(var_ok, 1)
            dve.wait_ge(root_ok, 1)
            link(dve.reciprocal(rstd[:, :], rstd[:, :]))
            for b in range(B):
                dve.tensor_scalar(xn[:, b, :], x_sb[:, b, :], mv[:, b, 0:1], rstd[:, b:b + 1], ALU.subtract, ALU.mult).then_inc(xn_ok, 1)
            for b in range(B):
                dve.wait_ge(t_mm, b + 1)
                dve.tensor_copy(xT[:, :, b * S:(b + 1) * S], bank[b % 2][:, :].rearrange("p (k s) -> p k s", k=KD)[:, :, 0:S]).then_inc(t_ok, 1)
            dve.wait_ge(l_mm, 1)
            dve.wait_ge(w_in, 64)
            dve.wait_ge(cs, 3)
            link(dve.tensor_copy(lga[:, :, :], bx[0:S, 0:B * 32].rearrange("p (b c) -> p b c", c=32)[:, :, 0:E_L + ER]))
            sc4 = score[:, :, 0:E_L]
            link(dve.tensor_tensor(sc4, lga[:, :, 0:E_L], bg[:, :].unsqueeze(1).broadcast_to([S, B, E_L]), ALU.add))
            link(dve.tensor_reduce(lmax[:, :], sc4, AX, ALU.max))
            dve.tensor_tensor(sc4, sc4, lmax[:, :].unsqueeze(2).broadcast_to([S, B, E_L]), ALU.subtract).then_inc(sub_ok, 1)
            dve.wait_ge(exp_ok, 1)
            link(dve.tensor_reduce(lsum[:, :], sc4, AX, ALU.add))
            link(dve.reciprocal(lsum[:, :], lsum[:, :]))
            link(dve.tensor_tensor(sc4, sc4, lsum[:, :].unsqueeze(2).broadcast_to([S, B, E_L]), ALU.mult))
            for b in range(B):
                ins = dve.max(top[:, b, :], score[:, b, :])
            link(ins)
            for b in range(B):
                ins = dve.max_index(topi[:, b, :], top[:, b, :], score[:, b, :])
            link(ins)
            link(dve.tensor_copy(topf[:, :, :], topi[:, :, :]))
            for k in range(2):
                ins = dve.tensor_tensor(hot[k][:, :, :], iota_e[:, :].unsqueeze(1).broadcast_to([S, B, E_L]),
                                        topf[:, :, k:k + 1].broadcast_to([S, B, E_L]), ALU.is_equal)
            link(ins)
            link(dve.tensor_tensor(hot[1][:, :, :], hot[1][:, :, :], hot[0][:, :, :], ALU.subtract))
            for b in range(B):
                for k in range(2):
                    ins = dve.tensor_tensor(low[:, b, 32 * k:32 * k + ER].rearrange("p (e r) -> p e r", r=R_L),
                                            lga[:, b, E_L:E_L + ER].rearrange("p (e r) -> p e r", r=R_L),
                                            hot[k][:, b, :].unsqueeze(2).broadcast_to([S, E_L, R_L]), ALU.mult)
            ins.then_inc(low_ok, 1)
            for g in range(2):
                dve.wait_ge(lt_mm, g + 1)
                dve.tensor_copy(lowT[:, g * NT4:(g + 1) * NT4], bank[g][0:64, 0:NT4]).then_inc(lt_ok, 1)
            for i in range(2 * B):
                k, b = i // B, i % B
                if i >= 2:
                    dve.wait_ge(wb_mm, i - 1)
                dve.tensor_scalar(wrep[i % 2][:, :], ones[0:S, :], top[:, b, k:k + 1], None, ALU.mult).then_inc(rep_ok, 1)
            dve.wait_ge(wb_mm, 2 * B)
            for q in range(4):
                k, g = q // 2, q % 2
                dve.tensor_copy(wb[k][:, g * NT4:(g + 1) * NT4], acc[q][:, 0:NT4]).then_inc(wb_ok, 1)
            dve.wait_ge(wb_ok, 4)

            def weigh(i, k):
                g = i // FJ
                dve.wait_ge((base_mm, d_mm)[k], i + 1)
                if i >= 2:
                    dve.wait_ge(hs_ok, i - 1)
                dve.scalar_tensor_tensor((h1, h2)[k][i % 2][:, :], bank[i % NBK][:, 0:NT4], 0.0, wb[k][:, g * NT4:(g + 1) * NT4],
                                         ALU.max, ALU.mult).then_inc((read1, read2)[k], 1)

            def finish(g):
                dve.wait_ge(acc_mm, FJ * (g + 1))
                for j in range(4):
                    dve.tensor_tensor(x_sb[:, 4 * g + j, :], x_sb[:, 4 * g + j, :], acc[j][0:S, :], ALU.add).then_inc(acc_rd, 1)

            n = 2 * FJ
            for i in range(n):
                weigh(i, 0)
                if i:
                    weigh(i - 1, 1)
                if i == FJ + 2:
                    finish(0)
            weigh(n - 1, 1)
            finish(1)

def build(nc, io, scratch):
    ctx = ExitStack()
    with ctx:
        sb, pb, sem = allocator(nc, ctx)
        res = dict(scratch)
        res["x"] = sb("x_res", [S, B, D])
        res["ident"] = sb("ident", [P, P])
        res["ones"] = sb("ones", [P, P])
        res["gates"] = sb("gates", [S, TOPK, B])
        res["slots"] = sb("slots", [S, TOPK * B], I32)
        res["table"] = sb("table", [S, E_N + 2], I32)
        res["flag"], res["runs"] = sb("flags", [P, B], I32), sb("runs_n", [P, B + 1], I32)
        res["attn_in"], res["vec_in"], res["vec_ok"] = sem("attn_in"), sem("vec_in"), sem("vec_ok")
        res["dve_chain"] = [sem("dve_chain"), 0]
        res["z0"] = sem("z0")
        with ExitStack() as rows:
            res["ctx_rows"] = rows.enter_context(nc.sbuf_tensor("ctx_rows", [P, B * CT, D], FP32))
            distances(nc, io, res)
            warp(nc, io, res)
            route(nc, io, res)
        res["rows_k"] = sb("rows_k", [P, B, D])
        res["kbias"] = sb("kbias", [S, B, NK])
        experts(nc, io, res)
        with ExitStack() as attn:
            def at(name, shape):
                return attn.enter_context(nc.sbuf_tensor(name, shape, FP32))
            res["lat"], res["att"] = at("lat", [S, B, D]), at("att", [S, B, D])
            res["Wq"], res["Wkv"], res["Wo"] = at("Wq", [P, KD, INNER]), at("Wkv", [P, KD, 2 * INNER]), at("Wo", [P, INNER // P, D])
            res["vec"], res["qk_scale"], res["bout"] = at("vec", [P, 4, KD]), at("qk_scale", [P, 1]), at("bout", [S, D])
            attend(nc, io, res)
            attend_full(nc, io, res)
        feed_forward(nc, io, res)


def kernel(**inputs):
    import numpy as _np
    import concourse.bacc as _bacc
    from concourse import mybir as _mybir
    from concourse.bass_utils import run_bass_kernel_spmd as _run

    nc = _bacc.Bacc("TRN2", target_bir_lowering=False, num_devices=1)
    ctx_rows = _np.ascontiguousarray(inputs["ctx_1024"])
    arrays = {"x": _np.ascontiguousarray(inputs["x"]), "ctx": ctx_rows,
              "gate": _np.ascontiguousarray(inputs["L0_ffn_gate"]),
              "W1": _np.ascontiguousarray(inputs["L0_ffn_W1"]), "W2": _np.ascontiguousarray(inputs["L0_ffn_W2"]),
              "b2": _np.ascontiguousarray(inputs["L0_ffn_b2"]),
              "b1T": _np.ascontiguousarray(inputs["L0_ffn_b1"].reshape(16, 8, 128).transpose(2, 0, 1)).reshape(128, 128),
              "maskT": _np.ascontiguousarray(inputs["mask_BxS2_bk0"].T),
              "mask": _np.ascontiguousarray(inputs["mask_BxS2_bk0"]),
              "vec": _np.ascontiguousarray(_np.stack([inputs["L1_xattn_ln_" + n] for n in ("x_g", "x_b", "l_g", "l_b")])
                                           .reshape(4, 4, 128).transpose(2, 0, 1)),
              "gammas": _np.ascontiguousarray(_np.stack([_np.concatenate([inputs["L1_xattn_" + n]] * 2) for n in ("q_gamma", "k_gamma")], 1)),
              "Wq": _np.ascontiguousarray(inputs["L1_xattn_W_q"]), "Wkv": _np.ascontiguousarray(inputs["L1_xattn_W_kv"]),
              "Wout": _np.ascontiguousarray(inputs["L1_xattn_W_out"]), "bout": _np.ascontiguousarray(inputs["L1_xattn_b_out"]),
              "WgA": _np.ascontiguousarray(_np.concatenate([inputs["L1_ffn_Wg"], _np.asarray(inputs["L1_ffn_A"]).reshape(16, 512)]).T),
              "bg": _np.ascontiguousarray(inputs["L1_ffn_bg"]), "WiT": _np.ascontiguousarray(inputs["L1_ffn_Wi"].T),
              "WoT": _np.ascontiguousarray(inputs["L1_ffn_Wo"].T),
              "Bt": _np.ascontiguousarray(_np.asarray(inputs["L1_ffn_B"]).transpose(0, 2, 1)).reshape(16, 2048),
              "ctxT": _np.ascontiguousarray(ctx_rows.transpose(0, 2, 1))}
    io = {n: nc.dram_tensor("in_" + n, a.shape, _mybir.dt.from_np(a.dtype), kind="ExternalInput").ap() for n, a in arrays.items()}
    io["out"] = nc.dram_tensor("out", (8, 100, 512), FP32, kind="ExternalOutput").ap()
    sc = {"dist": nc.dram_tensor("dist", (8, 722, 100), FP32, kind="Internal").ap(),
          "xg": nc.dram_tensor("xg", (SLOT_TILES * P, D), FP32, kind="Internal").ap(),
          "yg": nc.dram_tensor("yg", (SLOT_TILES * P, D), FP32, kind="Internal").ap(),
          "path": nc.dram_tensor("path", (8, 722, 100), BF16, kind="Internal").ap()}
    build(nc, io, sc)
    r = _run(nc, [{"in_" + n: a for n, a in arrays.items()}], core_ids=[0])
    return r.results[0]["out"]
```

```python
import numpy as np
import concourse.bass as bass
from concourse import mybir
from contextlib import ExitStack

FP32 = mybir.dt.float32
BF16 = mybir.dt.bfloat16
I32 = mybir.dt.int32
U32 = mybir.dt.uint32
ALU = mybir.AluOpType
ACT = mybir.ActivationFunctionType
AX = mybir.AxisListType.X

B, S, D = 8, 100, 512
C = 722
P = 128
KD = D // P
CT = -(-C // P)
CR = [min(P, C - P * t) for t in range(CT)]
NB = P // B
BL = -(-C // NB)
SK = 2
ST = S + SK * (NB - 1)
BIG = 1e30
EPS = 1e-5


def allocator(nc, ctx):
    used = []

    def clear():
        nc.clear_and_free_semaphores(used)
        nc.all_engine_barrier()
    ctx.callback(clear)

    def sb(name, shape, dt=FP32):
        return ctx.enter_context(nc.sbuf_tensor(name, shape, dt))

    def pb(name, shape):
        n = 1
        for m in shape[1:]:
            n *= m
        bank = ctx.enter_context(nc.psum_tensor(name, [P, 512], FP32))[0:shape[0], 0:n]
        return bank if len(shape) == 2 else bank.rearrange("p (a b) -> p a b", b=shape[2])

    def sem(name):
        used.append(nc.alloc_semaphore(name))
        return used[-1]
    return sb, pb, sem


def make_linker(eng, sem):
    def link(ins):
        sem[1] += 1
        ins.then_inc(sem[0], 1)
        eng.wait_ge(sem[0], sem[1])
    return link


def distances(nc, io, res):
    ctx = ExitStack()
    with ctx:
        sb, pb, sem = allocator(nc, ctx)
        x_sb, ident = res["x"], res["ident"]
        ones = res["ones"]
        xl = sb("xl", [S, B, D])
        stats = sb("stats_a", [S, B, 6])
        mv = sb("mv_a", [S, B, 2])
        rstd = sb("rstd_a", [S, B])
        xlT = sb("xlT", [P, KD, B * S])
        xlq = sb("xlq", [P, KD, B * S])
        bb = sb("bb", [P, B * S])
        NCT = 4
        cT = [sb(f"cT{i}", [P, KD, C]) for i in range(NCT)]
        cq = [sb(f"cq{i}", [P, KD, C]) for i in range(2)]
        cs = [sb(f"cs{i}", [P, C]) for i in range(2)]
        aa = sb("aa", [P, B * CT])
        d2 = sb("d2", [P, 2, CT, S])
        ds = sb("ds", [P, 2, CT, S])
        tp = [pb(f"tpa{i}", [P, KD, P]) for i in range(2)]
        pbb = [pb(f"pbb{i}", [P, 512]) for i in range(2)]
        pd = [[pb(f"pd{i}", [P, 512]) for i in range(2)], [t[:, :, :].rearrange("p k s -> p (k s)") for t in tp]]
        pa = [pb(f"pa{i}", [P, CT]) for i in range(2)]
        x_in, id0, id1, on = sem("x_in"), sem("id0"), sem("id1"), sem("ones_set")
        ct_in = [sem(f"ct_in{i}") for i in range(NCT)]
        cq_ok, half_ok, cs_ok, aa_mm = sem("cq_ok"), sem("half_a"), sem("cs_a"), sem("aa_mm")
        st_ok, var_ok, rs_ok, xl_ok = sem("st_ok"), sem("var_ok"), sem("rs_ok"), sem("xl_ok")
        tp_ok, xt_ok, xq_ok, bb_mm, bb_ok = sem("tp_ok"), sem("xt_ok"), sem("xq_ok"), sem("bb_mm"), sem("bb_ok")
        aa_ok, pd_ok, d2_ok, ds_ok = sem("aa_ok"), sem("pd_ok"), sem("d2_ok"), sem("ds_ok")
        ds_out = [sem(f"ds_out{i}") for i in range(2)]
        zf, outside = sem("zf"), sem("outside")
        TPT = 3
        block = ctx.enter_context(nc.Block())

        def store(act, b):
            act.wait_ge(ds_ok, b + 1)
            act.dma_start(res["dist"][b, 0:P * (CT - 1), :].rearrange("(t p) j -> p t j", p=P),
                         ds[:, b % 2, 0:CT - 1, :]).then_inc(ds_out[b % 2], 16)
            act.dma_start(res["dist"][b, P * (CT - 1):C, :], ds[0:CR[-1], b % 2, CT - 1, :]).then_inc(ds_out[b % 2], 16)

        @block.sync
        def _(sp):
            sp.dma_start(x_sb[:, :, :], io["x"].rearrange("b s d -> s b d")).then_inc(x_in, 16)
            for b in range(B):
                if b >= NCT:
                    sp.wait_ge(pd_ok, 2 * (b - NCT + 1))
                    sp.wait_ge(cq_ok, b - NCT + 1)
                sp.dma_start(cT[b % NCT][:, :, :], io["ctxT"][b].rearrange("(k p) c -> p k c", p=P)).then_inc(ct_in[b % NCT], 16)
            for i in range(2):
                sp.wait_ge(ds_out[i], 32 * (B // 2))

        @block.gpsimd
        def _(pool):
            pool.memset(ident[:, :], 0.0).then_inc(id0, 1)
            pool.memset(ones[:, :], 1.0).then_inc(on, 1)
            pool.wait_ge(id0, 1)
            pool.affine_select(out=ident[:, :], in_=ident[:, :], compare_op=ALU.not_equal, fill=1.0, base=0,
                               pattern=[[-1, P]], channel_multiplier=1).then_inc(id1, 1)
            pool.memset(res["cost"][:, :, 0:ST - S], BIG).then_inc(outside, 1)
            pool.memset(res["cost"][:, :, S:ST], BIG).then_inc(outside, 1)
            pool.wait_ge(outside, 2)
            pool.memset(res["cost"][P - 32:P, C - (NB - 1) * BL:BL, ST - S:S], BIG)

        @block.vector
        def _(dve):
            link = make_linker(dve, res["dve_chain"])
            dve.memset(d2[:, :, :, :], 0.0).then_inc(zf, 1)
            dve.wait_ge(x_in, 16)
            for g in range(2):
                bs = slice(g * B // 2, (g + 1) * B // 2)
                layernorm_stats(link, dve, x_sb[:, bs, :], stats[:, bs, :], mv[:, bs, :], B // 2)
                dve.tensor_scalar(rstd[:, bs], mv[:, bs, 1], EPS, None, ALU.add).then_inc(var_ok, 1)
                dve.wait_ge(st_ok, g + 1)
                link(dve.reciprocal(rstd[:, bs], rstd[:, bs]))
                for b in range(g * B // 2, (g + 1) * B // 2):
                    dve.tensor_scalar(xl[:, b, :], x_sb[:, b, :], mv[:, b, 0:1], rstd[:, b:b + 1],
                                      ALU.subtract, ALU.mult).then_inc(xl_ok, 1)
            def square_sums(b):
                q = cq[b % 2]
                dve.wait_ge(cq_ok, b + 1)
                dve.tensor_tensor(q[:, 0:2, :], q[:, 0:2, :], q[:, 2:4, :], ALU.add).then_inc(half_ok, 1)
                dve.wait_ge(half_ok, b + 1)
                if b >= 2:
                    dve.wait_ge(aa_mm, b - 1)
                dve.tensor_tensor(cs[b % 2][:, :], q[:, 0, :], q[:, 1, :], ALU.add).then_inc(cs_ok, 1)

            def squares(b):
                dve.wait_ge(aa_mm, b + 1)
                dve.tensor_copy(aa[:, b * CT:b * CT + CT - 1], pa[b % 2][:, 0:CT - 1])
                dve.tensor_copy(aa[0:CR[-1], b * CT + CT - 1:b * CT + CT], pa[b % 2][0:CR[-1], CT - 1:CT]).then_inc(aa_ok, 1)
                dve.wait_ge(aa_ok, b + 1)
                if b >= 2:
                    dve.wait_ge(ds_ok, b - 1)
                for t in range(CT):
                    if t % TPT == 0:
                        dve.wait_ge(pd_ok, 2 * b + t // TPT + 1)
                    r, q = CR[t], t % TPT
                    ins = dve.scalar_tensor_tensor(d2[0:r, b % 2, t, :], pd[b % 2][t // TPT][0:r, q * S:(q + 1) * S],
                                                   aa[0:r, b * CT + t:b * CT + t + 1], bb[0:r, b * S:(b + 1) * S],
                                                   ALU.add, ALU.add)
                    if q == TPT - 1:
                        ins.then_inc(d2_ok, 1)
                dve.wait_ge(d2_ok, 2 * b + 2)
                dve.tensor_scalar(d2[:, b % 2, :, :], d2[:, b % 2, :, :], 0.0, None, ALU.max).then_inc(rs_ok, 1)

            square_sums(0)
            for g in range(2):
                dve.wait_ge(bb_mm, g + 1)
                dve.tensor_copy(bb[:, g * 400:(g + 1) * 400], pbb[g][:, 0:400]).then_inc(bb_ok, 1)
            dve.wait_ge(bb_ok, 2)
            for n in range(B):
                if n + 1 < B:
                    square_sums(n + 1)
                squares(n)

        def roots(act, b):
            act.wait_ge(rs_ok, b + 1)
            if b >= 2:
                act.wait_ge(ds_out[b % 2], 32 * (b // 2))
            act.activation(ds[:, b % 2, :, :], d2[:, b % 2, :, :], ACT.Sqrt).then_inc(ds_ok, 1)
            store(act, b)

        @block.scalar
        def _(act):
            for g in range(2):
                act.wait_ge(var_ok, g + 1)
                act.activation(rstd[:, g * B // 2:(g + 1) * B // 2], rstd[:, g * B // 2:(g + 1) * B // 2], ACT.Sqrt).then_inc(st_ok, 1)
            for b in range(B):
                act.wait_ge(tp_ok, b + 1)
                act.activation(xlT[:, :, b * S:(b + 1) * S], tp[b % 2][:, :, 0:S], ACT.Copy, scale=-2.0).then_inc(xt_ok, 1)
            for n in range(B + 3):
                if n < B:
                    act.wait_ge(ct_in[n % NCT], 16 * (n // NCT + 1))
                    if n >= 2:
                        act.wait_ge(cs_ok, n - 1)
                    act.activation(cq[n % 2][:, :, :], cT[n % NCT][:, :, :], ACT.Square).then_inc(cq_ok, 1)
                if n == 0:
                    for g in range(2):
                        act.wait_ge(xt_ok, 4 * g + 4)
                        act.activation(xlq[:, :, g * 400:(g + 1) * 400], xlT[:, :, g * 400:(g + 1) * 400], ACT.Square,
                                       scale=0.5).then_inc(xq_ok, 1)
                if n >= 3:
                    roots(act, n - 3)

        @block.tensor
        def _(pe):
            pe.wait_ge(id1, 1)
            pe.wait_ge(on, 1)
            for b in range(B):
                pe.wait_ge(xl_ok, b + 1)
                if b >= 2:
                    pe.wait_ge(xt_ok, b - 1)
                for k in range(KD):
                    ins = pe.transpose(tp[b % 2][:, k, 0:S], xl[:, b, k * P:(k + 1) * P], ident[0:S, 0:S])
                ins.then_inc(tp_ok, 1)
            def products(b):
                pe.wait_ge(ct_in[b % NCT], 16 * (b // NCT + 1))
                if b < 2:
                    pe.wait_ge(xt_ok, (1, B)[b])
                for t in range(CT):
                    r, q = CR[t], t % TPT
                    if q == 0 and b >= 2:
                        pe.wait_ge(d2_ok, 2 * b + t // TPT - 3)
                    for k in range(KD):
                        ins = pe.matmul(pd[b % 2][t // TPT][0:r, q * S:(q + 1) * S], cT[b % NCT][:, k, t * P:t * P + r],
                                        xlT[:, k, b * S:(b + 1) * S], start=k == 0, stop=k == KD - 1)
                    if q == TPT - 1:
                        ins.then_inc(pd_ok, 1)

            def lengths(b):
                pe.wait_ge(cs_ok, b + 1)
                if b >= 2:
                    pe.wait_ge(aa_ok, b - 1)
                for t in range(CT):
                    ins = pe.matmul(pa[b % 2][0:CR[t], t:t + 1], cs[b % 2][:, t * P:t * P + CR[t]], ones[:, 0:1], start=True, stop=True)
                ins.then_inc(aa_mm, 1)

            products(0)
            lengths(0)
            for g in range(2):
                pe.wait_ge(xq_ok, g + 1)
                for k in range(KD):
                    ins = pe.matmul(pbb[g][:, 0:400], ones[:, :], xlq[:, k, g * 400:(g + 1) * 400], start=k == 0, stop=k == KD - 1)
                ins.then_inc(bb_mm, 1)
            for n in range(1, B):
                lengths(n)
                products(n)


def warp(nc, io, res):
    ctx = ExitStack()
    with ctx:
        sb, pb, sem = allocator(nc, ctx)
        cost_mem, cost = res["cost_mem"], res["cost"]
        path = cost_mem[:, 0:(BL + 2) * ST // 2].bitcast(BF16).rearrange("p (a s) -> p a s", s=ST)
        rise = cost_mem[:, (BL + 2) * ST // 2:(BL + 2) * ST].bitcast(BF16).rearrange("p (a s) -> p a s", s=ST)
        reach_mem = sb("reach_mem", [P, (BL + 2) * ST])
        reach = reach_mem[:, 0:(BL + 1) * (ST + 1)].rearrange("p (a s) -> p a s", s=ST + 1)
        reach_up = sb("reach_up", [P, BL + 1, ST + 1])
        path_down = reach_up[:, :, :].rearrange("p a s -> p (a s)")[:, 0:BL * ST // 2 + 1].bitcast(BF16)[:, 0:BL * ST].rearrange("p (a s) -> p a s", s=ST)
        step_min = sb("step_min", [P, BL])
        lastrow = sb("lastrow", [P, 1])
        down = sb("down", [P, P])
        up = sb("up", [P, P], BF16)
        move = reach_mem[:, 0:(BL + 2) * ST // 2].bitcast(BF16).rearrange("p (a s) -> p a s", s=ST)
        CH = ST // 2
        best = sb("best", [P, BL, CH])
        diag = sb("diag", [P, BL, CH], BF16)
        flow = sb("flow", [P, BL + 2], BF16)
        into = sb("into", [P, BL + 1], BF16)
        ph = [pb(f"ph{i}", [P, 512]) for i in range(4)]
        c_in, k_set, k2_set = sem("c_in"), sem("k_set"), sem("k2_set")
        scanned, handed, scanned_r, handed_r = sem("scanned"), sem("handed"), sem("scanned_r"), sem("handed_r")
        least, flowed, summed = sem("least"), sem("flowed"), sem("summed")
        p_out, zero_set, z_out = sem("p_out"), sem("zero_set"), sem("z_out")
        ctx_rows, rows_in = res["ctx_rows"], sem("rows_in")
        turned, row_out = sem("turned"), sem("row_out")
        zero = sb("zero", [P, D])
        last_rows = C - (NB - 1) * BL
        U = len(ph)
        block = ctx.enter_context(nc.Block())

        def turn_rows(eng, copy, rows):
            eng.wait_ge(scanned, SK + 2 * (ST - SK))
            for a in rows:
                copy(reach_up[:, BL - a, :], reach[:, a, :]).then_inc(turned, 1)

        def moves(dve, c, link):
            cd, cu, cl = reach_up[:, 1:BL + 1, c:c + CH], reach_up[:, 1:BL + 1, c + 1:c + CH + 1], reach_up[:, 0:BL, c:c + CH]
            mv, rs = move[:, 1:BL + 1, c:c + CH], rise[:, 1:BL + 1, c:c + CH]
            dve.tensor_tensor(mv, cl, cu, ALU.is_lt)
            link(dve.tensor_tensor(best[:, :, :], cu, cl, ALU.min))
            link(dve.tensor_tensor(diag[:, :, :], cd, best[:, :, :], ALU.is_le))
            link(dve.tensor_tensor(mv, mv, diag[:, :, :], ALU.is_gt))
            link(dve.tensor_tensor(mv, mv, diag[:, :, :], ALU.subtract))
            link(dve.tensor_scalar(rs, mv, 0.0, None, ALU.is_equal))

        def rows_out(eng, copy, rows):
            eng.wait_ge(scanned_r, ST)
            for a in rows:
                copy(path_down[:, a, :], path[:, BL - a, :]).then_inc(row_out, 1)

        @block.sync
        def _(sp):
            for k in range(NB):
                r = BL if k < NB - 1 else last_rows
                sp.dma_start(cost[k * B:(k + 1) * B, 0:r, SK * k:SK * k + S],
                             res["dist"][:, k * BL:k * BL + r, :]).then_inc(c_in, 16)
            for b in range(B):
                sp.dma_start(ctx_rows[:, b * CT:b * CT + CT - 1, :],
                             io["ctx"][b, 0:P * (CT - 1), :].rearrange("(t p) d -> p t d", p=P)).then_inc(rows_in, 16)
                sp.dma_start(ctx_rows[0:CR[-1], b * CT + CT - 1, :], io["ctx"][b, P * (CT - 1):C, :]).then_inc(rows_in, 16)
            sp.wait_ge(zero_set, 1)
            for t in range(SLOT_TILES):
                sp.dma_start(res["xg"][t * P:(t + 1) * P, :], zero[:, :]).then_inc(z_out, 16)
                sp.dma_start(res["yg"][t * P:(t + 1) * P, :], zero[:, :]).then_inc(z_out, 16)
            sp.wait_ge(row_out, BL)
            for k in range(NB):
                r = BL if k < NB - 1 else last_rows
                sp.dma_start(res["path"][:, k * BL:k * BL + r, :],
                             path_down[k * B:(k + 1) * B, 0:r, SK * k:SK * k + S]).then_inc(p_out, 16)
            sp.wait_ge(p_out, 16 * NB)
            sp.wait_ge(rows_in, 32 * B)
            sp.wait_ge(z_out, 32 * SLOT_TILES)

        @block.gpsimd
        def _(pool):
            pool.memset(reach[:, 0, 0:SK + 1], BIG).then_inc(k_set, 1)
            pool.memset(reach[:, 1:BL + 1, 0], BIG).then_inc(k_set, 1)
            pool.memset(down[:, :], 0.0).then_inc(k_set, 1)
            pool.memset(up[:, :], 0.0).then_inc(k_set, 1)
            pool.memset(lastrow[:, :], 0.0).then_inc(k_set, 1)
            pool.wait_ge(k_set, 5)
            pool.affine_select(out=lastrow[:, :], in_=lastrow[:, :], compare_op=ALU.is_gt, fill=1.0, base=P - B,
                               pattern=[[0, 1]], channel_multiplier=-1).then_inc(k2_set, 1)
            pool.memset(reach[0:B, 0, 0:1], 0.0).then_inc(k2_set, 1)
            pool.affine_select(out=down[:, :], in_=down[:, :], compare_op=ALU.not_equal, fill=1.0, base=B,
                               pattern=[[-1, P]], channel_multiplier=1).then_inc(k2_set, 1)
            pool.wait_ge(k2_set, 3)
            pool.affine_select(out=down[:, :], in_=down[:, :], compare_op=ALU.not_equal, fill=1.0, base=B - P,
                               pattern=[[-1, P]], channel_multiplier=1).then_inc(k2_set, 1)
            pool.affine_select(out=up[:, :], in_=up[:, :], compare_op=ALU.not_equal, fill=1.0, base=-B,
                               pattern=[[-1, P]], channel_multiplier=1).then_inc(k2_set, 1)

            turn_rows(pool, pool.tensor_copy, range(1, BL + 1, 8))
            rows_out(pool, pool.tensor_copy, range(1, BL, 8))

        @block.scalar
        def _(act):
            turn_rows(act, act.copy, [a for a in range(0, BL + 1, 3) if a % 8 != 1])
            rows_out(act, act.copy, [a for a in range(0, BL, 3) if a % 8 != 1])

        def col(a):
            return a.rearrange("p a o -> p (a o)")


        @block.tensor
        def _(pe):
            pe.wait_ge(k2_set, 5)

            def hand(s, u):
                pe.wait_ge(scanned, min(s + 1, SK) + 2 * max(0, s + 1 - SK))
                pe.matmul(ph[u][:, 0:1], down[:, :], reach[:, BL, s + 1:s + 2], start=True, stop=True).then_inc(handed, 1)

            for s in range(ST - SK):
                hand(s, s % U)

            def hand_back(n, s, u):
                pe.wait_ge(scanned_r, n + 1)
                pe.matmul(ph[u][:, 0:1], up[:, :], path[:, BL + 1, s:s + 1], start=True, stop=True).then_inc(handed_r, 1)

            for n in range(ST - SK):
                hand_back(n, ST - 1 - n, n % U)

        @block.vector
        def _(dve):
            link = make_linker(dve, res["dve_chain"])
            dve.memset(zero[:, :], 0.0).then_inc(zero_set, 1)
            dve.wait_ge(k2_set, 5)
            dve.wait_ge(c_in, 16 * NB)
            assert last_rows < BL
            def step(s, u):
                if s:
                    dve.wait_ge(scanned, min(s, SK) + 2 * max(0, s - SK))
                dve.tensor_tensor(step_min[:, :], col(reach[:, 1:BL + 1, s:s + 1]),
                                  col(reach[:, 0:BL, s:s + 1]), ALU.min).then_inc(least, 1)
                if u is not None:
                    dve.wait_ge(handed, s - SK + 1)
                    dve.tensor_copy(reach[:, 0, s + 1:s + 2], ph[u][:, 0:1]).then_inc(scanned, 1)
                dve.wait_ge(least, s + 1)
                dve.tensor_tensor_scan(col(reach[:, 1:BL + 1, s + 1:s + 2]), step_min[:, :],
                                       col(cost[:, :, s:s + 1]), reach[:, 0, s + 1:s + 2] if u is None else ph[u][:, 0:1],
                                       ALU.min, ALU.add).then_inc(scanned, 1)

            for s in range(SK):
                step(s, None)
            for s in range(SK, ST):
                step(s, (s - SK) % U)


            turn_rows(dve, dve.tensor_copy, [a for a in range(BL + 1) if a % 3 and a % 8 != 1])
            dve.memset(path[:, 0, :], 0.0)
            dve.memset(rise[:, 0, :], 1.0)
            dve.memset(rise[:, BL + 1, :], 0.0)
            dve.wait_ge(turned, BL + 1)
            dve.memset(move[:, 0, :], 0.0)
            link(dve.memset(move[:, BL + 1, :], 0.0))
            for c in range(0, ST, CH):
                moves(dve, c, link)

            seed = dve.memset(into[:, :], 0.0)
            link(seed)
            link(dve.tensor_copy(into[:, BL - last_rows:BL - last_rows + 1], lastrow[:, 0:1]))

            def back(n, s, u):
                if n:
                    dve.wait_ge(scanned_r, n)
                    dve.tensor_tensor(flow[:, :], col(move[:, :, s + 1:s + 2]), col(path[:, :, s + 1:s + 2]),
                                      ALU.mult).then_inc(flowed, 1)
                    dve.wait_ge(flowed, n)
                    dve.tensor_tensor(into[:, :], flow[:, 1:BL + 2], flow[:, 0:BL + 1], ALU.subtract).then_inc(summed, 1)
                    dve.wait_ge(summed, n)
                if u is not None:
                    dve.wait_ge(handed_r, n - SK + 1)
                dve.tensor_tensor_scan(col(path[:, 1:BL + 2, s:s + 1]), col(rise[:, 0:BL + 1, s:s + 1]), into[:, :],
                                       0.0 if u is None else ph[u][:, 0:1], ALU.mult, ALU.max).then_inc(scanned_r, 1)

            for n in range(SK):
                back(n, ST - 1 - n, None)
            for n in range(SK, ST):
                back(n, ST - 1 - n, (n - SK) % U)
            rows_out(dve, dve.tensor_copy, [a for a in range(BL) if a % 3 and a % 8 != 1])



E_N, H = 16, 1024
HJ = H // P
TOPK = 3
SLOT_TILES = B * S * TOPK // P + E_N
XT = B * S


def layernorm_stats(link, dve, src, stats, mv, n):
    for i in range(n):
        ins = dve.bn_stats(stats[:, i, :], src[:, i, :])
    link(ins)
    for i in range(n):
        ins = dve.bn_aggr(mv[:, i, :], stats[:, i, :])
    link(ins)


def route(nc, io, res):
    ctx = ExitStack()
    with ctx:
        sb, pb, sem = allocator(nc, ctx)
        x_sb, ctx_rows, ident, ones = res["x"], res["ctx_rows"], res["ident"], res["ones"]
        pathb = sb("pathb", [P, B * CT, S], BF16)
        pathf = sb("pathf", [P, B * CT, S])
        gate_w = sb("gate_w", [P, KD, E_N])
        xn = sb("xn", [S, B, D])
        stats, mv, rstd = sb("stats_c", [S, B, 6]), sb("mv_c", [S, B, 2]), sb("rstd_c", [S, B])
        xnT = [sb(f"xnT{i}", [P, KD, S]) for i in range(2)]
        logit = sb("logit", [S, B, E_N])
        prob = sb("prob", [S, B, E_N])
        lmax, lsum = sb("lmax", [S, B]), sb("lsum", [S, B])
        top = sb("top", [S, B, 8])
        topi = sb("topi", [S, B, 8], U32)
        topf = sb("topf", [S, B, 8])
        tsum = sb("tsum", [S, B])
        iota_e = sb("iota_e", [S, E_N])
        hot = [sb(f"hot{k}", [S, B, E_N]) for k in range(TOPK)]
        chosen = sb("chosen", [S, B, E_N])
        before = sb("before", [S, S])
        tot = sb("tot", [S, B, E_N])
        off = sb("off", [S, B + 1, E_N])
        ntile, tiles_to, one_e = sb("ntile", [S, E_N]), sb("tiles_to", [S, E_N]), sb("one_e", [S, E_N])
        slot = sb("slot", [S, B, E_N])
        picked = sb("picked", [S, B, E_N])
        slotf = sb("slotf", [S, TOPK, B])
        px = [pb(f"px{i}", [S, D]) for i in range(2)]
        pt = [pb(f"pt{i}", [P, KD, P]) for i in range(2)]
        pl = pb("pl", [S, B, E_N])
        prank = pb("prank", [S, B * E_N])
        ptot = pb("ptot", [S, B, E_N])
        path_in, gate_in = [sem(f"path_in{b}") for b in range(B)], sem("gate_in")
        pathf_ok, px_ok, x_ok, var_ok, st_ok, xn_ok = (sem(n) for n in ("pathf_ok", "px_ok", "x_ok", "var_c", "st_c", "xn_ok"))
        pt_ok, xnT_ok, pl_ok, sub_ok, exp_ok, cs_ok = (sem(n) for n in ("pt_ok", "xnT_ok", "pl_ok", "sub_ok", "exp_ok", "cs_ok"))
        cs0, hot_ok, rank_ok, slot_ok, sent = (sem(n) for n in ("cs0", "hot_ok", "rank_ok", "slot_ok", "sent"))
        block = ctx.enter_context(nc.Block())

        @block.sync
        def _(sp):
            sp.dma_start(gate_w[:, :, :], io["gate"].rearrange("(k p) e -> p k e", p=P)).then_inc(gate_in, 16)
            for b in range(B):
                sp.dma_start(pathb[:, b * CT:b * CT + CT - 1, :],
                             res["path"][b, 0:P * (CT - 1), :].rearrange("(t p) j -> p t j", p=P)).then_inc(path_in[b], 16)
                sp.dma_start(pathb[0:CR[-1], b * CT + CT - 1, :], res["path"][b, P * (CT - 1):C, :]).then_inc(path_in[b], 16)

        @block.gpsimd
        def _(pool):
            pool.iota(iota_e[:, :], pattern=[[1, E_N]], base=0, channel_multiplier=0,
                      allow_small_or_imprecise_dtypes=True).then_inc(cs_ok, 1)
            pool.memset(before[:, :], 1.0).then_inc(cs0, 1)
            pool.wait_ge(cs0, 1)
            pool.affine_select(out=before[:, :], in_=before[:, :], compare_op=ALU.is_gt, fill=0.0, base=0,
                               pattern=[[1, S]], channel_multiplier=-1).then_inc(cs_ok, 1)
            pool.wait_ge(slot_ok, 1)
            for k in range(TOPK):
                for b in range(B):
                    pool.indirect_dma_start(out=res["xg"], out_offset=bass.IndirectOffsetOnAxis(ap=res["slots"][:, k * B + b:k * B + b + 1], axis=0),
                                            in_=xn[:, b, :], in_offset=None).then_inc(sent, 16)
            pool.wait_ge(sent, 16 * TOPK * B)

        @block.tensor
        def _(pe):
            def along_path(b):
                pe.wait_ge(pathf_ok, b + 1)
                if b >= 2:
                    pe.wait_ge(x_ok, b - 1)
                for t in range(CT):
                    r = CR[t]
                    ins = pe.matmul(px[b % 2][:, :], pathf[0:r, b * CT + t, :], ctx_rows[0:r, b * CT + t, :], start=t == 0, stop=t == CT - 1)
                ins.then_inc(px_ok, 1)

            def turn(b):
                pe.wait_ge(xn_ok, b + 1)
                if b >= 2:
                    pe.wait_ge(xnT_ok, b - 1)
                for k in range(KD):
                    ins = pe.transpose(pt[b % 2][:, k, 0:S], xn[:, b, k * P:(k + 1) * P], ident[0:S, 0:S])
                ins.then_inc(pt_ok, 1)

            def logits(b):
                if b == 0:
                    pe.wait_ge(gate_in, 16)
                pe.wait_ge(xnT_ok, b + 1)
                for k in range(KD):
                    ins = pe.matmul(pl[:, b, :], xnT[b % 2][:, k, :], gate_w[:, k, :], start=k == 0, stop=k == KD - 1)
                ins.then_inc(pl_ok, 1)

            for n in range(B + 2):
                if n < B:
                    along_path(n)
                if 1 <= n <= B:
                    turn(n - 1)
                if n >= 2:
                    logits(n - 2)
            pe.wait_ge(hot_ok, 1)
            pe.wait_ge(cs_ok, 2)
            pe.matmul(prank[:, :], before[:, :], chosen[:, :, :].rearrange("p b e -> p (b e)"), start=True, stop=True).then_inc(rank_ok, 1)
            pe.matmul(ptot[:, :, :].rearrange("p b e -> p (b e)"), ones[0:S, 0:S], chosen[:, :, :].rearrange("p b e -> p (b e)"), start=True, stop=True).then_inc(rank_ok, 1)

        @block.scalar
        def _(act):
            for b in range(B):
                act.wait_ge(var_ok, b + 1)
                act.activation(rstd[:, b:b + 1], rstd[:, b:b + 1], ACT.Sqrt).then_inc(st_ok, 1)
            act.wait_ge(sub_ok, 1)
            act.activation(prob[:, :, :], logit[:, :, :], ACT.Exp).then_inc(exp_ok, 1)

        @block.vector
        def _(dve):
            link = make_linker(dve, res["dve_chain"])
            dve.memset(one_e[:, :], 1.0)
            for b in range(B):
                n = b * CT
                dve.wait_ge(path_in[b], 32)
                dve.tensor_copy(pathf[:, n:n + CT - 1, :], pathb[:, n:n + CT - 1, :])
                dve.tensor_copy(pathf[0:CR[-1], n + CT - 1, :], pathb[0:CR[-1], n + CT - 1, :]).then_inc(pathf_ok, 1)
            def keep_T(b):
                dve.wait_ge(pt_ok, b + 1)
                if b >= 2:
                    dve.wait_ge(pl_ok, b - 1)
                dve.tensor_copy(xnT[b % 2][:, :, :], pt[b % 2][:, :, 0:S]).then_inc(xnT_ok, 1)

            for b in range(B):
                dve.wait_ge(px_ok, b + 1)
                dve.tensor_tensor(x_sb[:, b, :], x_sb[:, b, :], px[b % 2][:, :], ALU.add).then_inc(x_ok, 1)
                dve.wait_ge(x_ok, b + 1)
                link(dve.bn_stats(stats[:, b, :], x_sb[:, b, :]))
                link(dve.bn_aggr(mv[:, b, :], stats[:, b, :]))
                dve.tensor_scalar(rstd[:, b:b + 1], mv[:, b, 1:2], EPS, None, ALU.add).then_inc(var_ok, 1)
                dve.wait_ge(st_ok, b + 1)
                link(dve.reciprocal(rstd[:, b:b + 1], rstd[:, b:b + 1]))
                dve.tensor_scalar(xn[:, b, :], x_sb[:, b, :], mv[:, b, 0:1], rstd[:, b:b + 1], ALU.subtract, ALU.mult).then_inc(xn_ok, 1)
                if b:
                    keep_T(b - 1)
            keep_T(B - 1)
            dve.wait_ge(pl_ok, B)
            link(dve.tensor_reduce(lmax[:, :], pl[:, :, :], AX, ALU.max))
            dve.tensor_tensor(logit[:, :, :], pl[:, :, :], lmax[:, :].unsqueeze(2).broadcast_to([S, B, E_N]), ALU.subtract).then_inc(sub_ok, 1)
            dve.wait_ge(exp_ok, 1)
            link(dve.tensor_reduce(lsum[:, :], prob[:, :, :], AX, ALU.add))
            link(dve.reciprocal(lsum[:, :], lsum[:, :]))
            link(dve.tensor_tensor(prob[:, :, :], prob[:, :, :], lsum[:, :].unsqueeze(2).broadcast_to([S, B, E_N]), ALU.mult))
            for b in range(B):
                ins = dve.max(top[:, b, :], prob[:, b, :])
            link(ins)
            for b in range(B):
                ins = dve.max_index(topi[:, b, :], top[:, b, :], prob[:, b, :])
            link(ins)
            link(dve.tensor_copy(topf[:, :, :], topi[:, :, :]))
            dve.wait_ge(cs_ok, 2)
            for k in range(TOPK):
                ins = dve.tensor_tensor(hot[k][:, :, :], iota_e[:, :].unsqueeze(1).broadcast_to([S, B, E_N]),
                                        topf[:, :, k:k + 1].broadcast_to([S, B, E_N]), ALU.is_equal)
            link(ins)
            link(dve.tensor_tensor(chosen[:, :, :], hot[0][:, :, :], hot[1][:, :, :], ALU.add))
            ins = dve.tensor_tensor(chosen[:, :, :], chosen[:, :, :], hot[2][:, :, :], ALU.add)
            ins.then_inc(hot_ok, 1)
            link(dve.tensor_reduce(tsum[:, :], top[:, :, 0:TOPK], AX, ALU.add))
            link(dve.tensor_scalar(tsum[:, :], tsum[:, :], 1e-12, None, ALU.max))
            link(dve.reciprocal(tsum[:, :], tsum[:, :]))
            for k in range(TOPK):
                dve.tensor_tensor(res["gates"][:, k, :], top[:, :, k], tsum[:, :], ALU.mult)
            dve.wait_ge(rank_ok, 2)
            dve.memset(off[:, 0, :], 0.0)
            link(dve.tensor_copy(tot[:, :, :], ptot[:, :, :]))
            for b in range(B):
                link(dve.tensor_tensor(off[:, b + 1, :], off[:, b, :], tot[:, b, :], ALU.add))
            link(dve.memset(ntile[:, :], 1.0))
            for m in range(1, -(-XT // P)):
                link(dve.scalar_tensor_tensor(ntile[:, :], off[:, B, :], float(P * m), ntile[:, :], ALU.is_gt, ALU.add))
            link(dve.tensor_tensor_scan(tiles_to[:, :], one_e[:, :], ntile[:, :], 0.0, ALU.mult, ALU.add))
            dve.memset(res["table"][:, 0:1], 0)
            dve.tensor_copy(res["table"][:, 1:E_N + 1], tiles_to[:, :])
            link(dve.tensor_tensor(ntile[:, :], tiles_to[:, :], ntile[:, :], ALU.subtract))
            link(dve.tensor_tensor(slot[:, :, :], prank[:, :].rearrange("p (b e) -> p b e", e=E_N), off[:, 0:B, :], ALU.add))
            link(dve.scalar_tensor_tensor(slot[:, :, :], ntile[:, :].unsqueeze(1).broadcast_to([S, B, E_N]), float(P), slot[:, :, :], ALU.mult, ALU.add))
            for k in range(TOPK):
                link(dve.tensor_tensor(picked[:, :, :], hot[k][:, :, :], slot[:, :, :], ALU.mult))
                link(dve.tensor_reduce(slotf[:, k, :], picked[:, :, :], AX, ALU.add))
            dve.tensor_copy(res["slots"][:, :], slotf[:, :, :].rearrange("p k b -> p (k b)")).then_inc(slot_ok, 1)


INNER, HEADS, DH = 512, 8, 64
KC = P
NK = KC + S
NKD = C + S


def keep_rows(io, res, sb, sem, banks):
    mask8 = sb("mask8", [P, CT, B], mybir.dt.uint8)
    kept = sb("kept", [P, CT, B], BF16)
    lower = sb("lower", [P, P], BF16)
    onesb = sb("onesb", [P, P], BF16)
    slots_row = sb("slots_row", [P, KC])
    where = sb("where", [P, CT, 3], BF16)
    tot = sb("tot_k", [P, CT, B])
    off = sb("off_k", [P, CT + 1, B])
    pos = sb("pos_k", [P, CT, B])
    sel = [sb(f"sel{i}", [P, CT, KC], BF16) for i in range(2)]
    idxf = sb("idxf", [P, B])
    t128 = sb("t128", [P, B])
    base = sb("base_k", [P, B])
    idx = sb("idx_k", [P, B], I32)
    stats, mv, rstd = sb("stats_k", [P, B, 6]), sb("mv_k", [P, B, 2]), sb("rstd_k", [P, B])
    flag = sb("flag", [P, B])
    one8 = sb("one8", [P, B])
    runs = sb("runs", [P, B])
    kbias = res["kbias"]
    prk, ptk = banks[4][:, 0:CT * B], banks[4][:, CT * B:2 * CT * B]
    pidx = [banks[i][:, 0:3] for i in range(2)]
    pfil = [banks[2 + i][:, 0:KC] for i in range(2)]
    m_in, m0, cs0, cs, kept_ok, rk_ok, sel_ok, idx_mm, idx_rd, idx_ok = (sem(n) for n in (
        "m_in", "m0", "cs0k", "csk", "kept_ok", "rk_ok", "sel_ok", "idx_mm", "idx_rd", "idx_ok"))
    g_in, vark, sqk = sem("g_in"), sem("vark"), sem("sqk")

    def load(sp):
        sp.wait_ge(m0, 1)
        for t in range(CT):
            sp.dma_start(mask8[0:CR[t], t, :], io["maskT"][t * P:t * P + CR[t], :]).then_inc(m_in, 16)

    def constants(pool):
        pool.memset(lower[:, :], 1.0).then_inc(cs0, 1)
        pool.memset(onesb[:, :], 1.0).then_inc(cs, 1)
        pool.iota(slots_row[:, :], pattern=[[1, KC]], base=0, channel_multiplier=0,
                  allow_small_or_imprecise_dtypes=True).then_inc(cs, 1)
        pool.iota(where[:, :, 0], pattern=[[0, CT]], base=0, channel_multiplier=1,
                  allow_small_or_imprecise_dtypes=True).then_inc(cs, 1)
        pool.iota(where[:, :, 1], pattern=[[1, CT]], base=0, channel_multiplier=0,
                  allow_small_or_imprecise_dtypes=True).then_inc(cs, 1)
        pool.memset(where[:, :, 2], 1.0).then_inc(cs, 1)
        pool.iota(base[:, :], pattern=[[C, B]], base=0, channel_multiplier=0,
                  allow_small_or_imprecise_dtypes=True).then_inc(cs, 1)
        pool.wait_ge(cs0, 1)
        pool.affine_select(out=lower[:, :], in_=lower[:, :], compare_op=ALU.is_gt, fill=0.0, base=0,
                           pattern=[[1, P]], channel_multiplier=-1).then_inc(cs, 1)

    def gather(pool):
        pool.wait_ge(idx_ok, 1)
        for b in range(B):
            pool.indirect_dma_start(out=res["rows_k"][:, b, :], out_offset=None, in_=io["ctx"].rearrange("b c d -> (b c) d"),
                                    in_offset=bass.IndirectOffsetOnAxis(ap=idx[:, b:b + 1], axis=0)).then_inc(g_in, 16)

    def ranks(pe):
        pe.wait_ge(cs, 7)
        pe.wait_ge(kept_ok, 1)
        pe.matmul(prk[:, :], lower[:, :], kept[:, :, :].rearrange("p t b -> p (t b)"), start=True, stop=True).then_inc(rk_ok, 1)
        pe.matmul(ptk[:, :], onesb[:, :], kept[:, :, :].rearrange("p t b -> p (t b)"), start=True, stop=True).then_inc(rk_ok, 1)

    def choose(pe, b):
        pe.wait_ge(sel_ok, b + 1)
        if b >= 2:
            pe.wait_ge(idx_rd, b - 1)
        for t in range(CT):
            pe.matmul(pidx[b % 2][:, :], sel[b % 2][:, t, :], where[:, t, :], start=t == 0, stop=t == CT - 1)
        for t in range(CT):
            ins = pe.matmul(pfil[b % 2][:, :], onesb[:, :], sel[b % 2][:, t, :], start=t == 0, stop=t == CT - 1)
        ins.then_inc(idx_mm, 1)

    def root(act):
        act.wait_ge(vark, 1)
        act.activation(rstd[:, :], rstd[:, :], ACT.Sqrt).then_inc(sqk, 1)

    def read_index(dve, b):
        dve.wait_ge(idx_mm, b + 1)
        dve.tensor_copy(idxf[:, b:b + 1], pidx[b % 2][:, 0:1])
        dve.tensor_copy(t128[:, b:b + 1], pidx[b % 2][:, 1:2])
        dve.tensor_scalar(kbias[:, b, 0:KC], pfil[b % 2][0:S, :], -BIG, BIG, ALU.mult, ALU.add).then_inc(idx_rd, 1)

    def rows(dve, link):
        dve.memset(mask8[:, :, :], 0).then_inc(m0, 1)
        dve.memset(off[:, 0, :], 0.0)
        dve.memset(one8[:, :], 1.0)
        dve.memset(kbias[:, :, KC:NK], 0.0)
        dve.memset(res["runs"][:, 0:1], 0)
        dve.wait_ge(m_in, 16 * CT)
        dve.tensor_copy(kept[:, :, :], mask8[:, :, :]).then_inc(kept_ok, 1)
        dve.wait_ge(rk_ok, 2)
        link(dve.tensor_copy(tot[:, :, :], ptk[:, :].rearrange("p (t b) -> p t b", b=B)))
        for t in range(CT):
            link(dve.tensor_tensor(off[:, t + 1, :], off[:, t, :], tot[:, t, :], ALU.add))
        link(dve.tensor_tensor(pos[:, :, :], prk[:, :].rearrange("p (t b) -> p t b", b=B), off[:, 0:CT, :], ALU.add))
        link(dve.scalar_tensor_tensor(pos[:, :, :], pos[:, :, :], 1.0, kept[:, :, :], ALU.add, ALU.mult))
        link(dve.tensor_scalar(pos[:, :, :], pos[:, :, :], -1.0, None, ALU.add))
        link(dve.tensor_scalar(flag[:, :], off[:, CT, :], float(KC), None, ALU.is_gt))
        link(dve.tensor_tensor_scan(runs[:, :], one8[:, :], flag[:, :], 0.0, ALU.mult, ALU.add))
        dve.tensor_copy(res["flag"][:, 0:B], flag[:, :])
        dve.tensor_scalar(res["flag"][:, B:B + 1], runs[:, B - 1:B], 1.0, None, ALU.is_ge)
        link(dve.tensor_copy(res["runs"][:, 1:B + 1], runs[:, :]))
        dve.wait_ge(cs, 7)
        for b in range(B):
            if b >= 2:
                dve.wait_ge(idx_mm, b - 1)
            for t in range(CT):
                ins = dve.tensor_scalar(sel[b % 2][:, t, :], slots_row[:, :], pos[:, t, b:b + 1], None, ALU.is_equal)
            ins.then_inc(sel_ok, 1)
            if b:
                read_index(dve, b - 1)
        read_index(dve, B - 1)
        dve.wait_ge(idx_rd, B)
        link(dve.scalar_tensor_tensor(idxf[:, :], t128[:, :], float(P), idxf[:, :], ALU.mult, ALU.add))
        link(dve.tensor_tensor(idxf[:, :], idxf[:, :], base[:, :], ALU.add))
        dve.tensor_copy(idx[:, :], idxf[:, :]).then_inc(idx_ok, 1)
        dve.wait_ge(g_in, 16 * B)
        rk = res["rows_k"]
        layernorm_stats(link, dve, rk, stats, mv, B)
        dve.tensor_scalar(rstd[:, :], mv[:, :, 1], EPS, None, ALU.add).then_inc(vark, 1)
        dve.wait_ge(sqk, 1)
        link(dve.reciprocal(rstd[:, :], rstd[:, :]))
        for b in range(B):
            dve.tensor_scalar(rk[:, b, :], rk[:, b, :], mv[:, b, 0:1], rstd[:, b:b + 1], ALU.subtract, ALU.mult)

    def free(act):
        act.wait_ge(idx_rd, B)
    return load, constants, gather, ranks, choose, root, rows, free


def experts(nc, io, res):
    ctx = ExitStack()
    with ctx:
        sb, pb, sem = allocator(nc, ctx)
        x_sb, ident = res["x"], res["ident"]
        W1 = [res["W_first"], sb("W1_1", [P, KD, H])]
        W2 = [res["W_second"], sb("W2_1", [P, HJ, D])]
        b1 = sb("b1", [P, E_N * HJ])
        b2 = [sb(f"b2_{u}", [P, D]) for u in range(2)]
        xgT, lat = res["tiles"], res["lat"]
        diag = xgT[0:S, B:B + 5, :].rearrange("p t d -> p (t d)")[:, 0:TOPK * B * S].rearrange("p (i s) -> p i s", s=S)
        diag_ok, sum_mm = sem("diag_ok"), sem("sum_mm")
        stats, mv = sb("stats_e", [S, 2, B, 6]), sb("mv_e", [S, 2, B, 2])
        rstd, nmr = sb("rstd_e", [S, 2, B]), sb("nmr_e", [S, B])
        hT = sb("hT", [P, HJ, P])
        y = sb("y", [P, D])
        NY = 8
        yk = res["att"]
        assert NY == B
        NX = 4
        xg = [yk[:, u, :] for u in range(NX)]
        NH = 4
        banks = [pb(f"phid{i}", [P, D]) for i in range(NH)]
        ph = [bank[:, 0:P] for bank in banks]
        py = pb("py", [P, D])
        ptx = [pb(f"ptx{i}", [P, KD * P]) for i in range(2)]
        w1_in, w2_in = [sem(f"w1_in{u}") for u in range(2)], [sem(f"w2_in{u}") for u in range(2)]
        b1_in, xg_in = sem("b1_in"), [sem(f"xg_in{u}") for u in range(NX)]
        xt_mm, xt_ok, h_mm, relu_ok, y_mm, y_ok, y_out, y_free = (sem(n) for n in (
            "xt_mm", "xt_okd", "h_mm", "relu_ok", "y_mm", "y_ok", "y_out", "y_free"))
        yk_in = [sem(f"yk_in{i}") for i in range(NY)]
        added, var_ok, root_ok, norm_ok, lat_ok = sem("added"), sem("var_e"), sem("root_e"), sem("norm_e"), sem("lat_e")
        load_mask, constants, gather_kept, ranks, choose, root, keep_all, free = keep_rows(io, res, sb, sem, banks + [py])
        TAIL = SLOT_TILES - SLOT_TILES % NX
        HEAD = 2 * B
        block = ctx.enter_context(nc.Block())
        first_tile = res["table"]

        def norms_of(m):
            return ([(0, b) for b in (2 * m, 2 * m + 1) if m < B // 2] + [(1, b) for b in (2 * m - 2, 2 * m - 1) if m])

        def tiles_of(eng, e):
            a = eng.value_load(first_tile[0:1, bass.ds(e, 1)], min_val=0, max_val=SLOT_TILES - 1)
            b = eng.value_load(first_tile[0:1, bass.ds(e + 1, 1)], min_val=1, max_val=SLOT_TILES)
            return a, b

        @block.sync
        def _(sp):
            def load(e, u):
                sp.dma_start(W1[u][:, :, :], io["W1"][bass.ds(e, 1), :, :].rearrange("o (k p) h -> p (o k) h", p=P)).then_inc(w1_in[u], 16)
                sp.dma_start(W2[u][:, :, :], io["W2"][bass.ds(e, 1), :, :].rearrange("o (j p) d -> p (o j) d", p=P)).then_inc(w2_in[u], 16)
                sp.dma_start(b2[u][:, :], io["b2"][bass.ds(e, 1), :].broadcast_to([P, D])).then_inc(w2_in[u], 16)

            def load_x(w, u, wait=True):
                if wait:
                    sp.wait_ge(xt_mm, w + (1 - NX))
                sp.dma_start(xg[u][:, :], res["xg"][bass.ds(w * P, P), :]).then_inc(xg_in[u], 16)

            for u in range(NX):
                load_x(u, u, False)
            load_mask(sp)
            for w in range(NX, HEAD):
                load_x(w, w % NX)
            with sp.Fori(HEAD, TAIL - 1, NX) as w:
                for u in range(NX):
                    load_x(w + u, u)
            for w in range(TAIL, SLOT_TILES):
                load_x(w, w % NX)
            load(0, 0)
            sp.dma_start(b1[:, :], io["b1T"]).then_inc(b1_in, 16)
            sp.dma_start(res["vec"][:, :, :], io["vec"]).then_inc(res["vec_in"], 16)
            sp.dma_start(res["gammas"][:, :], io["gammas"]).then_inc(res["vec_in"], 16)
            sp.dma_start(res["bout"][:, :], io["bout"].rearrange("(o d) -> o d", o=1).broadcast_to([S, D])).then_inc(res["vec_in"], 16)
            load(1, 1)
            with sp.Fori(2, E_N - 1, 2) as e:
                for u in range(2):
                    done = sp.value_load(first_tile[0:1, bass.ds(e + (u - 1), 1)], min_val=1, max_val=SLOT_TILES)
                    sp.wait_ge(y_ok, done + 1)
                    load(e + u, u)
            done = sp.value_load(first_tile[0:1, E_N - 1:E_N], min_val=1, max_val=SLOT_TILES)
            sp.wait_ge(y_ok, done + 1)
            sp.dma_start(res["Wq"], io["Wq"].rearrange("(k p) n -> p k n", p=P)).then_inc(res["attn_in"], 16)
            sp.dma_start(res["Wkv"], io["Wkv"].rearrange("(k p) n -> p k n", p=P)).then_inc(res["attn_in"], 16)
            sp.dma_start(res["Wo"], io["Wout"].rearrange("(k p) n -> p k n", p=P)).then_inc(res["attn_in"], 16)

        @block.tensor
        def _(pe):
            def turn(w, u, wait=True):
                pe.wait_ge(xg_in[u], NX * (w - u) + 16)
                if wait:
                    pe.wait_ge(xt_ok, w - 1)
                for k in range(KD):
                    ins = pe.transpose(ptx[u % 2][:, k * P:(k + 1) * P], xg[u][:, k * P:(k + 1) * P], ident[:, :])
                ins.then_inc(xt_mm, 1)

            turn(0, 0, False)
            turn(1, 1, False)
            ranks(pe)
            for b in range(B):
                if b:
                    turn(2 * b, 2 * b % NX)
                    turn(2 * b + 1, (2 * b + 1) % NX)
                choose(pe, b)
            with pe.Fori(HEAD, TAIL - 1, NX) as w:
                for u in range(NX):
                    turn(w + u, u)
            for w in range(TAIL, SLOT_TILES):
                turn(w, w % NX)

            with pe.Fori(0, E_N - 1, 2) as e:
                for u in range(2):
                    t0, t1 = tiles_of(pe, e + u)
                    with pe.Fori(t0, t1) as w:
                        pe.wait_ge(w1_in[u], 8 * e + 16)
                        pe.wait_ge(xt_ok, w + 1)
                        for j in range(HJ + 2):
                            if j < HJ:
                                pe.wait_ge(relu_ok, 8 * w + j + 1)
                                for k in range(KD):
                                    ins = pe.matmul(ph[j % NH][:, :], W1[u][:, k, j * P:(j + 1) * P],
                                                    xgT[:, bass.ds(w, 1), k * P:(k + 1) * P].rearrange("p o t -> p (o t)"), start=k == 0, stop=k == KD - 1)
                                ins.then_inc(h_mm, 1)
                            if j >= 2:
                                if j == 2:
                                    pe.wait_ge(w2_in[u], 16 * e + 32)
                                    pe.wait_ge(y_ok, w + 1)
                                pe.wait_ge(relu_ok, 8 * w + j - 2 + 1 + NH)
                                ins = pe.matmul(py[:, :], hT[:, j - 2, :], W2[u][:, j - 2, :], start=j == 2, stop=j == HJ + 1)
                        ins.then_inc(y_mm, 1)
            for i in range(TOPK * B):
                b, k = i // TOPK, i % TOPK
                pe.wait_ge(diag_ok, i + 1)
                if k == 0 and b >= 2:
                    pe.wait_ge(added, b - 1)
                pe.wait_ge(yk_in[i % NY], 16 * (i // NY + 1))
                ins = pe.matmul(banks[b % 2][0:S, :], diag[:, i, :], yk[0:S, i % NY, :], start=k == 0, stop=k == TOPK - 1)
                if k == TOPK - 1:
                    ins.then_inc(sum_mm, 1)

        @block.scalar
        def _(act):
            def keep(w, u):
                act.wait_ge(xt_mm, w + 1)
                act.copy(xgT[:, bass.ds(w, 1), :].rearrange("p o t -> p (o t)"), ptx[u][:, :]).then_inc(xt_ok, 1)

            with act.Fori(0, SLOT_TILES - 1, 2) as w:
                for u in range(2):
                    keep(w + u, u)
            root(act)
            act.wait_ge(b1_in, 16)
            free(act)
            act.memzero(hT[:, 0, :]).then_inc(relu_ok, NH)
            with act.Fori(0, E_N - 1, 2) as e:
                for u in range(2):
                    t0, t1 = tiles_of(act, e + u)
                    with act.Fori(t0, t1) as w:
                        for j in range(HJ):
                            act.wait_ge(h_mm, 8 * w + j + 1)
                            act.activation(hT[:, j, :], ph[j % NH][:, :], ACT.Relu,
                                           bias=b1[:, bass.ds((e + u) * HJ + j, 1)]).then_inc(relu_ok, 1)
            done = act.value_load(first_tile[0:1, E_N:E_N + 1], min_val=E_N, max_val=SLOT_TILES)
            act.wait_ge(y_ok, done + 1)
            for i in range(TOPK * B):
                b, k = i // TOPK, i % TOPK
                act.activation(diag[:, i, :], ident[0:S, 0:S], ACT.Copy, scale=res["gates"][:, k, b:b + 1]).then_inc(diag_ok, 1)
            for m in range(B // 2 + 1):
                work = norms_of(m)
                act.wait_ge(var_ok, m + 1)
                for i, b in work[::2]:
                    ins = act.activation(rstd[:, i, b:b + 2], rstd[:, i, b:b + 2], ACT.Sqrt)
                ins.then_inc(root_ok, 1)
                if m < B // 2:
                    act.wait_ge(norm_ok, m + 1)
                    for i, b in work[:2]:
                        ins = act.activation(lat[:, b, :], x_sb[:, b, :], ACT.Identity, scale=rstd[:, 0, b:b + 1], bias=nmr[:, b:b + 1])
                    ins.then_inc(lat_ok, 1)

        @block.vector
        def _(dve):
            dve.sem_inc(y_ok, 1)
            keep_all(dve, make_linker(dve, res["dve_chain"]))
            with dve.Fori(0, E_N - 1, 2) as e:
                for u in range(2):
                    t0, t1 = tiles_of(dve, e + u)
                    with dve.Fori(t0, t1) as w:
                        dve.wait_ge(w2_in[u], 16 * e + 32)
                        dve.wait_ge(y_mm, w + 1)
                        dve.wait_ge(y_free, w + 1)
                        dve.tensor_tensor(y[:, :], py[:, :], b2[u][:, :], ALU.add).then_inc(y_ok, 1)
            def add(b):
                dve.wait_ge(sum_mm, b + 1)
                dve.tensor_tensor(x_sb[:, b, :], x_sb[:, b, :], banks[b % 2][0:S, :], ALU.add).then_inc(added, 1)

            link = make_linker(dve, res["dve_chain"])
            for m in range(B // 2 + 1):
                work = norms_of(m)
                if m < B // 2:
                    add(2 * m)
                    add(2 * m + 1)
                    dve.wait_ge(added, 2 * m + 2)
                if m:
                    dve.wait_ge(lat_ok, m)
                for i, b in work:
                    ins = dve.bn_stats(stats[:, i, b, :], (x_sb, lat)[i][:, b, :])
                link(ins)
                for i, b in work:
                    ins = dve.bn_aggr(mv[:, i, b, :], stats[:, i, b, :])
                link(ins)
                for i, b in work[::2]:
                    ins = dve.tensor_scalar(rstd[:, i, b:b + 2], mv[:, i, b:b + 2, 1], EPS, None, ALU.add)
                ins.then_inc(var_ok, 1)
                dve.wait_ge(root_ok, m + 1)
                for i, b in work[::2]:
                    ins = dve.reciprocal(rstd[:, i, b:b + 2], rstd[:, i, b:b + 2])
                link(ins)
                if m < B // 2:
                    dve.scalar_tensor_tensor(nmr[:, 2 * m:2 * m + 2], mv[:, 0, 2 * m:2 * m + 2, 0], -1.0, rstd[:, 0, 2 * m:2 * m + 2],
                                             ALU.mult, ALU.mult).then_inc(norm_ok, 1)
                for i, b in work:
                    if i:
                        dve.tensor_scalar(lat[:, b, :], lat[:, b, :], mv[:, 1, b, 0:1], rstd[:, 1, b:b + 1], ALU.subtract, ALU.mult)

        @block.gpsimd
        def _(pool):
            constants(pool)
            gather_kept(pool)
            last = pool.value_load(first_tile[0:1, E_N:E_N + 1], min_val=E_N, max_val=SLOT_TILES)
            pool.sem_inc(y_free, 1)
            with pool.Fori(0, last) as w:
                pool.wait_ge(y_ok, w + 2)
                pool.dma_start(res["yg"][bass.ds(w * P, P), :], y[:, :]).then_inc(y_out, 16)
                pool.wait_ge(y_out, 16 * w + 16)
                pool.sem_inc(y_free, 1)
            for i in range(TOPK * B):
                b, k = i // TOPK, i % TOPK
                if i >= NY:
                    pool.wait_ge(sum_mm, (i - NY) // TOPK + 1)
                pool.indirect_dma_start(out=yk[0:S, i % NY, :], out_offset=None, in_=res["yg"],
                                        in_offset=bass.IndirectOffsetOnAxis(ap=res["slots"][:, k * B + b:k * B + b + 1], axis=0)).then_inc(yk_in[i % NY], 16)


def attend(nc, io, res):
    ctx = ExitStack()
    with ctx:
        sb, pb, sem = allocator(nc, ctx)
        ident, rows, lat = res["ident"], res["rows_k"], res["lat"]
        Wq, Wkv, Wo = res["Wq"], res["Wkv"], res["Wo"]
        vec, qk_scale, bout = res["vec"], res["qk_scale"], res["bout"]
        st_g, st_l = sb("st_g", [P, D]), sb("st_l", [S, D])
        kb = [sb(f"kb{u}", [S, NK]) for u in range(2)]
        lnT = sb("lnT", [P, KD, NK])
        qkn = sb("qkn", [P, 3, D])
        NR = [S, S, P]
        sq = sb("sq", [P, D])
        ssq = sb("ssq", [P, 3, HEADS])
        half = sb("half", [P, HEADS])
        rn = sb("rn", [P, 3, HEADS])
        v = [sb(f"v{u}", [P, 2, D]) for u in range(2)]
        kT = [sb(f"kT{u}", [P, KD, NK]) for u in range(2)]
        qT = [sb(f"qT{u}", [P, KD, S]) for u in range(2)]
        sc = [sb(f"sc{i}", [S, NK]) for i in range(2)]
        pr = [sb(f"pr{i}", [S, NK]) for i in range(2)]
        prT = [sb(f"prT{i}", [P, 2, S]) for i in range(2)]
        least = [sb(f"least{u}", [S, HEADS]) for u in range(2)]
        total = [sb(f"total{u}", [S, HEADS]) for u in range(2)]
        rtot = sb("rtot", [S, HEADS])
        took = sem("took")
        o = sb("o", [S, D])
        oT = sb("oT", [P, KD, S])
        att = res["att"]
        bt = pb("bt", [P, D])
        bk = [pb(f"bk{i}", [P, D]) for i in range(2)]
        bs = [pb(f"bs{i}", [S, NK]) for i in range(2)]
        bp = [pb(f"bp{i}", [P, 2 * S]) for i in range(2)]
        bo = pb("bo", [S, D])
        w_in = res["attn_in"]
        (staged, t_mm, t_free, k_mm, sq_ok, ss_ok, pow_ok, unit_ok, s_mm, least_ok, exp_ok, p_mm, pv_mm, o_ok, setup) = (
            sem(n) for n in ("staged", "t_mm", "t_free", "k_mm", "sq_ok", "ss_ok", "pow_ok", "unit_ok", "s_mm", "least_ok",
                             "exp_oke", "p_mm", "pv_mm", "o_ok", "setup"))
        k_free = [sem(f"k_free{i}") for i in range(2)]
        pt_ok = [sem("pt_oke0"), sem("pt_oke1")]
        sums, rt_ok = sem("sums"), sem("rt_ok")
        gammas = res["gammas"]
        block = ctx.enter_context(nc.Block())
        LAT = KC

        def rows_T(pe, n, idx):
            src, r = ((st_g, P), (st_l, S))[idx]
            pe.wait_ge(staged, n + 1)
            if not (isinstance(n, int) and n == 0 and idx == 0):
                pe.wait_ge(t_free, 6 * n + idx)
            for k in range(KD):
                ins = pe.transpose(bt[:, k * P:k * P + r], src[:, k * P:(k + 1) * P], ident[0:r, 0:r])
            ins.then_inc(t_mm, 1)

        def product(pe, n, idx):
            c0, c1 = (LAT, NK) if idx in (0, 1, 3) else (0, KC)
            w = Wq[:, :, :] if idx == 0 else Wkv[:, :, 0:D] if idx in (1, 2) else Wkv[:, :, D:2 * D]
            pe.wait_ge(t_free, 6 * n + 2)
            if not (isinstance(n, int) and n == 0 and idx < 2):
                pe.wait_ge(k_free[idx % 2], 3 * n + idx // 2)
            for k in range(KD):
                ins = pe.matmul(bk[idx % 2][0:c1 - c0, :], lnT[:, k, c0:c1], w[:, k, :], start=k == 0, stop=k == KD - 1)
            ins.then_inc(k_mm, 2 if isinstance(n, int) and n == 0 and idx == 4 else 1)

        def unit_T(pe, n, i):
            r = NR[i]
            pe.wait_ge(unit_ok, 3 * n + i + 1)
            pe.wait_ge(t_free, 6 * n + 2 + i)
            for k in range(KD):
                ins = pe.transpose(bt[:, k * P:k * P + r], qkn[0:r, i, k * P:(k + 1) * P], ident[0:r, 0:r])
            ins.then_inc(t_mm, 2 if isinstance(n, int) and n == 0 and i == 2 else 1)

        def scores(pe, b, u, h):
            pe.wait_ge(least_ok, 8 * b + h + 1)
            lo = DH * (h % 2)
            pe.matmul(bs[h % 2][:, :], qT[u][lo:lo + DH, h // 2, :], kT[u][lo:lo + DH, h // 2, :], start=True, stop=True).then_inc(s_mm, 1)

        def probs_T(pe, b, h):
            pe.wait_ge(exp_ok, 8 * b + h + 3)
            pe.wait_ge(pt_ok[h % 2], 4 * b + h // 2 + 1)
            pe.transpose(bp[h % 2][:, 0:S], pr[h % 2][:, 0:KC], ident[0:S, 0:S])
            pe.transpose(bp[h % 2][0:S, S:2 * S], pr[h % 2][:, KC:NK], ident[0:S, 0:S]).then_inc(p_mm, 1)

        def values(pe, b, u, h):
            pe.wait_ge(pt_ok[h % 2], 4 * b + h // 2 + 2)
            pe.matmul(bo[:, h * DH:(h + 1) * DH], prT[h % 2][:, 0, :], v[u][:, 0, h * DH:(h + 1) * DH], start=True, stop=False)
            pe.matmul(bo[:, h * DH:(h + 1) * DH], prT[h % 2][0:S, 1, :], v[u][0:S, 1, h * DH:(h + 1) * DH], start=False, stop=True).then_inc(pv_mm, 1)

        @block.tensor
        def _(pe):
            def prepare(n, i):
                if i < 2:
                    rows_T(pe, n, i)
                elif i in (5, 7, 9):
                    unit_T(pe, n, (i - 5) // 2)
                else:
                    product(pe, n, i - 2 if i < 5 else i // 2)

            def sums_T(b, last):
                pe.wait_ge(o_ok, b + 2)
                pe.wait_ge(t_free, 6 * b + (6 if last else 11))
                for k in range(KD):
                    ins = pe.transpose(bt[:, k * P:k * P + S], o[:, k * P:(k + 1) * P], ident[0:S, 0:S])
                ins.then_inc(t_mm, 1)

            def project(b, last, ks=range(KD)):
                if ks[0] == 0:
                    pe.wait_ge(t_free, 6 * b + (7 if last else 12))
                    pe.wait_ge(k_free[1], 3 * b + (3 if last else 5))
                for k in ks:
                    ins = pe.matmul(bk[1][0:S, :], oT[:, k, :], Wo[:, k, :], start=k == 0, stop=k == KD - 1)
                if ks[-1] == KD - 1:
                    ins.then_inc(k_mm, 1)

            def batch(b, u, first, last):
                pe.wait_ge(t_free, 6 * b + 5)
                scores(pe, b, u, 0)
                scores(pe, b, u, 1)
                if not first:
                    prepare(b, 8)
                    sums_T(b - 1, False)
                for h in range(HEADS):
                    if h and not last:
                        prepare(b + 1, h)
                    if h == 1 and not first:
                        project(b - 1, False, range(2, KD))
                    probs_T(pe, b, h)
                    if h + 2 < HEADS:
                        scores(pe, b, u, h + 2)
                    if h == 0 and not last:
                        prepare(b + 1, 0)
                    if h == 0 and not first:
                        project(b - 1, False, range(0, 2))
                    if h == 0:
                        pe.wait_ge(k_free[1], 3 * b + 2)
                        pe.wait_ge(k_free[0], 3 * b + 3)
                        pe.wait_ge(o_ok, b + 1)
                    if h >= 1:
                        values(pe, b, u, h - 1)
                if not last:
                    prepare(b + 1, 9)
                values(pe, b, u, HEADS - 1)

            pe.wait_ge(w_in, 48)
            pe.sem_inc(p_mm, 2)
            pe.sem_inc(pv_mm, 2)
            for i in range(10):
                prepare(0, i)
            batch(0, 0, True, False)
            with pe.Fori(1, B - 2, 2) as b:
                for u in range(2):
                    batch(b + u, 1 - u, False, False)
            batch(B - 1, 1, False, True)
            sums_T(B - 1, True)
            project(B - 1, True)

        @block.gpsimd
        def _(pool):
            def stage(n, u):
                if not (isinstance(n, int) and n == 0):
                    pool.wait_ge(t_mm, 6 * n - 4)
                    pool.wait_ge(least_ok, 8 * n - 6)
                pool.tensor_copy(st_g[:, :], rows[:, bass.ds(n, 1), :].rearrange("p o d -> p (o d)"))
                pool.tensor_copy(st_l[:, :], lat[:, bass.ds(n, 1), :].rearrange("p o d -> p (o d)"))
                pool.tensor_copy(kb[u][:, :], res["kbias"][:, bass.ds(n, 1), :].rearrange("p o d -> p (o d)")).then_inc(staged, 1)

            def norms(n):
                for i in range(3):
                    r = NR[i]
                    pool.wait_ge(k_free[i % 2], 3 * n + 1 + i // 2)
                    if not (isinstance(n, int) and n == 0 and i == 0):
                        pool.wait_ge(ss_ok, 3 * n + i)
                    pool.tensor_tensor(sq[0:r, :], qkn[0:r, i, :], qkn[0:r, i, :], ALU.mult).then_inc(sq_ok, 1)
                    pool.wait_ge(ss_ok, 3 * n + i + 1)
                    pool.tensor_tensor(rn[0:r, i, :], ssq[0:r, i, :], half[0:r, :], ALU.pow).then_inc(pow_ok, 1)

            pool.memset(half[:, :], -0.5).then_inc(setup, 1)
            pool.wait_ge(setup, 1)
            norms(0)
            with pool.Fori(1, B - 2, 2) as n:
                for u in range(2):
                    stage(n + u, 1 - u)
                    norms(n + u)
            stage(B - 1, 1)
            norms(B - 1)

        @block.scalar
        def _(act):
            def soft(b, u, h):
                act.wait_ge(least_ok, 8 * b + h + 3)
                act.wait_ge(p_mm, 8 * b + h + 1)
                act.activation(pr[h % 2][:, :], sc[h % 2][:, :], ACT.Exp, bias=least[u][:, h:h + 1], scale=-1.0,
                               accum_out=total[u][:, h:h + 1]).then_inc(exp_ok, 1)

            def keep_probs(b, h):
                act.wait_ge(p_mm, 8 * b + h + 3)
                act.wait_ge(pv_mm, 8 * b + h + 1)
                act.activation(prT[1][:, 0, :], bp[1][:, 0:S], ACT.Copy)
                act.activation(prT[1][0:S, 1, :], bp[1][0:S, S:2 * S], ACT.Copy).then_inc(pt_ok[1], 1)

            def prepare(n, u, i):
                first = isinstance(n, int) and n == 0
                if i == 1:
                    act.wait_ge(t_mm, 6 * n + 2)
                    for k in range(KD):
                        ins = act.activation(lnT[:, k, LAT:NK], bt[:, k * P:k * P + S], ACT.Identity,
                                             scale=vec[:, 2, k:k + 1], bias=vec[:, 3, k:k + 1])
                    ins.then_inc(t_free, 1)
                if i == 2:
                    act.wait_ge(k_mm, 6 * n + 1)
                    act.activation(qkn[0:S, 0, :], bk[0][0:S, :], ACT.Copy).then_inc(k_free[0], 1)
                if i == 4:
                    act.wait_ge(k_mm, 6 * n + 3)
                    act.activation(qkn[:, 2, :], bk[0][:, :], ACT.Copy).then_inc(k_free[0], 1)
                if i == 6:
                    act.wait_ge(k_mm, 6 * n + 4)
                    act.activation(v[u][0:S, 1, :], bk[1][0:S, :], ACT.Copy).then_inc(k_free[1], 2 if first else 1)
                if i == 8:
                    act.wait_ge(k_mm, 6 * n + 5)
                    act.activation(v[u][:, 0, :], bk[0][:, :], ACT.Copy).then_inc(k_free[0], 1)
                if i == 5:
                    act.wait_ge(t_mm, 6 * n + 3)
                    act.activation(qT[u][:, :, :], bt[:, :].rearrange("p (k s) -> p k s", k=KD)[:, :, 0:S], ACT.Copy,
                                   scale=qk_scale[:, 0:1]).then_inc(t_free, 1)
                if i == 9:
                    act.wait_ge(t_mm, 6 * n + 5)
                    act.activation(kT[u][:, :, 0:KC], bt[:, :].rearrange("p (k s) -> p k s", k=KD), ACT.Copy).then_inc(t_free, 2 if first else 1)

            def batch(b, u, first, last):
                soft(b, u, 0)
                for h in range(HEADS):
                    if h + 1 < HEADS:
                        soft(b, u, h + 1)
                    if h == 0 and not first:
                        prepare(b, u, 8)
                    if not last:
                        prepare(b + 1, 1 - u, h)
                    if h % 2:
                        keep_probs(b, h)
                if not last:
                    prepare(b + 1, 1 - u, 9)

            act.wait_ge(w_in, 48)
            act.wait_ge(res["vec_in"], 48)
            act.wait_ge(res["vec_ok"], 1)
            act.sem_inc(exp_ok, 2)
            act.sem_inc(pt_ok[1], 1)
            for i in range(10):
                prepare(0, 0, i)
            batch(0, 0, True, False)
            with act.Fori(1, B - 2, 2) as b:
                for u in range(2):
                    batch(b + u, 1 - u, False, False)
            batch(B - 1, 1, False, True)

        @block.vector
        def _(dve):
            def reduce(n, i):
                r = NR[i]
                dve.wait_ge(sq_ok, 3 * n + i + 1)
                dve.tensor_reduce(ssq[0:r, i, :], sq[0:r, :].rearrange("p (h d) -> p h d", d=DH), AX, ALU.add).then_inc(sums, 1)
                dve.wait_ge(sums, 3 * n + i + 1)
                dve.tensor_scalar(ssq[0:r, i, :], ssq[0:r, i, :], 1.0 / DH, 1e-16, ALU.mult, ALU.max).then_inc(ss_ok, 1)

            def unit(n, i):
                r = NR[i]
                dve.wait_ge(pow_ok, 3 * n + i + 1)
                q = qkn[0:r, i, :].rearrange("p (h d) -> p h d", d=DH)
                dve.tensor_tensor(q, q, rn[0:r, i, :].unsqueeze(2).broadcast_to([r, HEADS, DH]), ALU.mult).then_inc(unit_ok, 1)

            def prepare(n, u, i):
                if i == 0:
                    dve.wait_ge(t_mm, 6 * n + 1)
                    for k in range(KD):
                        ins = dve.tensor_scalar(lnT[:, k, 0:KC], bt[:, k * P:(k + 1) * P], vec[:, 0, k:k + 1], vec[:, 1, k:k + 1],
                                                ALU.mult, ALU.add)
                    ins.then_inc(t_free, 1)
                if i == 3:
                    dve.wait_ge(k_mm, 6 * n + 2)
                    dve.tensor_copy(qkn[0:S, 1, :], bk[1][0:S, :]).then_inc(k_free[1], 1)
                    reduce(n, 0)
                if i == 4:
                    unit(n, 0)
                    reduce(n, 1)
                if i == 5:
                    unit(n, 1)
                    reduce(n, 2)
                if i == 6:
                    unit(n, 2)
                if i == 7:
                    dve.wait_ge(t_mm, 6 * n + 4)
                    dve.tensor_copy(kT[u][:, :, LAT:NK], bt[:, :].rearrange("p (k s) -> p k s", k=KD)[:, :, 0:S]).then_inc(t_free, 1)

            def lowest(b, u, h):
                dve.wait_ge(s_mm, 8 * b + h + 1)
                dve.wait_ge(exp_ok, 8 * b + h + 1)
                dve.sem_inc(took, 1)
                dve.tensor_tensor_reduce(out=sc[h % 2][:, :], in0=bs[h % 2][:, :], in1=kb[u][:, :], scale=1.0, scalar=3e38,
                                         op0=ALU.add, op1=ALU.min, accum_out=least[u][:, h:h + 1]).then_inc(least_ok, 1)

            def keep_probs(b, h):
                dve.wait_ge(p_mm, 8 * b + h + 3)
                dve.wait_ge(pv_mm, 8 * b + h + 1)
                dve.tensor_copy(prT[0][:, 0, :], bp[0][:, 0:S])
                dve.tensor_copy(prT[0][0:S, 1, :], bp[0][0:S, S:2 * S]).then_inc(pt_ok[0], 1)

            def sums_over(b, u):
                dve.wait_ge(exp_ok, 8 * b + 10)
                dve.reciprocal(rtot[:, :], total[u][:, :]).then_inc(rt_ok, 1)
                dve.wait_ge(rt_ok, b + 1)
                dve.wait_ge(pv_mm, 8 * b + 10)
                dve.wait_ge(t_mm, 6 * b + 6)
                dve.tensor_tensor(o[:, :].rearrange("p (h d) -> p h d", d=DH), bo[:, :].rearrange("p (h d) -> p h d", d=DH),
                                  rtot[:, :].unsqueeze(2).broadcast_to([S, HEADS, DH]), ALU.mult).then_inc(o_ok, 1)

            def sums_kept(b, last):
                dve.wait_ge(t_mm, 6 * b + (7 if last else 12))
                dve.tensor_copy(oT[:, :, :], bt[:, :].rearrange("p (k s) -> p k s", k=KD)[:, :, 0:S]).then_inc(t_free, 1)

            def add_bias(b, last):
                dve.wait_ge(k_mm, 6 * b + (7 if last else 12))
                dve.tensor_tensor(att[0:S, bass.ds(b, 1), :].rearrange("p o d -> p (o d)"), bk[1][0:S, :], bout[:, :], ALU.add).then_inc(k_free[1], 1)

            def batch(b, u, first, last):
                lowest(b, u, 0)
                if not first:
                    sums_over(b - 1, 1 - u)
                for h in range(HEADS):
                    if h + 1 < HEADS:
                        lowest(b, u, h + 1)
                    if h == 0 and not first:
                        sums_kept(b - 1, False)
                    if not last:
                        prepare(b + 1, 1 - u, h)
                    if h == 1 and not first:
                        add_bias(b - 1, False)
                    if h % 2 == 0:
                        keep_probs(b, h)

            dve.tensor_copy(st_g[:, :], rows[:, 0, :])
            dve.tensor_copy(st_l[:, :], lat[:, 0, :])
            dve.tensor_copy(kb[0][:, :], res["kbias"][:, 0, :]).then_inc(staged, 1)
            dve.wait_ge(res["vec_in"], 48)
            dve.scalar_tensor_tensor(qk_scale[:, :], gammas[:, 0:1], -DH ** -0.5, gammas[:, 1:2], ALU.mult, ALU.mult).then_inc(res["vec_ok"], 1)
            dve.sem_inc(least_ok, 2)
            dve.sem_inc(pt_ok[0], 1)
            dve.sem_inc(o_ok, 1)
            for i in range(10):
                prepare(0, 0, i)
            batch(0, 0, True, False)
            with dve.Fori(1, B - 2, 2) as b:
                for u in range(2):
                    batch(b + u, 1 - u, False, False)
            batch(B - 1, 1, False, True)
            sums_over(B - 1, 1)
            sums_kept(B - 1, True)
            add_bias(B - 1, True)


def attend_full(nc, io, res):
    NT = CT + 1
    KR = CR + [S]
    STEPS = NT + 2 * NT + 1 + NT + 1 + 3 * HEADS + 2
    HALF = NKD // 2
    FIRST_T = 512 // S
    ctx = ExitStack()
    with ctx:
        sb, pb, sem = allocator(nc, ctx)
        ident, lat = res["ident"], res["lat"]
        Wq, Wkv, Wo = res["Wq"], res["Wkv"], res["Wo"]
        vec, qk_scale, bout, att = res["vec"], res["qk_scale"], res["bout"], res["att"]
        stats, mv, rstd = sb("stats_d", [P, CT, 6]), sb("mv_d", [P, CT, 2]), sb("rstd_d", [P, CT])
        spare = [res["tiles"][:, B + i * NT:B + (i + 1) * NT, :] for i in range(3)]
        rows = spare[0]
        vals = spare[1]
        q = sb("q_d", [S, D])
        lnT = spare[2].rearrange("p t d -> p (t d)")[:, 0:KD * NKD].rearrange("p (k n) -> p k n", k=KD)
        qT = sb("qT_d", [P, KD, S])
        mask8 = sb("mask8_d", [S, C], mybir.dt.uint8)
        bias = sb("bias_d", [S, NKD])
        ssq, rn, half = sb("ssq_d", [P, HEADS]), sb("rn_d", [P, HEADS]), sb("half_d", [P, HEADS])
        sc, pr = sb("sc_d", [S, NKD]), sb("pr_d", [S, NKD])
        prT = sb("prT_d", [P, NT, S])
        low, least, total, rtot = sb("low_d", [S, 2]), sb("least_d", [S, 1]), sb("total_d", [S, HEADS]), sb("rtot_d", [S, HEADS])
        took = sem("took_d")
        o, oT = sb("o_d", [S, D]), sb("oT_d", [P, KD, S])
        bt, b0, b1, p0, p1, bo = (pb(n, [P, 512]) for n in ("bt_d", "b0_d", "b1_d", "p0_d", "p1_d", "bo_d"))
        d_in, batch_done, pe_turn, dve_turn, ask_act, act_did, ask_pool, pool_did, hset = (sem(n) for n in (
            "d_in", "batch_done", "pe_turn", "dve_turn", "ask_act", "act_did", "ask_pool", "pool_did", "hset"))
        block = ctx.enter_context(nc.Block())
        cols = [P * t for t in range(CT)] + [C]

        def each_full(eng, body):
            some = eng.value_load(res["flag"][0:1, B:B + 1], min_val=0, max_val=1)
            with eng.If(some == 1):
                with eng.Fori(0, B) as b:
                    f = eng.value_load(res["flag"][0:1, bass.ds(b, 1)], min_val=0, max_val=1)
                    r = eng.value_load(res["runs"][0:1, bass.ds(b, 1)], min_val=0, max_val=B - 1)
                    with eng.If(f == 1):
                        body(b, r)

        @block.sync
        def _(sp):
            def body(b, r):
                sp.wait_ge(batch_done, r + 1)
                sp.dma_start(rows[:, 0:CT - 1, :], io["ctx"][bass.ds(b, 1), 0:P * (CT - 1), :].rearrange("o (t p) d -> p (o t) d", p=P)).then_inc(d_in, 16)
                sp.dma_start(rows[0:CR[-1], CT - 1, :], io["ctx"][bass.ds(b, 1), P * (CT - 1):C, :].rearrange("o p d -> (o p) d")).then_inc(d_in, 16)
                sp.dma_start(mask8[:, :], io["mask"][bass.ds(b, 1), :].broadcast_to([S, C])).then_inc(d_in, 16)
            each_full(sp, body)

        @block.tensor
        def _(pe):
            def body(b, r):
                n = [0]

                def turn(work):
                    n[0] += 1
                    pe.wait_ge(dve_turn, STEPS * r + n[0])
                    work().then_inc(pe_turn, 1)

                def turned(dst, src, rr):
                    def work():
                        for k in range(KD):
                            ins = pe.transpose(dst[:, k * P:k * P + rr], src[:, k * P:(k + 1) * P], ident[0:rr, 0:rr])
                        return ins
                    return work

                def times(dst, lhs, w):
                    def work():
                        for k in range(KD):
                            ins = pe.matmul(dst, lhs(k), w[:, k, :], start=k == 0, stop=k == KD - 1)
                        return ins
                    return work

                for t in range(NT):
                    turn(turned(bt, rows[0:KR[t], t, :], KR[t]))
                for t in range(NT):
                    for w in (Wkv[:, :, 0:D], Wkv[:, :, D:2 * D]):
                        turn(times(b0[0:KR[t], :], lambda k: lnT[:, k, cols[t]:cols[t] + KR[t]], w))
                turn(times(b0[0:S, :], lambda k: lnT[:, k, C:NKD], Wq))
                for t in range(NT):
                    turn(turned(bt, rows[0:KR[t], t, :], KR[t]))
                turn(turned(bt, q[:, :], S))
                for h in range(HEADS):
                    lo, c, hd = DH * (h % 2), h // 2, slice(h * DH, (h + 1) * DH)

                    def scores():
                        pe.matmul(b0[0:S, 0:HALF], qT[lo:lo + DH, c, :], lnT[lo:lo + DH, c, 0:HALF], start=True, stop=True)
                        return pe.matmul(b1[0:S, 0:HALF], qT[lo:lo + DH, c, :], lnT[lo:lo + DH, c, HALF:NKD], start=True, stop=True)

                    def probs():
                        for t in range(NT):
                            dst, k = (p0, t) if t < FIRST_T else (p1, t - FIRST_T)
                            ins = pe.transpose(dst[0:KR[t], k * S:(k + 1) * S], pr[:, cols[t]:cols[t] + KR[t]], ident[0:S, 0:S])
                        return ins

                    def sums():
                        for t in range(NT):
                            ins = pe.matmul(bo[0:S, hd], prT[0:KR[t], t, :], vals[0:KR[t], t, hd], start=t == 0, stop=t == NT - 1)
                        return ins
                    turn(scores)
                    turn(probs)
                    turn(sums)
                turn(turned(bt, o[:, :], S))
                turn(times(b0[0:S, :], lambda k: oT[:, k, :], Wo))
                assert n[0] == STEPS
            each_full(pe, body)

        @block.scalar
        def _(act):
            def body(b, r):
                act.wait_ge(ask_act, (HEADS + 1) * r + 1)
                act.activation(rstd[:, :], rstd[:, :], ACT.Sqrt).then_inc(act_did, 1)
                for h in range(HEADS):
                    act.wait_ge(ask_act, (HEADS + 1) * r + h + 2)
                    act.activation(pr[:, :], sc[:, :], ACT.Exp, bias=least[:, 0:1], scale=-1.0, accum_out=total[:, h:h + 1]).then_inc(act_did, 1)
            each_full(act, body)

        @block.gpsimd
        def _(pool):
            pool.memset(half[:, :], -0.5).then_inc(hset, 1)
            pool.wait_ge(hset, 1)

            def body(b, r):
                for t in range(NT + 1):
                    n = KR[t] if t < NT else S
                    pool.wait_ge(ask_pool, (NT + 1) * r + t + 1)
                    pool.tensor_tensor(rn[0:n, :], ssq[0:n, :], half[0:n, :], ALU.pow).then_inc(pool_did, 1)
            each_full(pool, body)

        @block.vector
        def _(dve):
            dve.memset(rows[:, CT - 1, :], 0.0)
            dve.memset(rstd[:, :], 1.0)
            dve.drain()
            dve.sem_inc(batch_done, 1)

            def body(b, r):
                n, a, g = [0], [0], [0]

                def give():
                    dve.drain().then_inc(dve_turn, 1)

                def take():
                    n[0] += 1
                    dve.wait_ge(pe_turn, STEPS * r + n[0])
                    dve.sem_inc(took, 1)

                def ask(who, s_ask, s_did, per, count):
                    dve.drain().then_inc(s_ask, 1)
                    count[0] += 1
                    dve.wait_ge(s_did, per * r + count[0])
                    dve.sem_inc(took, 1)

                dve.wait_ge(d_in, 48 * r + 48)
                for t in range(CT):
                    dve.bn_stats(stats[0:CR[t], t, :], rows[0:CR[t], t, :])
                dve.drain()
                for t in range(CT):
                    dve.bn_aggr(mv[0:CR[t], t, :], stats[0:CR[t], t, :])
                dve.drain()
                for t in range(CT):
                    dve.tensor_scalar(rstd[0:CR[t], t:t + 1], mv[0:CR[t], t, 1:2], EPS, None, ALU.add)
                ask(None, ask_act, act_did, HEADS + 1, a)
                dve.reciprocal(rstd[:, :], rstd[:, :])
                dve.drain()
                for t in range(CT):
                    dve.tensor_scalar(rows[0:CR[t], t, :], rows[0:CR[t], t, :], mv[0:CR[t], t, 0:1], rstd[0:CR[t], t:t + 1], ALU.subtract, ALU.mult)
                dve.tensor_copy(rows[0:S, CT, :], lat[:, bass.ds(b, 1), :].rearrange("p o d -> p (o d)"))
                dve.tensor_copy(bias[:, 0:C], mask8[:, :])
                dve.drain()
                dve.tensor_scalar(bias[:, 0:C], bias[:, 0:C], -BIG, BIG, ALU.mult, ALU.add)
                dve.memset(bias[:, C:NKD], 0.0)
                give()
                for t in range(NT):
                    take()
                    i = 0 if t < CT else 2
                    for k in range(KD):
                        dve.tensor_scalar(lnT[:, k, cols[t]:cols[t] + KR[t]], bt[:, k * P:k * P + KR[t]], vec[:, i, k:k + 1],
                                          vec[:, i + 1, k:k + 1], ALU.mult, ALU.add)
                    give()

                def unit(x, rr):
                    xh = x.rearrange("p (h d) -> p h d", d=DH)
                    dve.tensor_tensor(sc[0:S, 0:D] if rr == S else prT[0:rr, 0:6, :].rearrange("p t s -> p (t s)")[:, 0:D], x, x, ALU.mult)
                    sq = (sc[0:S, 0:D] if rr == S else prT[0:rr, 0:6, :].rearrange("p t s -> p (t s)")[:, 0:D]).rearrange("p (h d) -> p h d", d=DH)
                    dve.drain()
                    dve.tensor_reduce(ssq[0:rr, :], sq, AX, ALU.add)
                    dve.drain()
                    dve.tensor_scalar(ssq[0:rr, :], ssq[0:rr, :], 1.0 / DH, 1e-16, ALU.mult, ALU.max)
                    ask(None, ask_pool, pool_did, NT + 1, g)
                    dve.tensor_tensor(xh, xh, rn[0:rr, :].unsqueeze(2).broadcast_to([rr, HEADS, DH]), ALU.mult)

                for t in range(NT):
                    take()
                    dve.tensor_copy(rows[0:KR[t], t, :], b0[0:KR[t], :])
                    dve.drain()
                    unit(rows[0:KR[t], t, :], KR[t])
                    give()
                    take()
                    dve.tensor_copy(vals[0:KR[t], t, :], b0[0:KR[t], :])
                    give()
                take()
                dve.tensor_copy(q[:, :], b0[0:S, :])
                dve.drain()
                unit(q[:, :], S)
                give()
                for t in range(NT):
                    take()
                    dve.tensor_copy(lnT[:, :, cols[t]:cols[t] + KR[t]], bt[:, :].rearrange("p (k s) -> p k s", k=KD)[:, :, 0:KR[t]])
                    give()
                take()
                dve.tensor_scalar(qT[:, :, :], bt[:, :].rearrange("p (k s) -> p k s", k=KD)[:, :, 0:S], qk_scale[:, 0:1], None, ALU.mult)
                give()
                for h in range(HEADS):
                    take()
                    for i, bank in enumerate((b0, b1)):
                        dve.tensor_tensor_reduce(out=sc[:, i * HALF:(i + 1) * HALF], in0=bank[0:S, 0:HALF], in1=bias[:, i * HALF:(i + 1) * HALF],
                                                 scale=1.0, scalar=3e38, op0=ALU.add, op1=ALU.min, accum_out=low[:, i:i + 1])
                    dve.drain()
                    dve.tensor_tensor(least[:, :], low[:, 0:1], low[:, 1:2], ALU.min)
                    ask(None, ask_act, act_did, HEADS + 1, a)
                    give()
                    take()
                    for t in range(NT):
                        src, k = (p0, t) if t < FIRST_T else (p1, t - FIRST_T)
                        dve.tensor_copy(prT[0:KR[t], t, :], src[0:KR[t], k * S:(k + 1) * S])
                    give()
                    take()
                    if h < HEADS - 1:
                        give()
                dve.reciprocal(rtot[:, :], total[:, :])
                dve.drain()
                dve.tensor_tensor(o[:, :].rearrange("p (h d) -> p h d", d=DH), bo[0:S, :].rearrange("p (h d) -> p h d", d=DH),
                                  rtot[:, :].unsqueeze(2).broadcast_to([S, HEADS, DH]), ALU.mult)
                give()
                take()
                dve.tensor_copy(oT[:, :, :], bt[:, :].rearrange("p (k s) -> p k s", k=KD)[:, :, 0:S])
                give()
                take()
                dve.tensor_tensor(att[0:S, bass.ds(b, 1), :].rearrange("p o d -> p (o d)"), b0[0:S, :], bout[:, :], ALU.add)
                dve.drain().then_inc(batch_done, 1)
                assert n[0] == STEPS
            each_full(dve, body)


F, E_L, R_L = 2048, 4, 4
FJ = F // P
ER = E_L * R_L


def feed_forward(nc, io, res):
    ctx = ExitStack()
    with ctx:
        sb, pb, sem = allocator(nc, ctx)
        x_sb, ident, ones = res["x"], res["ident"], res["ones"]
        Wi, WoT = sb("Wi", [P, KD, F]), sb("WoT", [P, FJ, D])
        Bt = sb("Bt", [2 * 32, F])
        WgA = sb("WgA", [P, KD, E_L + ER])
        bg = sb("bg", [S, E_L])
        stats, mv, rstd = sb("stats_f", [S, B, 6]), sb("mv_f", [S, B, 2]), sb("rstd_f", [S, B])
        xn = sb("xn_f", [S, B, D])
        xT = sb("xT_f", [P, KD, XT])
        lga = sb("lga", [S, B, E_L + ER])
        score = sb("score", [S, B, 8])
        lmax, lsum = sb("lmax_f", [S, B]), sb("lsum_f", [S, B])
        top, topi, topf = sb("top_f", [S, B, 8]), sb("topi_f", [S, B, 8], U32), sb("topf_f", [S, B, 8])
        iota_e = sb("iota_f", [S, E_L])
        hot = [sb(f"hot_f{k}", [S, B, E_L]) for k in range(2)]
        low = sb("low_f", [S, B, 64])
        lowT = sb("lowT", [64, XT])
        wdiag = [sb(f"wdiag{i}", [S, B // 2, S]) for i in range(2)]
        wb = [sb(f"wb{k}", [P, XT]) for k in range(2)]
        NT4 = XT // 2
        h1 = [sb(f"h1_{i}", [P, NT4]) for i in range(2)]
        h2 = [sb(f"h2_{i}", [P, NT4]) for i in range(2)]
        hs = [sb(f"hs{i}", [P, NT4]) for i in range(3)]
        NBK = 3
        bank = [pb(f"bf{i}", [P, 512]) for i in range(NBK)]
        acc = [pb(f"acc{i}", [P, 512]) for i in range(4)]
        bx = pb("bx", [P, 512])
        w_in, wi_in, wo_in = sem("wf_in"), sem("wi_in"), sem("wo_in")
        (var_ok, root_ok, xn_ok, t_mm, t_ok, l_mm, sub_ok, exp_ok, low_ok, lt_mm, lt_ok, rep_ok, wb_mm, wb_ok, cs,
         base_mm, read1, d_mm, read2, hs_ok, acc_mm, acc_rd, out_s) = (sem("f_" + n) for n in (
             "var_ok", "root_ok", "xn_ok", "t_mm", "t_ok", "l_mm", "sub_ok", "exp_ok", "low_ok", "lt_mm", "lt_ok",
             "rep_ok", "wb_mm", "wb_ok", "cs", "base_mm", "read1", "d_mm", "read2", "hs_ok", "acc_mm", "acc_rd", "out_s"))
        block = ctx.enter_context(nc.Block())

        @block.sync
        def _(sp):
            sp.dma_start(WgA[:, :, :], io["WgA"].rearrange("(k p) e -> p k e", p=P)).then_inc(w_in, 16)
            sp.dma_start(bg[:, :], io["bg"].rearrange("(o e) -> o e", o=1).broadcast_to([S, E_L])).then_inc(w_in, 16)
            for i in range(2):
                sp.dma_start(Bt[32 * i:32 * i + ER, :], io["Bt"]).then_inc(w_in, 16)
            sp.dma_start(Wi[:, :, :], io["WiT"].rearrange("(k p) f -> p k f", p=P)).then_inc(wi_in, 16)
            sp.dma_start(WoT[:, :, :], io["WoT"].rearrange("(j p) d -> p j d", p=P)).then_inc(wo_in, 16)
            for b in range(B):
                sp.wait_ge(acc_rd, b + 1)
                sp.dma_start(io["out"][b], x_sb[:, b, :]).then_inc(out_s, 16)
            sp.wait_ge(out_s, 16 * B)

        @block.gpsimd
        def _(pool):
            pool.iota(iota_e[:, :], pattern=[[1, E_L]], base=0, channel_multiplier=0,
                      allow_small_or_imprecise_dtypes=True).then_inc(cs, 1)
            pool.memset(low[:, :, :], 0.0).then_inc(cs, 1)
            pool.memset(score[:, :, :], -1.0).then_inc(cs, 1)
            for i in range(2 * FJ):
                pool.wait_ge(read2, i + 1)
                if i >= 3:
                    pool.wait_ge(acc_mm, i - 2)
                pool.tensor_tensor(hs[i % 3][:, :], h1[i % 2][:, :], h2[i % 2][:, :], ALU.add).then_inc(hs_ok, 1)

        @block.scalar
        def _(act):
            def keep_T(b):
                act.wait_ge(t_mm, b + 1)
                act.activation(xT[:, :, b * S:(b + 1) * S], acc[2 + b % 2][:, :].rearrange("p (k s) -> p k s", k=KD)[:, :, 0:S],
                               ACT.Copy).then_inc(t_ok, 1)

            for g in range(0, B, 2):
                act.wait_ge(var_ok, g // 2 + 1)
                act.activation(rstd[:, g:g + 2], rstd[:, g:g + 2], ACT.Sqrt).then_inc(root_ok, 1)
                if g:
                    keep_T(g - 2)
                    keep_T(g - 1)
            keep_T(B - 2)
            keep_T(B - 1)
            act.wait_ge(sub_ok, 1)
            act.activation(score[:, :, 0:E_L], score[:, :, 0:E_L], ACT.Exp).then_inc(exp_ok, 1)

        @block.tensor
        def _(pe):
            def turn(b):
                pe.wait_ge(xn_ok, b + 1)
                if b >= 2:
                    pe.wait_ge(t_ok, b - 1)
                for k in range(KD):
                    ins = pe.transpose(acc[2 + b % 2][:, k * P:k * P + S], xn[:, b, k * P:(k + 1) * P], ident[0:S, 0:S])
                ins.then_inc(t_mm, 1)

            def logits(b):
                if b == 0:
                    pe.wait_ge(w_in, 64)
                pe.wait_ge(t_ok, b + 1)
                for k in range(KD):
                    ins = pe.matmul(bx[0:S, b * 32:b * 32 + E_L + ER], xT[:, k, b * S:(b + 1) * S], WgA[:, k, :], start=k == 0, stop=k == KD - 1)
                ins.then_inc(l_mm, 1)

            for b in range(0, B, 2):
                if b:
                    logits(b - 2)
                    logits(b - 1)
                turn(b)
                turn(b + 1)
            logits(B - 2)
            logits(B - 1)

            def base_x(i):
                g, f = i // FJ, i % FJ
                for k in range(KD):
                    pe.matmul(bank[i % NBK][:, 0:NT4], Wi[:, k, f * P:(f + 1) * P], xT[:, k, g * NT4:(g + 1) * NT4], start=k == 0, stop=False)

            pe.wait_ge(wi_in, 16)
            for i in range(NBK):
                base_x(i)
            pe.wait_ge(low_ok, 1)
            for b in range(B):
                ins = pe.transpose(acc[b // 4][0:64, (b % 4) * S:(b % 4 + 1) * S], low[:, b, :], ident[0:S, 0:S])
                if b % 4 == 3:
                    ins.then_inc(lt_mm, 1)
            for i in range(4):
                pe.wait_ge(rep_ok, i + 1)
                if i == 0:
                    pe.wait_ge(lt_ok, 2)
                pe.matmul(acc[(i + 2) % 4][:, 0:NT4], ones[0:S, :], wdiag[i % 2][:, :, :].rearrange("p b s -> p (b s)"), start=True, stop=True).then_inc(wb_mm, 1)
            pe.wait_ge(wb_ok, 4)

            def base(i):
                g, f = i // FJ, i % FJ
                if i >= NBK:
                    pe.wait_ge(read2, i - NBK + 1)
                    base_x(i)
                pe.matmul(bank[i % NBK][:, 0:NT4], Bt[0:ER, f * P:(f + 1) * P], lowT[0:ER, g * NT4:(g + 1) * NT4], start=False, stop=True).then_inc(base_mm, 1)

            def second(i):
                g, f = i // FJ, i % FJ
                pe.wait_ge(read1, i + 1)
                pe.matmul(bank[i % NBK][:, 0:NT4], Bt[32:32 + ER, f * P:(f + 1) * P], lowT[32:32 + ER, g * NT4:(g + 1) * NT4],
                          start=False, stop=True, skip_group_check=True).then_inc(d_mm, 1)

            def down(i):
                g, f = i // FJ, i % FJ
                pe.wait_ge(hs_ok, i + 1)
                if g and f == 0:
                    pe.wait_ge(acc_rd, 4)
                for j in range(4):
                    ins = pe.matmul(acc[j][0:S, :], hs[i % 3][:, j * S:(j + 1) * S], WoT[:, f, :], start=f == 0, stop=f == FJ - 1)
                ins.then_inc(acc_mm, 1)

            n = 2 * FJ
            for i in range(n + 2):
                if i < n:
                    base(i)
                if 1 <= i <= n:
                    second(i - 1)
                if i == 2:
                    pe.wait_ge(wo_in, 16)
                if i >= 2:
                    down(i - 2)

        @block.vector
        def _(dve):
            link = make_linker(dve, res["dve_chain"])
            for g in range(0, B, 2):
                two = (g, g + 1)
                for b in two:
                    ins = dve.tensor_tensor(x_sb[:, b, :], x_sb[:, b, :], res["att"][0:S, b, :], ALU.add)
                link(ins)
                layernorm_stats(link, dve, x_sb[:, g:g + 2, :], stats[:, g:g + 2, :], mv[:, g:g + 2, :], 2)
                dve.tensor_scalar(rstd[:, g:g + 2], mv[:, g:g + 2, 1], EPS, None, ALU.add).then_inc(var_ok, 1)
                dve.wait_ge(root_ok, g // 2 + 1)
                link(dve.reciprocal(rstd[:, g:g + 2], rstd[:, g:g + 2]))
                for b in two:
                    dve.tensor_scalar(xn[:, b, :], x_sb[:, b, :], mv[:, b, 0:1], rstd[:, b:b + 1], ALU.subtract, ALU.mult).then_inc(xn_ok, 1)
            dve.wait_ge(l_mm, B)
            dve.wait_ge(w_in, 64)
            dve.wait_ge(cs, 3)
            link(dve.tensor_copy(lga[:, :, :], bx[0:S, 0:B * 32].rearrange("p (b c) -> p b c", c=32)[:, :, 0:E_L + ER]))
            sc4 = score[:, :, 0:E_L]
            link(dve.tensor_tensor(sc4, lga[:, :, 0:E_L], bg[:, :].unsqueeze(1).broadcast_to([S, B, E_L]), ALU.add))
            link(dve.tensor_reduce(lmax[:, :], sc4, AX, ALU.max))
            dve.tensor_tensor(sc4, sc4, lmax[:, :].unsqueeze(2).broadcast_to([S, B, E_L]), ALU.subtract).then_inc(sub_ok, 1)
            dve.wait_ge(exp_ok, 1)
            link(dve.tensor_reduce(lsum[:, :], sc4, AX, ALU.add))
            link(dve.reciprocal(lsum[:, :], lsum[:, :]))
            link(dve.tensor_tensor(sc4, sc4, lsum[:, :].unsqueeze(2).broadcast_to([S, B, E_L]), ALU.mult))
            for b in range(B):
                ins = dve.max(top[:, b, :], score[:, b, :])
            link(ins)
            for b in range(B):
                ins = dve.max_index(topi[:, b, :], top[:, b, :], score[:, b, :])
            link(ins)
            link(dve.tensor_copy(topf[:, :, :], topi[:, :, :]))
            for k in range(2):
                ins = dve.tensor_tensor(hot[k][:, :, :], iota_e[:, :].unsqueeze(1).broadcast_to([S, B, E_L]),
                                        topf[:, :, k:k + 1].broadcast_to([S, B, E_L]), ALU.is_equal)
            link(ins)
            link(dve.tensor_tensor(hot[1][:, :, :], hot[1][:, :, :], hot[0][:, :, :], ALU.subtract))
            for b in range(B):
                for k in range(2):
                    ins = dve.tensor_tensor(low[:, b, 32 * k:32 * k + ER].rearrange("p (e r) -> p e r", r=R_L),
                                            lga[:, b, E_L:E_L + ER].rearrange("p (e r) -> p e r", r=R_L),
                                            hot[k][:, b, :].unsqueeze(2).broadcast_to([S, E_L, R_L]), ALU.mult)
            ins.then_inc(low_ok, 1)
            for g in range(2):
                dve.wait_ge(lt_mm, g + 1)
                dve.tensor_copy(lowT[:, g * NT4:(g + 1) * NT4], acc[g][0:64, 0:NT4]).then_inc(lt_ok, 1)
            def keep_weights(q):
                dve.wait_ge(wb_mm, q + 1)
                dve.tensor_copy(wb[q // 2][:, q % 2 * NT4:(q % 2 + 1) * NT4], acc[(q + 2) % 4][:, 0:NT4]).then_inc(wb_ok, 1)

            for i in range(4):
                k, g = i // 2, i % 2
                if i >= 2:
                    dve.wait_ge(wb_mm, i - 1)
                dve.tensor_tensor(wdiag[i % 2][:, :, :], ident[0:S, 0:S].unsqueeze(1).broadcast_to([S, B // 2, S]),
                                  top[:, g * B // 2:(g + 1) * B // 2, k:k + 1].broadcast_to([S, B // 2, S]), ALU.mult).then_inc(rep_ok, 1)
                if i:
                    keep_weights(i - 1)
            keep_weights(3)
            dve.wait_ge(wb_ok, 4)

            def weigh(i, k):
                g = i // FJ
                dve.wait_ge((base_mm, d_mm)[k], i + 1)
                if i >= 2:
                    dve.wait_ge(hs_ok, i - 1)
                dve.scalar_tensor_tensor((h1, h2)[k][i % 2][:, :], bank[i % NBK][:, 0:NT4], 0.0, wb[k][:, g * NT4:(g + 1) * NT4],
                                         ALU.max, ALU.mult).then_inc((read1, read2)[k], 1)

            def finish(g):
                dve.wait_ge(acc_mm, FJ * (g + 1))
                for j in range(4):
                    dve.tensor_tensor(x_sb[:, 4 * g + j, :], x_sb[:, 4 * g + j, :], acc[j][0:S, :], ALU.add).then_inc(acc_rd, 1)

            n = 2 * FJ
            for i in range(n):
                weigh(i, 0)
                if i:
                    weigh(i - 1, 1)
                if i == FJ + 1:
                    finish(0)
            weigh(n - 1, 1)
            finish(1)

def build(nc, io, scratch):
    ctx = ExitStack()
    with ctx:
        sb, pb, sem = allocator(nc, ctx)
        res = dict(scratch)
        res["x"] = sb("x_res", [S, B, D])
        res["ident"] = sb("ident", [P, P])
        res["ones"] = sb("ones", [P, P])
        res["gates"] = sb("gates", [S, TOPK, B])
        res["slots"] = sb("slots", [S, TOPK * B], I32)
        res["table"] = sb("table", [S, E_N + 2], I32)
        res["flag"], res["runs"] = sb("flags", [P, B + 1], I32), sb("runs_n", [P, B + 1], I32)
        res["attn_in"], res["vec_in"], res["vec_ok"] = sem("attn_in"), sem("vec_in"), sem("vec_ok")
        res["dve_chain"] = [sem("dve_chain"), 0]
        with ExitStack() as rows:
            res["cost_mem"] = rows.enter_context(nc.sbuf_tensor("cost_mem", [P, (BL + 2) * ST], FP32))
            res["cost"] = res["cost_mem"][:, 0:BL * ST].rearrange("p (a s) -> p a s", s=ST)
            distances(nc, io, res)
            res["ctx_rows"] = rows.enter_context(nc.sbuf_tensor("ctx_rows", [P, B * CT, D], FP32))
            warp(nc, io, res)
            route(nc, io, res)
        res["rows_k"] = sb("rows_k", [P, B, D])
        res["kbias"] = sb("kbias", [S, B, NK])
        res["att"] = sb("att", [P, B, D])
        with ExitStack() as attn:
            def at(name, shape):
                return attn.enter_context(nc.sbuf_tensor(name, shape, FP32))
            res["tiles"] = at("tiles", [P, SLOT_TILES, KD * P])
            res["lat"] = res["tiles"][0:S, 0:B, :]
            first, second = res["W_first"], res["W_second"] = at("W_first", [P, KD, H]), at("W_second", [P, HJ, D])
            res["Wkv"], res["Wq"], res["Wo"] = first[:, :, :], second[:, 0:KD, :], second[:, KD:2 * KD, :]
            res["vec"], res["qk_scale"], res["bout"] = at("vec", [P, 4, KD]), at("qk_scale", [P, 1]), at("bout", [S, D])
            res["gammas"] = at("gammas", [P, 2])
            experts(nc, io, res)
            attend(nc, io, res)
            attend_full(nc, io, res)
        feed_forward(nc, io, res)


def kernel(**inputs):
    import numpy as _np
    import concourse.bacc as _bacc
    from concourse import mybir as _mybir
    from concourse.bass_utils import run_bass_kernel_spmd as _run

    nc = _bacc.Bacc("TRN2", target_bir_lowering=False, num_devices=1)
    ctx_rows = _np.ascontiguousarray(inputs["ctx_1024"])
    arrays = {"x": _np.ascontiguousarray(inputs["x"]), "ctx": ctx_rows,
              "gate": _np.ascontiguousarray(inputs["L0_ffn_gate"]),
              "W1": _np.ascontiguousarray(inputs["L0_ffn_W1"]), "W2": _np.ascontiguousarray(inputs["L0_ffn_W2"]),
              "b2": _np.ascontiguousarray(inputs["L0_ffn_b2"]),
              "b1T": _np.ascontiguousarray(inputs["L0_ffn_b1"].reshape(16, 8, 128).transpose(2, 0, 1)).reshape(128, 128),
              "maskT": _np.ascontiguousarray(inputs["mask_BxS2_bk0"].T),
              "mask": _np.ascontiguousarray(inputs["mask_BxS2_bk0"]),
              "vec": _np.ascontiguousarray(_np.stack([inputs["L1_xattn_ln_" + n] for n in ("x_g", "x_b", "l_g", "l_b")])
                                           .reshape(4, 4, 128).transpose(2, 0, 1)),
              "gammas": _np.ascontiguousarray(_np.stack([_np.concatenate([inputs["L1_xattn_" + n]] * 2) for n in ("q_gamma", "k_gamma")], 1)),
              "Wq": _np.ascontiguousarray(inputs["L1_xattn_W_q"]), "Wkv": _np.ascontiguousarray(inputs["L1_xattn_W_kv"]),
              "Wout": _np.ascontiguousarray(inputs["L1_xattn_W_out"]), "bout": _np.ascontiguousarray(inputs["L1_xattn_b_out"]),
              "WgA": _np.ascontiguousarray(_np.concatenate([inputs["L1_ffn_Wg"], _np.asarray(inputs["L1_ffn_A"]).reshape(16, 512)]).T),
              "bg": _np.ascontiguousarray(inputs["L1_ffn_bg"]), "WiT": _np.ascontiguousarray(inputs["L1_ffn_Wi"].T),
              "WoT": _np.ascontiguousarray(inputs["L1_ffn_Wo"].T),
              "Bt": _np.ascontiguousarray(_np.asarray(inputs["L1_ffn_B"]).transpose(0, 2, 1)).reshape(16, 2048),
              "ctxT": _np.ascontiguousarray(ctx_rows.transpose(0, 2, 1))}
    io = {n: nc.dram_tensor("in_" + n, a.shape, _mybir.dt.from_np(a.dtype), kind="ExternalInput").ap() for n, a in arrays.items()}
    io["out"] = nc.dram_tensor("out", (8, 100, 512), FP32, kind="ExternalOutput").ap()
    sc = {"dist": nc.dram_tensor("dist", (8, 722, 100), FP32, kind="Internal").ap(),
          "xg": nc.dram_tensor("xg", (SLOT_TILES * P, D), FP32, kind="Internal").ap(),
          "yg": nc.dram_tensor("yg", (SLOT_TILES * P, D), FP32, kind="Internal").ap(),
          "path": nc.dram_tensor("path", (8, 722, 100), BF16, kind="Internal").ap()}
    build(nc, io, sc)
    r = _run(nc, [{"in_" + n: a for n, a in arrays.items()}], core_ids=[0])
    return r.results[0]["out"]
```
